# Optimizing a Trainium2 kernel written in Bass

```python
import numpy as np
import jax
import jax.numpy as jnp

def _softmax(x, axis=-1):
    return jax.nn.softmax(x, axis=axis)

def _gelu(x):
    return jax.nn.gelu(x, approximate=True)

def _silu(x):
    return jax.nn.silu(x)

def _sigmoid(x):
    return jax.nn.sigmoid(x)

def _layernorm(x, axis=-1, eps=1e-05):
    m = jnp.mean(x, axis=axis, keepdims=True)
    v = jnp.var(x, axis=axis, keepdims=True)
    return (x - m) / jnp.sqrt(v + eps)

def _scatter_add(tgt, idx, src, axis=0):
    return tgt.at[idx].add(src)

def _segment_sum(src, seg, n):
    return jax.ops.segment_sum(src, seg, n)
kernel_name = 'mk_flamingo_gated_d4_seqx_r4_9620ba'

def setup_inputs(seed: int=0):
    np.random.seed(seed)
    _w = jnp.asarray

    def _rec_inputs():
        import jax
        import jax.numpy as jnp
        _rk = jax.random.key(seed)
        x = -0.0003929 + 0.9999 * jax.random.normal(jax.random.fold_in(_rk, 1), (2, 1024, 256), jnp.float32)
        _lenS = 1024 - jax.random.randint(jax.random.fold_in(_rk, 7), (2,), 0, max(1, 1024 // 4) + 1, jnp.int32)
        _lenS2 = 154 - jax.random.randint(jax.random.fold_in(_rk, 8), (2,), 0, max(1, 154 // 4) + 1, jnp.int32)
        _ctx_1024P = jax.random.normal(jax.random.fold_in(_rk, 11), (2, 16, 256), jnp.float32)
        _ctx_1024c = jax.random.dirichlet(jax.random.fold_in(_rk, 511), 0.3 * jnp.ones((16,), jnp.float32), (2, 154))
        _ctx_1024t = jnp.einsum('bsk,bkd->bsd', _ctx_1024c, _ctx_1024P)
        _ctx_1024t = _ctx_1024t * jax.lax.rsqrt(jnp.mean(jnp.square(_ctx_1024t)) + 1e-12) * 0.953939
        ctx_1024 = 2.81802e-05 + 1.00001 * (_ctx_1024t + 0.3 * jax.random.normal(jax.random.fold_in(_rk, 611), (2, 154, 256), jnp.float32))
        fside_BxSxS2_0 = jax.random.uniform(jax.random.fold_in(_rk, 12), (2, 1024, 154), jnp.float32, 0.0, 1)
        _validS = jnp.arange(1024)[None, :] < _lenS[:, None]
        _validS2 = jnp.arange(154)[None, :] < _lenS2[:, None]
        _causal = jnp.tril(jnp.ones((1024, 1024), dtype=bool))
        mask_BxSxS2_ik1 = jnp.where(jnp.broadcast_to(_validS2[:, None, :], (2, 1024, 154)), 1, 0).astype(jnp.int32)
        _g = jax.random.normal(jax.random.fold_in(_rk, 9001), (2, 4), jnp.float32)
        _g = jnp.sign(_g) * jnp.maximum(jnp.abs(_g), 1.0) + (_g == 0) * 1.0
        g_xattn = _g[0]
        g_ffn = _g[1]
        return (x, ctx_1024, fside_BxSxS2_0, mask_BxSxS2_ik1, g_xattn, g_ffn)
    x, ctx_1024, fside_BxSxS2_0, mask_BxSxS2_ik1, g_xattn, g_ffn = _rec_inputs()

    def _L0_xattn_setup():
        import jax, jax.numpy as jnp
        import numpy as np
        import math
        B, L, D = (4, 1024, 256)
        M = 64
        EPS = 1e-06
        key = jax.random.key(seed)
        kq, kk, kv, kp = jax.random.split(key, 4)
        Q = jax.random.normal(kq, (B, L, D), dtype=jnp.float32)
        K = jax.random.normal(kk, (B, L, D), dtype=jnp.float32)
        V = jax.random.normal(kv, (B, L, D), dtype=jnp.float32)
        projection = jax.random.normal(kp, (M, D), dtype=jnp.float32)
        return {'Q': Q, 'K': K, 'V': V, 'projection': projection}
    _L0_xattn_all = _L0_xattn_setup()
    _L0_xattn_in = {k: v for k, v in _L0_xattn_all.items() if k in ('projection',)}
    del _L0_xattn_all

    def _L0_ffn_setup():
        import jax, jax.numpy as jnp
        import numpy as np
        D_MODEL = 256
        N_EXPERTS = 8
        TOP_K = 2
        HIDDEN = 4 * D_MODEL
        key = jax.random.key(seed)
        ks = jax.random.split(key, 6)
        B, S = (2, 512)
        x = jax.random.normal(ks[0], (B, S, D_MODEL), dtype=jnp.float32)
        shared_w1 = jax.random.normal(ks[1], (HIDDEN, D_MODEL), dtype=jnp.float32) * 0.02
        shared_w2 = jax.random.normal(ks[2], (D_MODEL, HIDDEN), dtype=jnp.float32) * 0.02
        experts_w1 = jax.random.normal(ks[3], (N_EXPERTS, HIDDEN, D_MODEL), dtype=jnp.float32) * 0.02
        experts_w2 = jax.random.normal(ks[4], (N_EXPERTS, D_MODEL, HIDDEN), dtype=jnp.float32) * 0.02
        gate_w = jax.random.normal(ks[5], (N_EXPERTS, D_MODEL), dtype=jnp.float32) * 0.02
        return {'x': x, 'shared_w1': shared_w1, 'shared_w2': shared_w2, 'experts_w1': experts_w1, 'experts_w2': experts_w2, 'gate_w': gate_w}
    _L0_ffn_all = _L0_ffn_setup()
    _L0_ffn_in = {k: v for k, v in _L0_ffn_all.items() if k in ('shared_w1', 'shared_w2', 'experts_w1', 'experts_w2', 'gate_w')}
    del _L0_ffn_all

    def _L1_xattn_setup():
        import jax, jax.numpy as jnp
        import numpy as np
        NUM_HEADS = 16
        HIDDEN = 256
        B, S = (2, 512)

        def _split_heads(x, H):
            b, s, d = x.shape
            return x.reshape(b, s, H, d // H).transpose(0, 2, 1, 3)
        key = jax.random.key(seed)
        ks = jax.random.split(key, 14)
        D = HIDDEN
        scale = 1.0 / np.sqrt(D)
        inp = {'query': jax.random.normal(ks[0], (B, S, D), jnp.float32), 'key_in': jax.random.normal(ks[1], (B, S, D), jnp.float32), 'value': jax.random.normal(ks[2], (B, S, D), jnp.float32), 'group_prob': jax.random.uniform(ks[3], (B, S, S), jnp.float32), 'mask': jax.random.randint(ks[4], (B, S, S), 0, 2, jnp.int32), 'wq_k': jax.random.normal(ks[5], (D, D), jnp.float32) * scale, 'wq_b': jnp.zeros((D,), jnp.float32), 'wk_k': jax.random.normal(ks[6], (D, D), jnp.float32) * scale, 'wk_b': jnp.zeros((D,), jnp.float32), 'wv_k': jax.random.normal(ks[7], (D, D), jnp.float32) * scale, 'wv_b': jnp.zeros((D,), jnp.float32), 'wo_k': jax.random.normal(ks[8], (D, D), jnp.float32) * scale, 'wo_b': jnp.zeros((D,), jnp.float32)}
        return inp
    _L1_xattn_all = _L1_xattn_setup()
    _L1_xattn_in = {k: v for k, v in _L1_xattn_all.items() if k in ('wq_k', 'wq_b', 'wk_k', 'wk_b', 'wv_k', 'wv_b', 'wo_k', 'wo_b')}
    del _L1_xattn_all

    def _L1_ffn_setup():
        import jax, jax.numpy as jnp
        import numpy as np
        B, S, D, F, E, K = (2, 512, 256, 512, 8, 2)
        key = jax.random.key(seed)
        ks = jax.random.split(key, 5)
        scale = 0.02
        return {'x': jax.random.normal(ks[0], (B, S, D), dtype=jnp.float32), 'Wg': jax.random.normal(ks[1], (E, D), dtype=jnp.float32) * scale, 'W1': jax.random.normal(ks[2], (E, F, D), dtype=jnp.float32) * scale, 'W2': jax.random.normal(ks[3], (E, F, D), dtype=jnp.float32) * scale, 'W3': jax.random.normal(ks[4], (E, D, F), dtype=jnp.float32) * scale}
    _L1_ffn_all = _L1_ffn_setup()
    _L1_ffn_in = {k: v for k, v in _L1_ffn_all.items() if k in ('Wg', 'W1', 'W2', 'W3')}
    del _L1_ffn_all

    def _L2_xattn_setup():
        import jax, jax.numpy as jnp
        import numpy as np
        B, L_ENC, L_DEC, D = (16, 128, 128, 256)
        key = jax.random.key(seed)
        k1, k2, k3, k4, k5, k6 = jax.random.split(key, 6)
        encoder_hc = jax.random.normal(k1, (B, L_ENC, D), dtype=jnp.float32)
        decoder_hq = jax.random.normal(k2, (B, L_DEC, D), dtype=jnp.float32)
        w_sim = jax.random.normal(k3, (3 * D,), dtype=jnp.float32) * 0.02
        b_sim = jax.random.normal(k4, (1,), dtype=jnp.float32) * 0.02
        W_qv = jax.random.normal(k5, (4 * D, D), dtype=jnp.float32) * 0.02
        b_qv = jax.random.normal(k6, (D,), dtype=jnp.float32) * 0.02
        return {'encoder_hc': encoder_hc, 'decoder_hq': decoder_hq, 'w_sim': w_sim, 'b_sim': b_sim, 'W_qv': W_qv, 'b_qv': b_qv}
    _L2_xattn_all = _L2_xattn_setup()
    _L2_xattn_in = {k: v for k, v in _L2_xattn_all.items() if k in ('w_sim', 'b_sim', 'W_qv', 'b_qv')}
    del _L2_xattn_all

    def _L2_ffn_setup():
        import jax, jax.numpy as jnp
        import numpy as np
        D, H, O, E, TOPK = (256, 1024, 256, 8, 2)
        B, S = (4, 256)
        key = jax.random.key(seed)
        ks = jax.random.split(key, 12)
        std = 0.02
        return {'hidden_states': jax.random.normal(ks[0], (B, S, D), dtype=jnp.float32), 'norm_weight': jnp.ones((D,), dtype=jnp.float32), 'router_w': jax.random.normal(ks[1], (E, D), dtype=jnp.float32) * std, 'sw1': jax.random.normal(ks[2], (D, H), dtype=jnp.float32) * (1.0 / np.sqrt(D)), 'sb1': jnp.zeros((H,), dtype=jnp.float32), 'sw2': jax.random.normal(ks[3], (H, O), dtype=jnp.float32) * (1.0 / np.sqrt(H)), 'sb2': jnp.zeros((O,), dtype=jnp.float32), 'ew1': jax.random.normal(ks[4], (E, D, H), dtype=jnp.float32) * (1.0 / np.sqrt(D)), 'eb1': jnp.zeros((E, H), dtype=jnp.float32), 'ew2': jax.random.normal(ks[5], (E, H, O), dtype=jnp.float32) * (1.0 / np.sqrt(H)), 'eb2': jnp.zeros((E, O), dtype=jnp.float32)}
    _L2_ffn_all = _L2_ffn_setup()
    _L2_ffn_in = {k: v for k, v in _L2_ffn_all.items() if k in ('norm_weight', 'router_w', 'sw1', 'sb1', 'sw2', 'sb2', 'ew1', 'eb1', 'ew2', 'eb2')}
    del _L2_ffn_all

    def _L3_xattn_setup():
        import jax, jax.numpy as jnp
        import numpy as np
        D1, D2, D3 = (256, 256, 256)
        key = jax.random.key(seed)
        k1, k2, kw, kb = jax.random.split(key, 4)
        x1 = jax.random.normal(k1, (8, 512, D1), dtype=jnp.float32)
        x2 = jax.random.normal(k2, (8, 512, D2), dtype=jnp.float32)
        bound = 1.0 / np.sqrt(D1 + D2)
        W = jax.random.uniform(kw, (D3, D1 + D2), minval=-bound, maxval=bound, dtype=jnp.float32)
        b = jax.random.uniform(kb, (D3,), minval=-bound, maxval=bound, dtype=jnp.float32)
        return {'x1': x1, 'x2': x2, 'W': W, 'b': b}
    _L3_xattn_all = _L3_xattn_setup()
    _L3_xattn_in = {k: v for k, v in _L3_xattn_all.items() if k in ('W', 'b')}
    del _L3_xattn_all

    def _L3_ffn_setup():
        import jax, jax.numpy as jnp
        import numpy as np
        D = 256
        H = 512
        E = 8
        TOP_K = 2
        N_SHARED = 1
        B, S = (2, 256)
        key = jax.random.key(seed)
        ks = jax.random.split(key, 12)
        sc = 0.02
        return {'hidden': jax.random.normal(ks[0], (B, S, D), jnp.float32), 'router_w': jax.random.normal(ks[1], (D, E), jnp.float32) * sc, 'router_b': jnp.zeros((E,), jnp.float32), 'sw1': jax.random.normal(ks[2], (D, H), jnp.float32) * sc, 'sb1': jnp.zeros((H,), jnp.float32), 'sw2': jax.random.normal(ks[3], (H, D), jnp.float32) * sc, 'sb2': jnp.zeros((D,), jnp.float32), 'rw1': jax.random.normal(ks[4], (E, D, H), jnp.float32) * sc, 'rb1': jnp.zeros((E, H), jnp.float32), 'rw2': jax.random.normal(ks[5], (E, H, D), jnp.float32) * sc, 'rb2': jnp.zeros((E, D), jnp.float32)}
    _L3_ffn_all = _L3_ffn_setup()
    _L3_ffn_in = {k: v for k, v in _L3_ffn_all.items() if k in ('router_w', 'router_b', 'sw1', 'sb1', 'sw2', 'sb2', 'rw1', 'rb1', 'rw2', 'rb2')}
    del _L3_ffn_all
    return {'x': x, 'ctx_1024': ctx_1024, 'fside_BxSxS2_0': fside_BxSxS2_0, 'mask_BxSxS2_ik1': mask_BxSxS2_ik1, 'g_xattn': g_xattn, 'g_ffn': g_ffn, 'L0_xattn_projection': _L0_xattn_in['projection'], 'L0_ffn_shared_w1': _L0_ffn_in['shared_w1'], 'L0_ffn_shared_w2': _L0_ffn_in['shared_w2'], 'L0_ffn_experts_w1': _L0_ffn_in['experts_w1'], 'L0_ffn_experts_w2': _L0_ffn_in['experts_w2'], 'L0_ffn_gate_w': _L0_ffn_in['gate_w'], 'L1_xattn_wq_k': _L1_xattn_in['wq_k'], 'L1_xattn_wq_b': _L1_xattn_in['wq_b'], 'L1_xattn_wk_k': _L1_xattn_in['wk_k'], 'L1_xattn_wk_b': _L1_xattn_in['wk_b'], 'L1_xattn_wv_k': _L1_xattn_in['wv_k'], 'L1_xattn_wv_b': _L1_xattn_in['wv_b'], 'L1_xattn_wo_k': _L1_xattn_in['wo_k'], 'L1_xattn_wo_b': _L1_xattn_in['wo_b'], 'L1_ffn_Wg': _L1_ffn_in['Wg'], 'L1_ffn_W1': _L1_ffn_in['W1'], 'L1_ffn_W2': _L1_ffn_in['W2'], 'L1_ffn_W3': _L1_ffn_in['W3'], 'L2_xattn_w_sim': _L2_xattn_in['w_sim'], 'L2_xattn_b_sim': _L2_xattn_in['b_sim'], 'L2_xattn_W_qv': _L2_xattn_in['W_qv'], 'L2_xattn_b_qv': _L2_xattn_in['b_qv'], 'L2_ffn_norm_weight': _L2_ffn_in['norm_weight'], 'L2_ffn_router_w': _L2_ffn_in['router_w'], 'L2_ffn_sw1': _L2_ffn_in['sw1'], 'L2_ffn_sb1': _L2_ffn_in['sb1'], 'L2_ffn_sw2': _L2_ffn_in['sw2'], 'L2_ffn_sb2': _L2_ffn_in['sb2'], 'L2_ffn_ew1': _L2_ffn_in['ew1'], 'L2_ffn_eb1': _L2_ffn_in['eb1'], 'L2_ffn_ew2': _L2_ffn_in['ew2'], 'L2_ffn_eb2': _L2_ffn_in['eb2'], 'L3_xattn_W': _L3_xattn_in['W'], 'L3_xattn_b': _L3_xattn_in['b'], 'L3_ffn_router_w': _L3_ffn_in['router_w'], 'L3_ffn_router_b': _L3_ffn_in['router_b'], 'L3_ffn_sw1': _L3_ffn_in['sw1'], 'L3_ffn_sb1': _L3_ffn_in['sb1'], 'L3_ffn_sw2': _L3_ffn_in['sw2'], 'L3_ffn_sb2': _L3_ffn_in['sb2'], 'L3_ffn_rw1': _L3_ffn_in['rw1'], 'L3_ffn_rb1': _L3_ffn_in['rb1'], 'L3_ffn_rw2': _L3_ffn_in['rw2'], 'L3_ffn_rb2': _L3_ffn_in['rb2']}

def reference(x, ctx_1024, fside_BxSxS2_0, mask_BxSxS2_ik1, g_xattn, g_ffn, L0_xattn_projection, L0_ffn_shared_w1, L0_ffn_shared_w2, L0_ffn_experts_w1, L0_ffn_experts_w2, L0_ffn_gate_w, L1_xattn_wq_k, L1_xattn_wq_b, L1_xattn_wk_k, L1_xattn_wk_b, L1_xattn_wv_k, L1_xattn_wv_b, L1_xattn_wo_k, L1_xattn_wo_b, L1_ffn_Wg, L1_ffn_W1, L1_ffn_W2, L1_ffn_W3, L2_xattn_w_sim, L2_xattn_b_sim, L2_xattn_W_qv, L2_xattn_b_qv, L2_ffn_norm_weight, L2_ffn_router_w, L2_ffn_sw1, L2_ffn_sb1, L2_ffn_sw2, L2_ffn_sb2, L2_ffn_ew1, L2_ffn_eb1, L2_ffn_ew2, L2_ffn_eb2, L3_xattn_W, L3_xattn_b, L3_ffn_router_w, L3_ffn_router_b, L3_ffn_sw1, L3_ffn_sb1, L3_ffn_sw2, L3_ffn_sb2, L3_ffn_rw1, L3_ffn_rb1, L3_ffn_rw2, L3_ffn_rb2):
    import jax
    import jax.numpy as jnp

    def _L0_xattn_ref(Q, K, V, projection):
        import jax, jax.numpy as jnp
        import numpy as np
        import math
        B, L, D = (4, 1024, 256)
        M = 64
        EPS = 1e-06
        d_model = Q.shape[-1]
        m = projection.shape[0]
        inv_sqrt_d = 1.0 / math.sqrt(d_model)
        rf_q = jnp.exp(jnp.einsum('bld,md->blm', Q * inv_sqrt_d, projection)) / math.sqrt(m)
        rf_k = jnp.exp(jnp.einsum('bld,md->blm', K * inv_sqrt_d, projection))
        KV = jnp.einsum('blm,bld->bmd', rf_k, V)
        Z = jnp.sum(rf_k, axis=1)
        out = jnp.einsum('blm,bmd->bld', rf_q, KV)
        normalizer = jnp.einsum('blm,bm->bl', rf_q, Z) + EPS
        return out / normalizer[..., None]

    def _L0_ffn_ref(x, shared_w1, shared_w2, experts_w1, experts_w2, gate_w):
        import jax, jax.numpy as jnp
        import numpy as np
        D_MODEL = 256
        N_EXPERTS = 8
        TOP_K = 2
        HIDDEN = 4 * D_MODEL
        B, S, D = x.shape
        T = B * S
        x_flat = x.reshape(T, D)
        shared = jnp.einsum('td,dh->th', x_flat, shared_w1.T)
        shared = jnp.einsum('th,hd->td', jax.nn.silu(shared), shared_w2.T)
        gate_logits = x_flat @ gate_w.T
        top_k_gates, top_k_idx = jax.lax.top_k(gate_logits, TOP_K)
        top_k_gates = jax.nn.softmax(top_k_gates, axis=1)
        gates = jnp.zeros((T, N_EXPERTS), dtype=x.dtype)
        gates = gates.at[jnp.arange(T)[:, None], top_k_idx].set(top_k_gates)
        h = jnp.einsum('td,ehd->teh', x_flat, experts_w1)
        expert_out = jnp.einsum('teh,edh->ted', jax.nn.silu(h), experts_w2)
        selected = jnp.einsum('ted,te->td', expert_out, gates)
        return (shared + selected).reshape(B, S, D)

    def _L1_xattn_ref(query, key_in, value, group_prob, mask, wq_k, wq_b, wk_k, wk_b, wv_k, wv_b, wo_k, wo_b):
        import jax, jax.numpy as jnp
        import numpy as np
        NUM_HEADS = 16
        HIDDEN = 256
        B, S = (2, 512)

        def _split_heads(x, H):
            b, s, d = x.shape
            return x.reshape(b, s, H, d // H).transpose(0, 2, 1, 3)
        H = NUM_HEADS
        dh = query.shape[-1] // H
        q = _split_heads(query @ wq_k + wq_b, H)
        k = _split_heads(key_in @ wk_k + wk_b, H)
        v = _split_heads(value @ wv_k + wv_b, H)
        logits = jnp.einsum('bhqd,bhkd->bhqk', q, k) / jnp.sqrt(jnp.asarray(dh, q.dtype))
        neg = (1.0 - mask.astype(q.dtype)) * -1000000000.0
        logits = logits + neg[:, None, :, :]
        attn = jax.nn.softmax(logits, axis=-1)
        attn = attn * group_prob[:, None, :, :]
        out = jnp.einsum('bhqk,bhkd->bhqd', attn, v)
        out = out.transpose(0, 2, 1, 3).reshape(query.shape[0], -1, H * dh)
        return out @ wo_k + wo_b

    def _L1_ffn_ref(x, Wg, W1, W2, W3):
        import jax, jax.numpy as jnp
        import numpy as np
        B, S, D, F, E, K = (2, 512, 256, 512, 8, 2)
        k = K
        scores = jnp.einsum('bsd,ed->bse', x, Wg)
        topk_scores, topk_idx = jax.lax.top_k(scores, k)
        topk_probs = jax.nn.softmax(topk_scores, axis=-1)
        h1 = jnp.einsum('bsd,efd->bsef', x, W1)
        h2 = jnp.einsum('bsd,efd->bsef', x, W2)
        hidden = jax.nn.silu(h1) * h2
        expert_out = jnp.einsum('bsef,edf->bsed', hidden, W3)
        onehot = jax.nn.one_hot(topk_idx, scores.shape[-1], dtype=x.dtype)
        gating = jnp.einsum('bsk,bske->bse', topk_probs, onehot)
        return jnp.einsum('bse,bsed->bsd', gating, expert_out)

    def _L2_xattn_ref(encoder_hc, decoder_hq, w_sim, b_sim, W_qv, b_qv):
        import jax, jax.numpy as jnp
        import numpy as np
        B, L_ENC, L_DEC, D = (16, 128, 128, 256)
        d = encoder_hc.shape[-1]
        w1, w2, w3 = (w_sim[:d], w_sim[d:2 * d], w_sim[2 * d:])
        Sim = (encoder_hc @ w1)[:, :, None] + (decoder_hq @ w2)[:, None, :] + jnp.einsum('bid,bjd->bij', encoder_hc * w3, decoder_hq) + b_sim[0]
        A = jax.nn.softmax(Sim, axis=2)
        hq_hat = jnp.einsum('bij,bjd->bid', A, decoder_hq)
        Batt = jax.nn.softmax(jnp.max(Sim, axis=2), axis=1)
        hc_bar = jnp.einsum('bi,bid->bd', Batt, encoder_hc)[:, None, :]
        hc_hat = jnp.broadcast_to(hc_bar, encoder_hc.shape)
        feats = jnp.concatenate([encoder_hc, hq_hat, encoder_hc * hq_hat, encoder_hc * hc_hat], axis=-1)
        hcq = feats @ W_qv + b_qv
        return hcq

    def _L2_ffn_ref(hidden_states, norm_weight, router_w, sw1, sb1, sw2, sb2, ew1, eb1, ew2, eb2):
        import jax, jax.numpy as jnp
        import numpy as np
        D, H, O, E, TOPK = (256, 1024, 256, 8, 2)
        B, S = (4, 256)
        b, s, d = hidden_states.shape
        var = jnp.mean(jnp.square(hidden_states), axis=-1, keepdims=True)
        normed = hidden_states * jax.lax.rsqrt(var + 1e-08) * norm_weight
        shared = jnp.maximum(normed @ sw1 + sb1, 0.0) @ sw2 + sb2
        flat = normed.reshape(-1, d)
        T = flat.shape[0]
        probs = jax.nn.sigmoid(flat @ router_w.T)
        scores, idx = jax.lax.top_k(probs, TOPK)
        w = scores / (jnp.sum(scores, axis=-1, keepdims=True) + 1e-06)
        comb = jnp.zeros((T, E), dtype=flat.dtype)
        comb = comb.at[jnp.arange(T)[:, None], idx].add(w)
        h = jnp.maximum(jnp.einsum('td,edh->teh', flat, ew1) + eb1[None, :, :], 0.0)
        eo = jnp.einsum('teh,eho->teo', h, ew2) + eb2[None, :, :]
        routed = jnp.einsum('teo,te->to', eo, comb)
        return shared + routed.reshape(b, s, -1)

    def _L3_xattn_ref(x1, x2, W, b):
        import jax, jax.numpy as jnp
        import numpy as np
        D1, D2, D3 = (256, 256, 256)
        d1 = x1.shape[-1]
        W1 = W[:, :d1]
        W2 = W[:, d1:]
        part1 = jnp.einsum('bld,ed->ble', x1, W1)
        part2 = jnp.einsum('bld,ed->be', x2, W2) / x2.shape[1]
        return part1 + part2[:, None, :] + b

    def _L3_ffn_ref(hidden, router_w, router_b, sw1, sb1, sw2, sb2, rw1, rb1, rw2, rb2):
        import jax, jax.numpy as jnp
        import numpy as np
        D = 256
        H = 512
        E = 8
        TOP_K = 2
        N_SHARED = 1
        B, S = (2, 256)
        b, s, d = hidden.shape
        T = b * s
        flat = hidden.reshape(T, d)
        router_logits = flat @ router_w + router_b
        router_probs = jax.nn.softmax(router_logits, axis=-1)
        topk_probs, topk_idx = jax.lax.top_k(router_probs, TOP_K)
        weights = jnp.zeros_like(router_probs).at[jnp.arange(T)[:, None], topk_idx].add(topk_probs)
        sh = jax.nn.gelu(flat @ sw1 + sb1, approximate=False)
        shared_out = (sh @ sw2 + sb2) / N_SHARED
        h1 = jax.nn.gelu(jnp.einsum('td,edh->teh', flat, rw1) + rb1[None], approximate=False)
        expert_out = jnp.einsum('teh,ehd->ted', h1, rw2) + rb2[None]
        mixed = jnp.einsum('ted,te->td', expert_out, weights)
        return (shared_out + mixed).reshape(b, s, d)
    x = x + jnp.tanh(g_xattn[0]) * _L0_xattn_ref(_layernorm(x, axis=-1), ctx_1024, ctx_1024, L0_xattn_projection)
    x = x + jnp.tanh(g_ffn[0]) * _L0_ffn_ref(_layernorm(x, axis=-1), L0_ffn_shared_w1, L0_ffn_shared_w2, L0_ffn_experts_w1, L0_ffn_experts_w2, L0_ffn_gate_w)
    x = x + jnp.tanh(g_xattn[1]) * _L1_xattn_ref(_layernorm(x, axis=-1), ctx_1024, ctx_1024, fside_BxSxS2_0, mask_BxSxS2_ik1, L1_xattn_wq_k, L1_xattn_wq_b, L1_xattn_wk_k, L1_xattn_wk_b, L1_xattn_wv_k, L1_xattn_wv_b, L1_xattn_wo_k, L1_xattn_wo_b)
    x = x + jnp.tanh(g_ffn[1]) * _L1_ffn_ref(_layernorm(x, axis=-1), L1_ffn_Wg, L1_ffn_W1, L1_ffn_W2, L1_ffn_W3)
    x = x + jnp.tanh(g_xattn[2]) * _L2_xattn_ref(_layernorm(x, axis=-1), ctx_1024, L2_xattn_w_sim, L2_xattn_b_sim, L2_xattn_W_qv, L2_xattn_b_qv)
    x = x + jnp.tanh(g_ffn[2]) * _L2_ffn_ref(_layernorm(x, axis=-1), L2_ffn_norm_weight, L2_ffn_router_w, L2_ffn_sw1, L2_ffn_sb1, L2_ffn_sw2, L2_ffn_sb2, L2_ffn_ew1, L2_ffn_eb1, L2_ffn_ew2, L2_ffn_eb2)
    x = x + jnp.tanh(g_xattn[3]) * _L3_xattn_ref(_layernorm(x, axis=-1), ctx_1024, L3_xattn_W, L3_xattn_b)
    x = x + jnp.tanh(g_ffn[3]) * _L3_ffn_ref(_layernorm(x, axis=-1), L3_ffn_router_w, L3_ffn_router_b, L3_ffn_sw1, L3_ffn_sb1, L3_ffn_sw2, L3_ffn_sb2, L3_ffn_rw1, L3_ffn_rb1, L3_ffn_rw2, L3_ffn_rb2)
    return x

_drawn_inputs = setup_inputs


def setup_inputs(seed=0):
    import zlib

    import numpy as np

    out = dict(_drawn_inputs(seed))
    spreads = {'L1_xattn_wq_b': (0.0, 0.1),
     'L1_xattn_wk_b': (0.0, 0.8),
     'L1_xattn_wv_b': (0.0, 0.1),
     'L1_xattn_wo_b': (0.0, 0.1),
     'L2_ffn_norm_weight': (1.0, 0.2),
     'L2_ffn_sb1': (0.0, 0.1),
     'L2_ffn_sb2': (0.0, 0.1),
     'L2_ffn_eb1': (0.0, 0.282),
     'L2_ffn_eb2': (0.0, 0.1),
     'L3_ffn_router_b': (0.0, 0.8),
     'L3_ffn_sb1': (0.0, 0.518),
     'L3_ffn_sb2': (0.0, 0.1),
     'L3_ffn_rb1': (0.0, 0.8),
     'L3_ffn_rb2': (0.0, 0.515)}
    factors = {'g_ffn': 7.802,
     'L3_xattn_b': 4.236,
     'L3_ffn_router_w': 3.242,
     'L3_ffn_rw1': 4.671,
     'L3_ffn_rw2': 4.351}
    for name, (base, spread) in spreads.items():
        noise = np.random.default_rng([zlib.crc32(name.encode()), seed]).standard_normal(out[name].shape)
        drawn = base * np.exp(spread * noise) if base else spread * noise
        out[name] = jnp.asarray(drawn.astype(out[name].dtype))
    for name, factor in factors.items():
        out[name] = (out[name] * factor).astype(out[name].dtype)
    return out
```

```python
from contextlib import ExitStack

import numpy as np
import concourse.bass as bass
from concourse import mybir
from concourse.alu_op_type import AluOpType as ALU

F32 = mybir.dt.float32
I32 = mybir.dt.int32
U32 = mybir.dt.uint32
ACT = mybir.ActivationFunctionType
AX = mybir.AxisListType

P = 128
D = 256
DK = D // P
B = 2
S = 1024
T = B * S
NT = T // P
NTB = NT // B
S2 = 154
KH = S2 // 2
E = 8
TOPK = 2
SLOT_TILES = T * TOPK // P + E - 1
ROWS = (NT + SLOT_TILES) * P
HEADS = 16
DH = D // HEADS
HC = HEADS // DK
M = 64
NEG = 1.0e9
LAYERS = 4

UP = [1024, 1024, 1024, 512]
HID = [1024, 512, 1024, 512]
SHARED = [True, False, True, True]
WSLOTS = [E + SHARED[l] for l in range(LAYERS)]
WSIZE = [DK * UP[l] + HID[l] // P * D for l in range(LAYERS)]
ETILES = [SLOT_TILES + NT * SHARED[l] for l in range(LAYERS)]


def bass_flamingo_moe_kernel(nc, a, out, xn_rows, y_rows):
    with ExitStack() as ctx:
        def sb(name, shape, dt=F32):
            return ctx.enter_context(nc.sbuf_tensor(name, shape, dt))

        def sem(name):
            return ctx.enter_context(nc.semaphore(name))

        def sems(name, n=2):
            return [sem(f"{name}{k}") for k in range(n)]

        X = sb("X", [P, NT, D])
        W = sb("W", [P, max(WSLOTS[l] * WSIZE[l] for l in range(LAYERS))])
        arena = sb("arena", [P, 4 * 1024])
        misc = sb("misc", [P, 2560])
        xn = sb("xn", [P, 2, D])
        xT = sb("xT", [P, 2, DK, P])
        tiles = sb("tiles", [P, 4 * D])
        ident = sb("ident", [P, P])
        ones = sb("ones", [P, P])
        upper = sb("upper", [P, P])
        ctxT = sb("ctxT", [P, DK, B, S2])
        ctxr = sb("ctxr", [KH, 2, B, D + 1])
        projT = sb("projT", [P, DK, M])
        gateT = sb("gateT", [P, LAYERS, DK, E])
        tg = sb("tg", [P, 2 * LAYERS])
        junk = sb("junk", [1, 3])
        eps = sb("eps", [P, 2])
        MV = sb("MV", [P, NT, 2])
        STD = sb("STD", [P, NT])
        RSTD = sb("RSTD", [P, NT])
        VT = sb("VT", [P, NT])
        st6 = sb("st6", [P, NT, 6])
        g1 = sb("g1", [P, NT])
        g2 = sb("g2", [P, NT])
        pos = sb("pos", [P, NT, 2], I32)
        etab = sb("etab", [1, NT + SLOT_TILES], I32)
        idx = sb("idx", [P, 2, 2, 1], U32)
        b1T = sb("b1T", [P, (E + 1) * 8])
        bqk = sb("bqk", [P, 2, DK])
        headm = sb("headm", [P, HC])
        simw = sb("simw", [P, 3, DK])
        bsim = sb("bsim", [1, 1])
        rb3 = sb("rb3", [P, E])
        small = sb("small", [P, 24])
        rs = sb("rs", [P, 2, HEADS])
        rr = sb("rr", [P, 2, HEADS])
        MX = sb("MX", [P, NT])
        EB = sb("EB", [P, NT])
        simrow = sb("simrow", [1, B, S2])
        downb = sb("downb", [P, E])
        tidx = sb("tidx", [1, SLOT_TILES, E])
        tsum = sb("tsum", [1, SLOT_TILES])
        cnti = sb("cnti", [P, E], I32)
        cntf = sb("cntf", [P, 3, E])
        negm = sb("negm", [P, 2, HC * 2])

        xs = tiles[:, 0:2 * D].rearrange("p (u n) -> p u n", u=2)
        ybuf = tiles[:, 2 * D:4 * D].rearrange("p (u n) -> p u n", u=2)
        KVZ = arena[0:M, 0:B * (D + 1)].rearrange("p (b n) -> p b n", b=B)
        rfk = arena[0:KH, 1024:1280].rearrange("p (s b m) -> p s b m", s=2, b=B)
        rf = arena[0:M, 2048:2304].rearrange("p (u n) -> p u n", u=2)
        tcmp = arena[0:1, 3072 + 392:3072 + 704].rearrange("p (i e) -> p i e", e=E)
        h = arena[:, 0:2048].rearrange("p (u n) -> p u n", u=2)
        hT = arena[:, 2048:4096].rearrange("p (u n) -> p u n", u=2)
        ygat = arena[:, 0:1536].rearrange("p (u r n) -> p u r n", u=2, r=3)
        qkvo = arena[:, 1536:3584].rearrange("p (w k n) -> p w k n", w=4, k=DK)
        XN = arena[:, :].rearrange("p (i n) -> p i n", i=NT)
        qT = arena[:, 0:512].rearrange("p (u c n) -> p u c n", u=2, c=DK)
        hcW = arena[:, 0:1024].rearrange("p (b k n) -> p b k n", b=B, k=DK)
        AT2 = arena[:, 1024:1536].rearrange("p (u n) -> p u n", u=2)
        A2 = arena[:, 1536:1536 + 2 * S2].rearrange("p (u n) -> p u n", u=2)
        hqT = arena[:, 2048:2560].rearrange("p (u n) -> p u n", u=2)
        xhT = arena[:, 2560:3072].rearrange("p (u n) -> p u n", u=2)
        Rt = arena[:, 3072:4096]
        w_end = WSLOTS[1] * WSIZE[1]
        KBD = W[:, w_end:w_end + 4928].rearrange("p (c b h s) -> p c b h s", c=DK, b=B, h=HC)
        PR = W[:, w_end + 4928:w_end + 9856].rearrange("p (u h s) -> p u h s", u=2, h=HEADS)
        PT = W[0:KH, w_end + 9856:w_end + 11904].rearrange("p (g n) -> p g n", g=4)
        kT = PR[:, 0, 0:4, :].rearrange("p h s -> p (h s)").rearrange("p (c n) -> p c n", c=DK)
        Vh = [xs, ybuf]
        msk = misc[:, 0:2 * S2].bitcast(I32).rearrange("p (u s) -> p u s", u=2)
        side = misc[:, 2 * S2:4 * S2].rearrange("p (u s) -> p u s", u=2)
        neg = misc[:, 4 * S2:6 * S2].rearrange("p (u s) -> p u s", u=2)
        bvr = misc[0:KH, 1024:1280]
        orow = misc[:, 1280:1536]
        obuf = misc[:, 1536:2048].rearrange("p (u n) -> p u n", u=2)
        oT = misc[:, 2048:2560].rearrange("p (u n) -> p u n", u=2)
        Wqv = misc[:, 0:2048].rearrange("p (k n) -> p k n", k=4 * DK)
        qvrow = misc[:, 2048:2304]
        W3x = misc[:, 0:1024].rearrange("p (w k n) -> p w k n", w=2, k=DK)
        rowB = misc[:, 1024:1536].rearrange("p (b n) -> p b n", b=B)
        b3row = misc[:, 1536:1792]
        csum = small[:, 0:4].rearrange("p (k b) -> p k b", k=DK)
        b2b = misc[:, 0:(E + 1) * D]
        nwrow = misc[:, 2304:2560]
        CW = tiles[:, 0:DK * B * S2].rearrange("p (k b s) -> p k b s", k=DK, b=B)

        ps = [ctx.enter_context(nc.psum_tensor(f"ps{k}", [P, 512], F32)) for k in range(8)]

        x_in, ctx_in, w_shared, w_in = sem("x_in"), sem("ctx_in"), sem("w_shared"), sem("w_in")
        xw_in, b2_in, pad_in, padz = sem("xw_in"), sem("b2_in"), sem("pad_in"), sem("padz")
        consts, consts_v, tg_ready = sem("consts"), sem("consts_v"), sem("tg_ready")
        stats, std_ready = sem("stats"), sem("std_ready")
        xn_ready, t_done, xT_ready = sem("xn_ready"), sem("t_done"), sem("xT_ready")
        xn_copied = sem("xn_copied")
        x_done = sem("x_done")
        set_pe, set_act, set_v, set_pool = sem("set_pe"), sem("set_act"), sem("set_v"), sem("set_pool")
        r_done, rf_ready, o_done = sem("r_done"), sem("rf_ready"), sem("o_done")
        q_done, q_ready = sem("q_done"), sem("q_ready")
        s_done, l_ready, e_ready, p_ready = sem("s_done"), sem("l_ready"), sem("e_ready"), sem("p_ready")
        pt_done, pt_v, pt_a, pv_done = sem("pt_done"), sem("pt_v"), sem("pt_a"), sem("pv_done")
        pvh = sem("pvh")
        on_ready, ot_done, ot_ready = sem("on_ready"), sem("ot_done"), sem("ot_ready")
        side_in, neg_ready = sems("side_in"), sem("neg_ready")
        mx_ready, a_ready, an_ready, at_done, at_ready = (sem("mx_ready"), sem("a_ready"), sem("an_ready"),
                                                          sem("at_done"), sem("at_ready"))
        hq_done, hq_ready = sem("hq_done"), sem("hq_ready")
        xn_stored, lg_done, lg_used = sems("xn_stored"), sem("lg_done"), sem("lg_used")
        rt_act, rt_v, rt_pe = sem("rt_act"), sem("rt_v"), sem("rt_pe")
        pos_ready, pool_step = sem("pos_ready"), sem("pool_step")
        sc_in, sc_out = sems("sc_in"), sems("sc_out")
        xs_in, et_done, exT_ready = sems("xs_in"), sem("et_done"), sem("exT_ready")
        u_done, half_ready, h_ready, ht_done, hT_ready = (sem("u_done"), sem("half_ready"), sem("h_ready"),
                                                          sem("ht_done"), sem("hT_ready"))
        d_done, y_ready, y_stored = sem("d_done"), sem("y_ready"), sems("y_stored")
        y_in, ysh_in, c_done = sems("y_in"), sems("ysh_in"), sem("c_done")
        out_stored, x0_stats = sem("out_stored"), sem("x0_stats")
        v_step = [sem(f"v_step{l}") for l in range(LAYERS)]
        mx1, route, simset, gate_in, vready = sem("mx1"), sem("route"), sem("simset"), sem("gate_in"), sem("vready")

        def wait(eng, s, value):
            if type(value) is int and value <= 0:
                return
            eng.wait_ge(s, value)

        def alone(eng):
            eng.wait_ge(consts, 10)

        def alone_pool(u):
            return nc.gpsimd.tensor_tensor(junk[:, u:u + 1], ones[0:1, 0:1], ones[0:1, 0:1], ALU.mult)

        class Steps:
            def __init__(self, eng, s, count=0):
                self.eng, self.s, self.count = eng, s, count

            def then(self, ins):
                self.mark(ins)
                self.eng.wait_ge(self.s, self.count)

            def mark(self, ins):
                self.count = self.count + 1
                ins.then_inc(self.s, 1)

        def loop(eng, steps, first, last, body):
            before = steps.count if steps else 0
            n0 = probe[0] if steps else 0
            with eng.Fori(first, last) as q:
                if steps and n0:
                    steps.count = before + (q - first) * n0
                body(q)
            if steps:
                steps.count = before + (last - first) * n0

        probe = [0]

        def token_tiles(eng, steps, body):
            def pair(q, b, end=False):
                for u in range(2):
                    body(2 * q + u, u, q, b, 0 if not end else (1 if u == 0 else 2))
            before = steps.count if steps else 0
            pair(0, 0)
            probe[0] = steps.count - before if steps else 0
            loop(eng, steps, 1, NTB // 2, lambda q: pair(q, 0))
            loop(eng, steps, NTB // 2, NT // 2 - 1, lambda q: pair(q, 1))
            pair(NT // 2 - 1, 1, True)

        def expert_tiles(eng, steps, n, body, at=None, between=None):
            q1 = (n - 3) // 2
            def pair(q):
                for u in range(2):
                    body(2 * q + u, u, q, 3)
            before = steps.count if steps else 0
            pair(0)
            probe[0] = steps.count - before if steps else 0
            if between:
                loop(eng, steps, 1, at, pair)
                between()
                loop(eng, steps, at, q1, pair)
            else:
                loop(eng, steps, 1, q1, pair)
            for k in range(3):
                i = 2 * q1 + k
                body(i, i % 2, i // 2, 2 - k)

        FX = [0, 32, 64, 112]
        FX2 = 80
        FG = [16, 48, 96, 128]
        EB0 = [sum(ETILES[:l]) for l in range(LAYERS)]
        EP = [[sum((ETILES[k] + 1 - u) // 2 for k in range(l)) for u in range(2)] for l in range(LAYERS + 1)]

        block = ctx.enter_context(nc.Block())

        @block.sync
        def _(sp):
            sp.dma_start(X[:, :, :], a["x"].rearrange("(i p) d -> p i d", p=P)).then_inc(x_in, 16)
            first = [(ctxT[:, :, :, :], a["ctxT"]), (ctxr[:, :, :, 0:D], a["ctxr"]), (projT[:, :, :], a["projT"]),
                     (gateT[:, :, :, :], a["gateT"]), (small[:, 16:24], a["gates"].partition_broadcast(P)),
                     (bqk[:, :, :], a["bqk"]), (simw[:, :, :], a["simw"]), (bsim[:, :], a["bsim"]),
                     (rb3[:, :], a["rb3"].partition_broadcast(P))]
            for dst, src in first:
                sp.dma_start(dst, src).then_inc(ctx_in, 16)

            def weights(l):
                for e in reversed(range(WSLOTS[l])):
                    shared = SHARED[l] and e == E
                    sp.dma_start(W[:, e * WSIZE[l]:(e + 1) * WSIZE[l]],
                                 a[f"w{l}"][e]).then_inc(w_shared if shared else w_in, 16)
            weights(0)

            for l in range(LAYERS):
                def store_xn(i, u, q, b, last):
                    wait(sp, xn_ready, FG[l] + i + 1)
                    sp.dma_start(xn_rows[bass.ds(i * P, P), :], xn[:, u, :]).then_inc(xn_stored[u], 16)
                if l == 2:
                    sp.wait_ge(x_done, (l + 1) * NT)
                    sp.dma_start(nwrow, a["nw"].partition_broadcast(P)).then_inc(xw_in, 16)
                if l >= 2:
                    sp.wait_ge(x_done, (l + 1) * NT)
                    sp.dma_start(b2b, a[f"b2_{l}"].partition_broadcast(P)).then_inc(b2_in, 16)
                    sp.dma_start(b1T[:, 0:(E + 1) * HID[l] // P], a[f"b1_{l}"]).then_inc(b2_in, 16)
                token_tiles(sp, None, store_xn)
                for u in range(2):
                    sp.wait_ge(xn_stored[u], 16 * NTB * (l + 1))

                n, base = ETILES[l], 0 if SHARED[l] else NT

                def sorted_rows_ready():
                    for u in range(2):
                        sp.wait_ge(sc_out[u], 32 * NTB * (l + 1))
                    sp.wait_ge(w_in, 16 * E * (l + 1))

                def rows(i, u, q, left):
                    wait(sp, et_done, EB0[l] + i - 1 if not (type(i) is int and i < 2) else EB0[l])
                    sp.dma_start(xs[:, u, :], xn_rows[bass.ds((i + base) * P, P), :]).then_inc(xs_in[u], 16)
                    if type(i) is int and i < 2:
                        return
                    store(i - 2, u)

                def store(i, u):
                    wait(sp, y_ready, EB0[l] + i + 1)
                    sp.dma_start(y_rows[bass.ds((i + base) * P, P), :], ybuf[:, u, :]).then_inc(y_stored[u], 16)

                if SHARED[l]:
                    expert_tiles(sp, None, n, rows, NT // 2, sorted_rows_ready)
                else:
                    sorted_rows_ready()
                    expert_tiles(sp, None, n, rows)
                store(n - 2, (n - 2) % 2)
                store(n - 1, (n - 1) % 2)
                if l + 1 < LAYERS:
                    sp.wait_ge(d_done, EB0[l] + n)
                    if l == 0:
                        for w in range(4):
                            sp.dma_start(qkvo[:, w, :, :], a["qkvo"][w]).then_inc(xw_in, 16)
                        sp.dma_start(bvr, a["bv"].partition_broadcast(KH)).then_inc(xw_in, 16)
                        sp.dma_start(orow, a["bo"].partition_broadcast(P)).then_inc(xw_in, 16)
                    if l == 1:
                        sp.dma_start(Wqv, a["Wqv"]).then_inc(xw_in, 16)
                        sp.dma_start(qvrow, a["bqv"].partition_broadcast(P)).then_inc(xw_in, 16)
                    if l == 2:
                        sp.dma_start(W3x, a["W3x"]).then_inc(xw_in, 16)
                        sp.dma_start(b3row, a["b3"].partition_broadcast(P)).then_inc(xw_in, 16)
                    weights(l + 1)
            sp.wait_ge(c_done, LAYERS * NT)
            sp.dma_start(out.rearrange("(i p) d -> p i d", p=P), X[:, :, :]).then_inc(out_stored, 16)
            sp.wait_ge(out_stored, 16)

        @block.gpsimd
        def _(pool):
            st = Steps(pool, pool_step)
            st.mark(pool.memset(ident[:, :], 0.0))
            st.mark(pool.memset(upper[:, :], 0.0))
            st.mark(pool.memset(headm[:, :], 1.0))
            st.then(pool.memset(misc[:, :], 0.0))
            for i in range(8):
                k0, k1 = SLOT_TILES * i // 8, SLOT_TILES * (i + 1) // 8
                pool.dma_start(xn_rows[(NT + k0) * P:(NT + k1) * P, :].rearrange("(p r) d -> p (r d)", p=P),
                               misc[:, 0:(k1 - k0) * D]).then_inc(pad_in, 16)
            pool.memset(ones[:, :], 1.0).then_inc(consts, 1)
            pool.memset(ctxr[:, :, :, D:D + 1], 1.0).then_inc(consts, 1)
            pool.memset(eps[:, 0:1], 1e-5).then_inc(consts, 1)
            pool.memset(eps[:, 1:2], 1e-8).then_inc(consts, 1)
            pool.affine_select(out=ident[:, :], in_=ident[:, :], compare_op=ALU.not_equal, fill=1.0, base=0,
                               pattern=[[-1, P]], channel_multiplier=1).then_inc(consts, 1)
            pool.affine_select(out=upper[:, :], in_=upper[:, :], compare_op=ALU.is_ge, fill=1.0, base=0,
                               pattern=[[-1, P]], channel_multiplier=1).then_inc(consts, 1)
            st.then(pool.affine_select(out=headm[:, :], in_=headm[:, :], compare_op=ALU.is_ge, fill=0.0, base=0,
                                       pattern=[[-DH, HC]], channel_multiplier=1))
            pool.affine_select(out=headm[:, :], in_=headm[:, :], compare_op=ALU.is_ge, fill=0.0, base=DH - 1,
                               pattern=[[DH, HC]], channel_multiplier=-1).then_inc(consts, 1)
            pool.iota(downb[:, :], pattern=[[-1, E]], base=E, channel_multiplier=0,
                      allow_small_or_imprecise_dtypes=True).then_inc(consts, 1)
            pool.iota(tidx[:, :, :], pattern=[[1, SLOT_TILES], [0, E]], base=0, channel_multiplier=0,
                      allow_small_or_imprecise_dtypes=True).then_inc(consts, 1)
            pool.iota(etab[:, 0:NT], pattern=[[0, NT]], base=E, channel_multiplier=0).then_inc(consts, 1)

            for l in range(LAYERS):
                if l == 1:
                    def load(i, u, q):
                        wait(pool, p_ready, 2 * (i - 1))
                        wait(pool, neg_ready, i - 1)
                        pool.dma_start(msk[:, u, :], a["mask"][bass.ds(i * P, P), :]).then_inc(side_in[u], 16)
                        pool.dma_start(side[:, u, :], a["side"][bass.ds(i * P, P), :]).then_inc(side_in[u], 16)

                    def mask(i, u, q):
                        wait(pool, side_in[u], 32 * (q + 1))
                        wait(pool, l_ready, 2 * (i - 1))
                        alone_pool(u)
                        pool.tensor_scalar(neg[:, u, :], msk[:, u, :], 1.0, NEG, ALU.subtract,
                                           ALU.mult).then_inc(neg_ready, 1)

                    def weigh(i, u, q):
                        for c in range(DK):
                            wait(pool, e_ready, 2 * i + c + 1)
                            v = PR[:, u, c * HC:(c + 1) * HC, :]
                            pool.tensor_tensor(v, v, side[:, u, :].unsqueeze(1).to_broadcast([P, HC, S2]),
                                               ALU.mult).then_inc(p_ready, 1)
                    pool.wait_ge(d_done, EB0[1])
                    load(0, 0, 0)
                    load(1, 1, 0)
                    mask(0, 0, 0)
                    weigh(0, 0, 0)
                    mask(1, 1, 0)

                    def body(i, u, q, b, last):
                        if not last:
                            load(i + 2, u, q + 1)
                        if last < 2:
                            weigh(i + 1, 1 - u, q + u)
                        if not last:
                            mask(i + 2, u, q + 1)
                    token_tiles(pool, None, body)
                if l == 2:
                    pool.wait_ge(set_v, 6)
                    pool.partition_all_reduce(small[:, 6:8], small[:, 4:6], P,
                                              bass.bass_isa.ReduceOp.max).then_inc(set_pool, 1)

                pool.wait_ge(pos_ready, 2 * l + 1)
                if l == 0:
                    pool.wait_ge(pad_in, 16 * 8)
                for u in range(2):
                    pool.wait_ge(xn_stored[u], 16 * NTB * (l + 1))

                def places(i, u):
                    st.mark(pool.tensor_copy(idx[:, u, 0, :], pos[:, i, 0:1].bitcast(U32)))
                    st.then(pool.tensor_copy(idx[:, u, 1, :], pos[:, i, 1:2].bitcast(U32)))

                def scatter(i, u, q, b, last):
                    wait(pool, sc_out[u], 32 * (NTB * l + q))
                    pool.dma_start(xn[:, u, :], xn_rows[bass.ds(i * P, P), :]).then_inc(sc_in[u], 16)
                    places(i, u)
                    wait(pool, sc_in[u], 16 * (NTB * l + q + 1))
                    st.mark(alone_pool(2))
                    for k in range(TOPK):
                        pool.indirect_dma_start(xn_rows[:, :], bass.IndirectOffsetOnAxis(ap=idx[:, u, k, :], axis=0),
                                                xn[:, u, :], None).then_inc(sc_out[u], 16)
                token_tiles(pool, st, scatter)

                def gather(i, u, q, b, last):
                    if type(i) is int and i < 2:
                        wait(pool, sc_out[u], 32 * NTB * (l + 1))
                        wait(pool, y_stored[0], 16 * EP[l + 1][0])
                        wait(pool, y_stored[1], 16 * EP[l + 1][1])
                    else:
                        wait(pool, y_in[u], 32 * (NTB * l + q))
                        wait(pool, c_done, l * NT + i - 1)
                    if SHARED[l]:
                        pool.dma_start(ygat[:, u, 2, :], y_rows[bass.ds(i * P, P), :]).then_inc(ysh_in[u], 16)
                    places(i, u)
                    st.mark(alone_pool(2))
                    for k in range(TOPK):
                        pool.indirect_dma_start(ygat[:, u, k, :], None, y_rows[:, :],
                                                bass.IndirectOffsetOnAxis(ap=idx[:, u, k, :], axis=0)).then_inc(y_in[u], 16)
                token_tiles(pool, st, gather)

        @block.tensor
        def _(pe):
            def transpose_x(f, u):
                wait(pe, xn_ready, f + 1)
                wait(pe, xT_ready, f)
                for k in range(DK):
                    m = pe.transpose(ps[5][:, k * P:(k + 1) * P], xn[:, u, k * P:(k + 1) * P], ident[:, :])
                m.then_inc(t_done, 1)

            pe.wait_ge(consts, 10)
            pe.wait_ge(ctx_in, 16 * 9)
            for l in range(LAYERS):
                f0 = FX[l]
                if l == 0:
                    for b in range(B):
                        for s in range(2):
                            for k in range(DK):
                                m = pe.matmul(ps[0][0:KH, (2 * b + s) * M:(2 * b + s + 1) * M],
                                              ctxT[:, k, b, s * KH:(s + 1) * KH], projT[:, k, :],
                                              start=(k == 0), stop=(k == DK - 1))
                    m.then_inc(set_pe, 1)
                    pe.wait_ge(set_act, 1)
                    for b in range(B):
                        for s in range(2):
                            m = pe.matmul(ps[1 + b][0:M, 0:D + 1], rfk[:, s, b, :], ctxr[:, s, b, :],
                                          start=(s == 0), stop=(s == 1))
                    m.then_inc(set_pe, 1)
                    pe.wait_ge(set_v, 1)

                    def features(i, u):
                        wait(pe, xT_ready, f0 + i + 1)
                        wait(pe, rf_ready, i)
                        for k in range(DK):
                            m = pe.matmul(ps[0][0:M, 0:P], projT[:, k, :], xT[:, u, k, :],
                                          start=(k == 0), stop=(k == DK - 1))
                        m.then_inc(r_done, 1)
                    transpose_x(f0, 0)
                    features(0, 0)

                    def body(i, u, q, b, last):
                        if last < 2:
                            transpose_x(f0 + i + 1, 1 - u)
                        wait(pe, rf_ready, i + 1)
                        wait(pe, x_done, i)
                        pe.matmul(ps[1][:, 0:D + 1], rf[:, u, :], KVZ[:, b, :], start=True, stop=True).then_inc(o_done, 1)
                        if last < 2:
                            features(i + 1, 1 - u)
                    token_tiles(pe, None, body)
                if l == 1:
                    pe.wait_ge(xw_in, 16 * 6)
                    for c in range(DK):
                        for k in range(DK):
                            m = pe.matmul(ps[c][:, 0:B * S2], qkvo[:, 1, k, c * P:(c + 1) * P],
                                          ctxT[:, k, :, :].rearrange("p b s -> p (b s)"),
                                          start=(k == 0), stop=(k == DK - 1))
                    m.then_inc(set_pe, 1)
                    for b in range(B):
                        for s in range(2):
                            for k in range(DK):
                                m = pe.matmul(ps[2 + b][0:KH, s * D:(s + 1) * D], ctxT[:, k, b, s * KH:(s + 1) * KH],
                                              qkvo[:, 2, k, :], start=(k == 0), stop=(k == DK - 1))
                    m.then_inc(set_pe, 1)
                    pe.wait_ge(set_v, 5)
                    pe.wait_ge(vready, 1)

                    def queries(i, u):
                        wait(pe, xT_ready, f0 + i + 1)
                        wait(pe, q_ready, i)
                        for c in range(DK):
                            for k in range(DK):
                                m = pe.matmul(ps[1][:, c * P:(c + 1) * P], qkvo[:, 0, k, c * P:(c + 1) * P],
                                              xT[:, u, k, :], start=(k == 0), stop=(k == DK - 1))
                        m.then_inc(q_done, 1)

                    def scores(i, u, b):
                        wait(pe, q_ready, i + 1)
                        for c in range(DK):
                            wait(pe, l_ready, 2 * i + c)
                            for g in range(3):
                                n = min(3, HC - 3 * g)
                                m = pe.matmul(ps[2 + g][:, 0:n * S2], qT[:, u, c, :],
                                              KBD[:, c, b, 3 * g:3 * g + n, :].rearrange("p h s -> p (h s)"),
                                              start=True, stop=True)
                            m.then_inc(s_done, 1)

                    def values(i, u, b):
                        def turn(g):
                            if g % 4 == 0:
                                wait(pe, p_ready, 2 * i + g // 4 + 1)
                            wait(pe, pt_a if g % 2 else pt_v, 4 * i + g // 2)
                            for j in range(4):
                                hh, s = 2 * g + j // 2, j % 2
                                m = pe.transpose(ps[6 if g % 2 == 0 else 0][0:KH, j * P:(j + 1) * P],
                                                 PR[:, u, hh, s * KH:(s + 1) * KH], ident[:, :])
                            m.then_inc(pt_done, 1)

                        def product(g):
                            wait(pe, pt_a if g % 2 else pt_v, 4 * i + g // 2 + 1)
                            if g == 0:
                                wait(pe, x_done, NT + i)
                            for j in range(4):
                                hh, s = 2 * g + j // 2, j % 2
                                m = pe.matmul(ps[7][:, hh * DH:(hh + 1) * DH], PT[:, g % 4, j * P:(j + 1) * P],
                                              Vh[b][0:KH, s, hh * DH:(hh + 1) * DH], start=(s == 0), stop=(s == 1))
                            m.then_inc(pv_done, 1)
                        turn(0)
                        for g in range(1, 8):
                            turn(g)
                            product(g - 1)
                        product(7)
                        wait(pe, on_ready, i + 1)
                        for k in range(DK):
                            m = pe.transpose(ps[7][:, 256 + k * P:256 + (k + 1) * P], obuf[:, u, k * P:(k + 1) * P], ident[:, :])
                        m.then_inc(ot_done, 1)

                    def project(i, u):
                        wait(pe, ot_ready, i + 1)
                        for k in range(DK):
                            m = pe.matmul(ps[7][:, 0:256], oT[:, u, k * P:(k + 1) * P], qkvo[:, 3, k, :],
                                          start=(k == 0), stop=(k == DK - 1))
                        m.then_inc(o_done, 1)
                    transpose_x(f0, 0)
                    queries(0, 0)
                    transpose_x(f0 + 1, 1)
                    scores(0, 0, 0)
                    queries(1, 1)

                    def body(i, u, q, b, last, f0=f0):
                        if not last:
                            transpose_x(f0 + i + 2, u)
                        if last < 2:
                            scores(i + 1, 1 - u, (i + 1) // NTB)
                        values(i, u, b)
                        if not last:
                            queries(i + 2, u)
                        project(i, u)

                    token_tiles(pe, None, body)
                if l == 2:
                    pe.wait_ge(simset, 1)
                    for b in range(B):
                        for k in range(DK):
                            m = pe.matmul(ps[6][0:1, b * S2:(b + 1) * S2], simw[:, 1, k:k + 1], ctxT[:, k, b, :],
                                          start=(k == 0), stop=(k == DK - 1))
                    m.then_inc(set_pe, 1)
                    pe.wait_ge(simset, 2)

                    def similarity(i, u, b, n, used):
                        wait(pe, xT_ready, n + 1)
                        wait(pe, *used)
                        for k in range(DK):
                            pe.matmul(ps[2][:, 0:S2], xT[:, u, k, :], CW[:, k, b, :], start=(k == 0), stop=False)
                        pe.matmul(ps[2][:, 0:S2], ones[0:1, :], simrow[0:1, b, :], start=False, stop=True).then_inc(s_done, 1)
                    S0 = 2 * NT
                    transpose_x(f0, 0)

                    def body(i, u, q, b, last, f0=f0):
                        if last < 2:
                            transpose_x(f0 + i + 1, 1 - u)
                        similarity(i, u, b, f0 + i, (mx_ready, i))
                    token_tiles(pe, None, body)
                    pe.wait_ge(set_act, 4)
                    pe.wait_ge(xn_copied, NT)
                    for b in range(B):
                        for k in range(DK):
                            for j in range(NTB):
                                i = b * NTB + j
                                m = pe.matmul(ps[6][:, 2 * b + k:2 * b + k + 1], XN[:, i, k * P:(k + 1) * P],
                                              EB[:, i:i + 1], start=(j == 0), stop=(j == NTB - 1))
                    m = pe.matmul(ps[6][:, 4:6], ones[:, :], small[:, 8:10], start=True, stop=True)
                    m.then_inc(set_pe, 1)
                    pe.wait_ge(simset, 3)
                    f1 = FX2

                    def mix(i, u, b):
                        wait(pe, an_ready, i + 1)
                        wait(pe, at_ready, i)
                        for s in range(2):
                            m = pe.transpose(ps[3][0:KH, s * P:(s + 1) * P], A2[:, u, s * KH:(s + 1) * KH], ident[:, :])
                        m.then_inc(at_done, 1)
                        wait(pe, at_ready, i + 1)
                        wait(pe, hq_ready, 2 * i)
                        for k in range(DK):
                            for s in range(2):
                                m = pe.matmul(ps[4][:, k * P:(k + 1) * P], ctxr[:, s, b, k * P:(k + 1) * P],
                                              AT2[0:KH, u, s * P:(s + 1) * P], start=(s == 0), stop=(s == 1))
                        m.then_inc(hq_done, 1)

                    def project(i, u, b):
                        wait(pe, x_done, 2 * NT + i)
                        for k in range(DK):
                            pe.matmul(ps[7][:, 0:D], xT[:, u, k, :], hcW[:, b, k, :], start=(k == 0), stop=False)
                        wait(pe, hq_ready, 2 * (i + 1))
                        for k in range(DK):
                            pe.matmul(ps[7][:, 0:D], hqT[:, u, k * P:(k + 1) * P], Wqv[:, DK + k, :], start=False, stop=False)
                        for k in range(DK):
                            m = pe.matmul(ps[7][:, 0:D], xhT[:, u, k * P:(k + 1) * P], Wqv[:, 2 * DK + k, :],
                                          start=False, stop=(k == DK - 1))
                        m.then_inc(o_done, 1)
                    transpose_x(f1, 0)
                    similarity(0, 0, 0, f1, (mx_ready, NT))
                    transpose_x(f1 + 1, 1)

                    def body(i, u, q, b, last, f1=f1):
                        if last < 2:
                            similarity(i + 1, 1 - u, (i + 1) // NTB, f1 + i + 1, (a_ready, i + 1))
                        mix(i, u, b)
                        project(i, u, b)
                        if not last:
                            transpose_x(f1 + i + 2, u)
                    token_tiles(pe, None, body)
                if l == 3:
                    pe.wait_ge(simset, 4)
                    for b in range(B):
                        for k in range(DK):
                            m = pe.matmul(ps[6][:, b * D:(b + 1) * D], csum[:, k, b:b + 1].to_broadcast([P, P]),
                                          W3x[:, 1, k, :], start=(k == 0), stop=(k == DK - 1))
                    m.then_inc(set_pe, 1)
                    transpose_x(f0, 0)

                    def body(i, u, q, b, last, f0=f0):
                        if last < 2:
                            transpose_x(f0 + i + 1, 1 - u)
                        wait(pe, xT_ready, f0 + i + 1)
                        wait(pe, x_done, 3 * NT + i)
                        for k in range(DK):
                            m = pe.matmul(ps[1][:, 0:D], xT[:, u, k, :], W3x[:, 0, k, :], start=(k == 0), stop=(k == DK - 1))
                        m.then_inc(o_done, 1)
                    token_tiles(pe, None, body)

                g0 = FG[l]
                transpose_x(g0, 0)

                def body(i, u, q, b, last, g0=g0, l=l):
                    if last < 2:
                        transpose_x(g0 + i + 1, 1 - u)
                    wait(pe, xT_ready, g0 + i + 1)
                    wait(pe, lg_used, l * NT + i)
                    for k in range(DK):
                        m = pe.matmul(ps[6][:, 0:E], xT[:, u, k, :], gateT[:, l, k, :], start=(k == 0), stop=(k == DK - 1))
                    m.then_inc(lg_done, 1)
                token_tiles(pe, None, body)
                pe.wait_ge(rt_v, 2 * l + 2)
                cnt = Rt[:, 0:(NT + 1) * E]
                pe.matmul(ps[7][:, 0:(NT + 1) * E], ones[:, :],
                          cnt[:, NT * E:].unsqueeze(1).to_broadcast([P, NT + 1, E]), start=True, stop=False)
                for i in range(NT):
                    pe.matmul(ps[7][:, (i + 1) * E:(NT + 1) * E], ones[:, :],
                              cnt[:, i * E:(i + 1) * E].unsqueeze(1).to_broadcast([P, NT - i, E]),
                              start=False, stop=False)
                pe.matmul(ps[7][:, 0:(NT + 1) * E], upper[:, :], cnt, start=False, stop=True).then_inc(rt_pe, 1)

                n, e0, up, hid = ETILES[l], EB0[l], UP[l], HID[l]
                nb, nh = up // 512, hid // P
                if SHARED[l]:
                    pe.wait_ge(w_shared, 16 * sum(SHARED[:l + 1]))

                def take(i, u, q):
                    wait(pe, xs_in[u], 16 * (EP[l][u] + q + 1))
                    wait(pe, exT_ready, e0 + i)
                    for k in range(DK):
                        m = pe.transpose(ps[5][:, k * P:(k + 1) * P], xs[:, u, k * P:(k + 1) * P], ident[:, :])
                    m.then_inc(et_done, 1)

                def expert(i):
                    at = i if SHARED[l] else i + NT
                    e = pe.value_load(etab[0:1, bass.ds(at, 1)], min_val=0, max_val=WSLOTS[l] - 1)
                    return e

                def upward(i, u):
                    e = expert(i)
                    wait(pe, exT_ready, e0 + i + 1)
                    wait(pe, h_ready, e0 + i)
                    for n_ in range(nb):
                        for k in range(DK):
                            m = pe.matmul(ps[n_][:, 0:512], xT[:, u, k, :],
                                          W[:, bass.ds(e * WSIZE[l] + (k * up + n_ * 512), 512)],
                                          start=(k == 0), stop=(k == DK - 1))
                    m.then_inc(u_done, 1)
                    return e

                def turn(i, u):
                    wait(pe, h_ready, e0 + i + 1)
                    wait(pe, hT_ready, e0 + i)
                    for c in range(nh):
                        m = pe.transpose(ps[2 + c // 4][:, c % 4 * P:(c % 4 + 1) * P], h[:, u, c * P:(c + 1) * P], ident[:, :])
                    m.then_inc(ht_done, 1)

                def downward(i, u):
                    e = expert(i)
                    wait(pe, hT_ready, e0 + i + 1)
                    wait(pe, y_ready, e0 + i)
                    for c in range(nh):
                        m = pe.matmul(ps[4][:, 0:D], hT[:, u, c * P:(c + 1) * P],
                                      W[:, bass.ds(e * WSIZE[l] + (DK * up + c * D), D)],
                                      start=(c == 0), stop=(c == nh - 1))
                    m.then_inc(d_done, 1)

                take(0, 0, 0)
                upward(0, 0)
                take(1, 1, 0)

                def body(i, u, q, left):
                    turn(i, u)
                    if left > 0:
                        upward(i + 1, 1 - u)
                    downward(i, u)
                    if left > 1:
                        take(i + 2, u, q + 1)
                expert_tiles(pe, None, n, body)

        @block.scalar
        def _(act):
            act.wait_ge(ctx_in, 16 * 9)
            act.activation(tg[:, :], small[:, 16:24], ACT.Tanh).then_inc(tg_ready, 1)
            act.wait_ge(consts, 10)

            def std(n):
                wait(act, stats, NT * (n + 1))
                act.activation(STD[:, :], MV[:, :, 1], ACT.Sqrt, bias=eps[:, 0:1]).then_inc(std_ready, 1)

            nstd = 0
            for l in range(LAYERS):
                std(2 * l)
                if l == 0:
                    act.wait_ge(set_pe, 1)
                    act.activation(rfk[:, :, :, :].rearrange("p s b m -> p b s m"),
                                   ps[0][0:KH, 0:4 * M].rearrange("p (b s m) -> p b s m", b=B, s=2),
                                   ACT.Exp, scale=1.0 / 16.0).then_inc(set_act, 1)

                    def expo(i, u):
                        wait(act, r_done, i + 1)
                        wait(act, o_done, i - 1)
                        act.activation(rf[:, u, :], ps[0][0:M, 0:P], ACT.Exp, scale=1.0 / 16.0).then_inc(rf_ready, 1)
                    expo(0, 0)

                    def body(i, u, q, b, last):
                        if last < 2:
                            expo(i + 1, 1 - u)
                    token_tiles(act, None, body)
                if l == 1:
                    act.wait_ge(set_pe, 3)
                    for c in range(DK):
                        m = act.activation(kT[:, c, :], ps[c][:, 0:B * S2], ACT.Identity, bias=bqk[:, 1, c:c + 1])
                    m.then_inc(set_act, 1)

                    def queries(i, u):
                        wait(act, q_done, i + 1)
                        wait(act, s_done, 2 * (i - 1))
                        for c in range(DK):
                            m = act.activation(qT[:, u, c, :], ps[1][:, c * P:(c + 1) * P], ACT.Identity,
                                               bias=bqk[:, 0, c:c + 1])
                        m.then_inc(q_ready, 1)

                    def expo(i, u, c):
                        wait(act, mx1, 2 * i + c + 1)
                        for j in range(HC):
                            hh = c * HC + j
                            m = act.activation(PR[:, u, hh, :], PR[:, u, hh, :], ACT.Exp, bias=negm[:, u, hh:hh + 1],
                                               accum_out=rs[:, u, hh:hh + 1])
                        m.then_inc(e_ready, 1)

                    def copies(i, half):
                        for g in (1, 3) if half == 0 else (5, 7):
                            wait(act, pt_done, 8 * i + g + 1)
                            wait(act, pv_done, 8 * i + g - 3)
                            act.activation(PT[:, g % 4, :], ps[0][0:KH, :], ACT.Copy).then_inc(pt_a, 1)
                    queries(0, 0)
                    expo(0, 0, 0)
                    expo(0, 0, 1)
                    queries(1, 1)

                    def body(i, u, q, b, last):
                        if last < 2:
                            expo(i + 1, 1 - u, 0)
                        copies(i, 0)
                        if last < 2:
                            expo(i + 1, 1 - u, 1)
                        copies(i, 1)
                        if not last:
                            queries(i + 2, u)
                    token_tiles(act, None, body)
                if l == 2:
                    def keep(i, u):
                        wait(act, xn_ready, FX[2] + i + 1)
                        act.activation(XN[:, i, :], xn[:, u, :], ACT.Copy).then_inc(xn_copied, 1)
                    keep(0, 0)

                    def body(i, u, q, b, last):
                        if last < 2:
                            keep(i + 1, 1 - u)
                    token_tiles(act, None, body)
                    act.wait_ge(set_v, 7)
                    for b in range(B):
                        m = act.activation(EB[:, b * NTB:(b + 1) * NTB], MX[:, b * NTB:(b + 1) * NTB], ACT.Exp,
                                           bias=small[:, 10 + b:11 + b], scale=-1.0, accum_out=small[:, 8 + b:9 + b])
                        m.then_inc(set_act, 1)

                    def expo(i, u):
                        wait(act, s_done, 2 * NT + NT + i + 1)
                        wait(act, at_done, i - 1)
                        wait(act, simset, 3)
                        act.activation(A2[:, u, :], ps[2][:, 0:S2], ACT.Exp, bias=MX[:, i:i + 1] if type(i) is int
                                       else MX[:, bass.ds(i, 1)], accum_out=rs[:, u, 0:1]).then_inc(a_ready, 1)
                    expo(0, 0)

                    def body(i, u, q, b, last):
                        if last < 2:
                            expo(i + 1, 1 - u)
                    token_tiles(act, None, body)
                std(2 * l + 1)
                if l == 2:
                    act.wait_ge(rt_v, 2 * l + 1)
                    act.activation(STD[:, :], VT[:, :], ACT.Sqrt, bias=eps[:, 1:2]).then_inc(rt_act, 1)
                    act.wait_ge(route, 1)
                    act.activation(Rt[:, 896:1024], Rt[:, 136:264], ACT.Sigmoid).then_inc(rt_act, 1)
                elif l == 3:
                    act.wait_ge(route, 2)
                    act.activation(Rt[:, 136:264], Rt[:, 264:392], ACT.Exp).then_inc(rt_act, 1)
                else:
                    act.wait_ge(gate_in, l + 1)
                    act.activation(g2[:, :], g2[:, :], ACT.Exp).then_inc(rt_act, 1)
                n, e0, nh = ETILES[l], EB0[l], HID[l] // P

                def body(i, u, q, left):
                    if l == 0:
                        wait(act, u_done, e0 + i + 1)
                        wait(act, ht_done, e0 + i - 1)
                        for k in range(2):
                            m = act.activation(h[:, u, k * 512:(k + 1) * 512], ps[k][:, :], ACT.Silu)
                        m.then_inc(h_ready, 1)
                    elif l == 1:
                        wait(act, u_done, e0 + i + 1)
                        wait(act, h_ready, e0 + i - 1)
                        act.activation(h[:, u, 512:1024], ps[0][:, :], ACT.Silu).then_inc(half_ready, 1)
                    else:
                        at = i
                        e = act.value_load(etab[0:1, bass.ds(at, 1)], min_val=0, max_val=E)
                        wait(act, ht_done, e0 + i + 1)
                        wait(act, d_done, e0 + i - 1)
                        for c in range(nh):
                            m = act.activation(hT[:, u, c * P:(c + 1) * P], ps[2 + c // 4][:, c % 4 * P:(c % 4 + 1) * P],
                                               ACT.Relu if l == 2 else ACT.Gelu,
                                               bias=b1T[:, bass.ds(e * nh + c, 1)])
                        m.then_inc(hT_ready, 1)
                if l >= 2:
                    act.wait_ge(b2_in, 32 * (l - 1))
                expert_tiles(act, None, n, body)

        @block.vector
        def _(v):
            st = [Steps(v, v_step[0])]

            def then(ins):
                st[0].then(ins)

            def col(t, i):
                return t[:, bass.ds(i, 1)]

            def rstd(n):
                v.wait_ge(std_ready, n + 1)
                then(v.reciprocal(RSTD[:, :], STD[:, :]))

            def norm(i, u, f, extra=()):
                wait(v, t_done, f - 1)
                for s, k in extra:
                    wait(v, s, k)
                return v.tensor_scalar(xn[:, u, :], X[:, i, :], MV[:, i, 0:1], col(RSTD, i), ALU.subtract, ALU.mult)

            def take(u, f, used):
                wait(v, t_done, f + 1)
                for s, k in used:
                    wait(v, s, k)
                v.tensor_copy(xT[:, u, :, :].rearrange("p k n -> p (k n)"), ps[5][:, 0:D]).then_inc(xT_ready, 1)

            def finish(i, s):
                alone(v)
                v.bn_stats(st6[:, i, :], X[:, i, :]).then_inc(s, 1)

            def gather_statistics(s, count):
                v.wait_ge(s, count)
                for i in range(NT):
                    v.bn_aggr(MV[:, i, :], st6[:, i, :]).then_inc(stats, 1)

            v.wait_ge(x_in, 16)
            for i in range(NT):
                v.bn_stats(st6[:, i, :], X[:, i, :]).then_inc(x0_stats, 1)
            gather_statistics(x0_stats, NT)
            v.wait_ge(consts, 10)
            v.wait_ge(ctx_in, 16 * 9)
            v.wait_ge(tg_ready, 1)

            for l in range(LAYERS):
                if l:
                    st[0] = Steps(v, v_step[l])
                f0, tgx, tgf = FX[l], tg[:, l:l + 1], tg[:, LAYERS + l:LAYERS + l + 1]
                stp = st[0]
                rstd(2 * l)
                if l == 0:
                    norm(0, 0, f0).then_inc(xn_ready, 1)
                    v.wait_ge(set_pe, 2)
                    v.tensor_copy(KVZ[:, 0, :], ps[1][0:M, 0:D + 1])
                    v.tensor_copy(KVZ[:, 1, :], ps[2][0:M, 0:D + 1]).then_inc(set_v, 1)
                    take(0, f0, ())

                    def body(i, u, q, b, last):
                        if last < 2:
                            norm(i + 1, 1 - u, f0 + i + 1).then_inc(xn_ready, 1)
                            take(1 - u, f0 + i + 1, [(r_done, i)])
                        v.wait_ge(o_done, i + 1)
                        then(v.tensor_scalar(small[:, 12 + u:13 + u], ps[1][:, D:D + 1], 8e-6, None, ALU.add))
                        then(v.reciprocal(small[:, 14 + u:15 + u], small[:, 12 + u:13 + u]))
                        then(v.tensor_tensor(small[:, 12 + u:13 + u], small[:, 14 + u:15 + u], tgx, ALU.mult))
                        st[0].then(v.scalar_tensor_tensor(X[:, i, :], ps[1][:, 0:D], small[:, 12 + u:13 + u], X[:, i, :],
                                                          ALU.mult, ALU.add))
                        finish(i, x_done)
                    token_tiles(v, stp, body)
                if l == 1:
                    v.wait_ge(set_act, 2)
                    for c in range(DK):
                        for b in range(B):
                            m = v.tensor_tensor(KBD[:, c, b, :, :],
                                                kT[:, c, b * S2:(b + 1) * S2].unsqueeze(1).to_broadcast([P, HC, S2]),
                                                headm[:, :].unsqueeze(2).to_broadcast([P, HC, S2]), ALU.mult)
                            m.then_inc(set_v, 1)
                    v.wait_ge(set_pe, 4)
                    for b in range(B):
                        for s in range(2):
                            m = v.tensor_tensor(Vh[b][0:KH, s, :], ps[2 + b][0:KH, s * D:(s + 1) * D], bvr, ALU.add)
                            if b == 1 and s == 1:
                                m.then_inc(vready, 1)
                    then(v.tensor_scalar(orow, orow, tgx, None, ALU.mult))

                    def logits(i, u):
                        for c in range(DK):
                            wait(v, s_done, 2 * i + c + 1)
                            if c == 0:
                                wait(v, neg_ready, i + 1)
                                wait(v, pt_done, 8 * (i - 1))
                            for g in range(3):
                                n = min(3, HC - 3 * g)
                                m = v.scalar_tensor_tensor(
                                    PR[:, u, c * HC + 3 * g:c * HC + 3 * g + n, :],
                                    ps[2 + g][:, 0:n * S2].rearrange("p (h s) -> p h s", h=n), 0.25,
                                    neg[:, u, :].unsqueeze(1).to_broadcast([P, n, S2]), ALU.mult, ALU.add)
                            m.then_inc(l_ready, 1)
                            wait(v, l_ready, 2 * i + c + 1)
                            v.tensor_reduce(negm[:, u, c * HC:(c + 1) * HC], PR[:, u, c * HC:(c + 1) * HC, :], AX.X,
                                            ALU.max, negate=True).then_inc(mx1, 1)
                    norm(0, 0, f0).then_inc(xn_ready, 1)
                    take(0, f0, ())
                    norm(1, 1, f0 + 1).then_inc(xn_ready, 1)
                    take(1, f0 + 1, ())
                    logits(0, 0)

                    def body(i, u, q, b, last):
                        if not last:
                            norm(i + 2, u, f0 + i + 2).then_inc(xn_ready, 1)
                        if last < 2:
                            logits(i + 1, 1 - u)
                        if not last:
                            take(u, f0 + i + 2, [(q_done, i + 1)])
                        for g in (0, 2, 4, 6):
                            wait(v, pt_done, 8 * i + g + 1)
                            wait(v, pv_done, 8 * i + g - 3)
                            v.tensor_copy(PT[:, g % 4, :], ps[6][0:KH, :]).then_inc(pt_v, 1)
                        wait(v, e_ready, 2 * (i + 1))
                        then(v.reciprocal(rr[:, u, :], rs[:, u, :]))
                        wait(v, pv_done, 8 * (i + 1))
                        v.tensor_tensor(obuf[:, u, :].rearrange("p (h d) -> p h d", h=HEADS),
                                        ps[7][:, 0:D].rearrange("p (h d) -> p h d", h=HEADS),
                                        rr[:, u, :].unsqueeze(2).to_broadcast([P, HEADS, DH]), ALU.mult).then_inc(on_ready, 1)
                        wait(v, ot_done, i + 1)
                        wait(v, o_done, NT + i - 1)
                        v.tensor_copy(oT[:, u, :], ps[7][:, 256:512]).then_inc(ot_ready, 1)
                        wait(v, o_done, NT + i + 1)
                        then(v.scalar_tensor_tensor(X[:, i, :], ps[7][:, 0:256], tgx, X[:, i, :], ALU.mult, ALU.add))
                        then(v.tensor_tensor(X[:, i, :], X[:, i, :], orow, ALU.add))
                        finish(i, x_done)
                    token_tiles(v, stp, body)
                if l == 2:
                    for k in range(DK):
                        m = v.tensor_scalar(CW[:, k, :, :].rearrange("p b s -> p (b s)"),
                                            ctxT[:, k, :, :].rearrange("p b s -> p (b s)"),
                                            simw[:, 2, k:k + 1], simw[:, 0, k:k + 1], ALU.mult, ALU.add)
                    m.then_inc(simset, 1)
                    v.wait_ge(set_pe, 5)
                    v.tensor_scalar(simrow[:, :, :].rearrange("p b s -> p (b s)"), ps[6][0:1, 0:B * S2], bsim[0:1, 0:1],
                                    None, ALU.add).then_inc(simset, 1)
                    norm(0, 0, f0).then_inc(xn_ready, 1)
                    take(0, f0, ())

                    def body(i, u, q, b, last):
                        if last < 2:
                            norm(i + 1, 1 - u, f0 + i + 1, [(xn_copied, i)]).then_inc(xn_ready, 1)
                            take(1 - u, f0 + i + 1, [(s_done, 2 * NT + i)])
                        wait(v, s_done, 2 * NT + i + 1)
                        v.tensor_reduce(col(MX, i), ps[2][:, 0:S2], AX.X, ALU.max, negate=True).then_inc(mx_ready, 1)
                    token_tiles(v, stp, body)
                    v.wait_ge(mx_ready, NT)
                    for b in range(B):
                        m = v.tensor_reduce(small[:, 4 + b:5 + b], MX[:, b * NTB:(b + 1) * NTB], AX.X, ALU.min, negate=True)
                        stp.mark(m)
                    v.wait_ge(v_step[2], stp.count)
                    v.engine_nop().then_inc(set_v, 1)
                    v.wait_ge(set_pool, 1)
                    v.tensor_scalar(small[:, 10:12], small[:, 6:8], -1.0, None, ALU.mult).then_inc(set_v, 1)
                    v.wait_ge(set_pe, 6)
                    v.wait_ge(xw_in, 16 * 8)
                    then(v.reciprocal(small[:, 12:14], ps[6][:, 4:6]))
                    for b in range(B):
                        stp.mark(v.tensor_scalar(csum[:, b, :], ps[6][:, 2 * b:2 * b + 2], small[:, 12 + b:13 + b], None, ALU.mult))
                    v.wait_ge(v_step[2], stp.count)
                    for b in range(B):
                        for k in range(DK):
                            m = v.scalar_tensor_tensor(hcW[:, b, k, :], Wqv[:, 3 * DK + k, :], csum[:, b, k:k + 1],
                                                       Wqv[:, k, :], ALU.mult, ALU.add)
                    stp.mark(m)
                    stp.then(v.tensor_scalar(qvrow, qvrow, tgx, None, ALU.mult))
                    v.engine_nop().then_inc(simset, 1)
                    f1 = FX2

                    def soften(i, u):
                        wait(v, a_ready, i + 1)
                        then(v.reciprocal(rr[:, u, 0:1], rs[:, u, 0:1]))
                        v.tensor_scalar(A2[:, u, :], A2[:, u, :], rr[:, u, 0:1], None, ALU.mult).then_inc(an_ready, 1)
                    norm(0, 0, f1).then_inc(xn_ready, 1)
                    take(0, f1, ())
                    norm(1, 1, f1 + 1).then_inc(xn_ready, 1)
                    take(1, f1 + 1, ())
                    soften(0, 0)

                    def body(i, u, q, b, last):
                        if last < 2:
                            soften(i + 1, 1 - u)
                        wait(v, at_done, i + 1)
                        wait(v, hq_done, i - 1)
                        v.tensor_copy(AT2[0:KH, u, :], ps[3][0:KH, 0:D]).then_inc(at_ready, 1)
                        wait(v, hq_done, i + 1)
                        wait(v, o_done, 2 * NT + i - 1)
                        v.tensor_copy(hqT[:, u, :], ps[4][:, 0:D]).then_inc(hq_ready, 1)
                        wait(v, hq_ready, 2 * i + 1)
                        v.tensor_tensor(xhT[:, u, :], hqT[:, u, :], xT[:, u, :, :].rearrange("p k n -> p (k n)"),
                                        ALU.mult).then_inc(hq_ready, 1)
                        if not last:
                            norm(i + 2, u, f1 + i + 2).then_inc(xn_ready, 1)
                        wait(v, o_done, 2 * NT + i + 1)
                        then(v.scalar_tensor_tensor(X[:, i, :], ps[7][:, 0:D], tgx, X[:, i, :], ALU.mult, ALU.add))
                        then(v.tensor_tensor(X[:, i, :], X[:, i, :], qvrow, ALU.add))
                        finish(i, x_done)
                        if not last:
                            take(u, f1 + i + 2, [(o_done, 2 * NT + i + 1)])
                    token_tiles(v, stp, body)
                if l == 3:
                    v.wait_ge(xw_in, 16 * 11)
                    for k in range(DK):
                        for b in range(B):
                            stp.mark(v.tensor_reduce(csum[:, k, b:b + 1], ctxT[:, k, b, :], AX.X, ALU.add))
                    v.wait_ge(v_step[3], stp.count)
                    v.engine_nop().then_inc(simset, 1)
                    v.wait_ge(set_pe, 7)
                    for b in range(B):
                        stp.mark(v.scalar_tensor_tensor(rowB[:, b, :], ps[6][:, b * D:(b + 1) * D], 1.0 / S2, b3row,
                                                        ALU.mult, ALU.add))
                    v.wait_ge(v_step[3], stp.count)
                    stp.then(v.tensor_scalar(rowB[:, :, :].rearrange("p b n -> p (b n)"),
                                             rowB[:, :, :].rearrange("p b n -> p (b n)"), tgx, None, ALU.mult))
                    norm(0, 0, f0).then_inc(xn_ready, 1)
                    take(0, f0, ())

                    def body(i, u, q, b, last):
                        if last < 2:
                            norm(i + 1, 1 - u, f0 + i + 1).then_inc(xn_ready, 1)
                            take(1 - u, f0 + i + 1, [(o_done, 3 * NT + i)])
                        wait(v, o_done, 3 * NT + i + 1)
                        then(v.scalar_tensor_tensor(X[:, i, :], ps[1][:, 0:D], tgx, X[:, i, :], ALU.mult, ALU.add))
                        then(v.tensor_tensor(X[:, i, :], X[:, i, :], rowB[:, b, :], ALU.add))
                        finish(i, x_done)
                    token_tiles(v, stp, body)

                gather_statistics(x_done, (l + 1) * NT)

                g0 = FG[l]
                rstd(2 * l + 1)
                if l == 2:
                    then(v.tensor_tensor(VT[:, :], RSTD[:, :], RSTD[:, :], ALU.mult))
                    v.tensor_tensor(VT[:, :], VT[:, :], MV[:, :, 1], ALU.mult).then_inc(rt_v, 1)
                    v.wait_ge(rt_act, 3)
                    then(v.reciprocal(VT[:, :], STD[:, :]))
                    then(v.tensor_tensor(RSTD[:, :], RSTD[:, :], VT[:, :], ALU.mult))
                    v.wait_ge(xw_in, 16 * 9)
                else:
                    v.engine_nop().then_inc(rt_v, 1)
                LG = Rt[:, 136:264]

                def normg(i, u):
                    f = g0 + i
                    m = norm(i, u, f, [(xn_stored[u], 16 * (NTB * l + (i - u) // 2) if type(i) is not int
                                        else 16 * (NTB * l + i // 2))])
                    if l == 2:
                        then(m)
                        m = v.tensor_tensor(xn[:, u, :], xn[:, u, :], nwrow, ALU.mult)
                    m.then_inc(xn_ready, 1)
                normg(0, 0)
                take(0, g0, ())

                def body(i, u, q, b, last):
                    if last < 2:
                        normg(i + 1, 1 - u)
                        take(1 - u, g0 + i + 1, [(lg_done, l * NT + i)])
                    wait(v, lg_done, l * NT + i + 1)
                    m = v.tensor_copy(LG[:, bass.ds(i * E, E)], ps[6][:, 0:E]).then_inc(lg_used, 1)
                token_tiles(v, stp, body)
                v.wait_ge(lg_used, NT * (l + 1))
                sc3 = LG.rearrange("p (i e) -> p i e", e=E)
                SC = LG
                t16 = small[:, 0:16]
                bc = lambda ap: ap.unsqueeze(2).to_broadcast([P, NT, E])
                tmp = Rt[:, 264:392]
                tmp3 = tmp.rearrange("p (i e) -> p i e", e=E)
                if l == 2:
                    v.engine_nop().then_inc(route, 1)
                    v.wait_ge(rt_act, 4)
                    then(v.tensor_copy(LG, Rt[:, 896:1024]))
                if l == 3:
                    then(v.tensor_tensor(sc3, sc3, rb3[:, :].unsqueeze(1).to_broadcast([P, NT, E]), ALU.add))
                    then(v.tensor_reduce(t16, sc3, AX.X, ALU.max))
                    then(v.tensor_tensor(tmp3, sc3, bc(t16), ALU.subtract))
                    v.engine_nop().then_inc(route, 1)
                    v.wait_ge(rt_act, 5)
                    then(v.tensor_reduce(t16, sc3, AX.X, ALU.add))
                    then(v.reciprocal(t16, t16))
                    then(v.tensor_tensor(sc3, sc3, bc(t16), ALU.mult))
                down3 = downb[:, :].unsqueeze(1).to_broadcast([P, NT, E])
                oh = [Rt[:, 392:520].rearrange("p (i e) -> p i e", e=E), Rt[:, 520:648].rearrange("p (i e) -> p i e", e=E)]
                best = [g1, g2]
                for k in range(TOPK):
                    then(v.tensor_reduce(best[k][:, :], sc3, AX.X, ALU.max))
                    then(v.tensor_tensor(tmp3, sc3, bc(best[k][:, :]), ALU.is_equal))
                    then(v.tensor_tensor(tmp3, tmp3, down3, ALU.mult))
                    then(v.tensor_reduce(t16, tmp3, AX.X, ALU.max))
                    then(v.tensor_tensor(oh[k], down3, bc(t16), ALU.is_equal))
                    if k == 0:
                        then(v.scalar_tensor_tensor(sc3, oh[0], -3.0e38, sc3, ALU.mult, ALU.add))
                then(v.memset(Rt[:, NT * E:(NT + 1) * E], 0.0))
                then(v.tensor_tensor(Rt[:, 0:NT * E].rearrange("p (i e) -> p i e", e=E), oh[0], oh[1], ALU.add))
                v.engine_nop().then_inc(rt_v, 1)
                if l < 2:
                    then(v.tensor_tensor(g2[:, :], g2[:, :], g1[:, :], ALU.subtract))
                    v.engine_nop().then_inc(gate_in, 1)
                    v.wait_ge(rt_act, l + 1)
                    then(v.tensor_scalar(t16, g2[:, :], 1.0, None, ALU.add))
                    then(v.reciprocal(g1[:, :], t16))
                    then(v.tensor_tensor(g2[:, :], g2[:, :], g1[:, :], ALU.mult))
                elif l == 2:
                    then(v.tensor_tensor(t16, g1[:, :], g2[:, :], ALU.add))
                    then(v.tensor_scalar(t16, t16, 1e-6, None, ALU.add))
                    then(v.reciprocal(t16, t16))
                    then(v.tensor_tensor(g1[:, :], g1[:, :], t16, ALU.mult))
                    then(v.tensor_tensor(g2[:, :], g2[:, :], t16, ALU.mult))
                v.wait_ge(rt_pe, l + 1)
                then(v.tensor_scalar(cnti[:, :], ps[7][:, NT * E:(NT + 1) * E], float(P - 1), None, ALU.add))
                then(v.tensor_scalar(cnti[:, :], cnti[:, :], 7, None, ALU.logical_shift_right))
                then(v.tensor_copy(cntf[:, 0, :], cnti[:, :]))
                then(v.tensor_tensor_scan(cntf[:, 1, :], ones[:, 0:E], cntf[:, 0, :], 0.0, ALU.mult, ALU.add))
                then(v.tensor_tensor(cntf[:, 2, :], cntf[:, 1, :], cntf[:, 0, :], ALU.subtract))
                then(v.tensor_scalar(cntf[:, 2, :], cntf[:, 2, :], float(P), float(T), ALU.mult, ALU.add))
                then(v.tensor_tensor(tmp3, ps[7][:, 0:NT * E].rearrange("p (i e) -> p i e", e=E),
                                     cntf[:, 2, :].unsqueeze(1).to_broadcast([P, NT, E]), ALU.add))
                for k in range(TOPK):
                    then(v.tensor_tensor(oh[k], oh[k], tmp3, ALU.mult))
                    then(v.tensor_reduce(t16, oh[k], AX.X, ALU.add))
                    then(v.tensor_copy(pos[:, :, k], t16))
                then(v.tensor_tensor(tcmp[:, :, :], cntf[0:1, 1, :].unsqueeze(1).to_broadcast([1, SLOT_TILES, E]),
                                     tidx[:, :, :], ALU.is_le))
                then(v.tensor_reduce(tsum[:, :], tcmp[:, :, :], AX.X, ALU.add))
                then(v.tensor_scalar(etab[:, NT:], tsum[:, :], float(E - 1), None, ALU.min))
                v.engine_nop().then_inc(pos_ready, 2)

                n, e0, nh, up = ETILES[l], EB0[l], HID[l] // P, UP[l]
                if l >= 2:
                    v.wait_ge(b2_in, 32 * (l - 1))

                def take_e(i, u):
                    wait(v, et_done, e0 + i + 1)
                    wait(v, u_done, e0 + i - 1)
                    v.tensor_copy(xT[:, u, :, :].rearrange("p k n -> p (k n)"), ps[5][:, 0:D]).then_inc(exT_ready, 1)

                def hidden(i, u):
                    if l == 1:
                        wait(v, half_ready, i + 1)
                        wait(v, ht_done, e0 + i - 1)
                        v.tensor_tensor(h[:, u, 0:512], h[:, u, 512:1024], ps[1][:, :], ALU.mult)\
                            .then_inc(h_ready, 1)
                    if l >= 2:
                        wait(v, u_done, e0 + i + 1)
                        wait(v, ht_done, e0 + i - 1)
                        for k in range(up // 512):
                            m = v.tensor_copy(h[:, u, k * 512:(k + 1) * 512], ps[k][:, :])
                        m.then_inc(h_ready, 1)
                take_e(0, 0)
                hidden(0, 0)
                take_e(1, 1)

                def body(i, u, q, left):
                    if l < 2:
                        wait(v, ht_done, e0 + i + 1)
                        wait(v, d_done, e0 + i - 1)
                        for k in range(nh // 4):
                            m = v.tensor_copy(hT[:, u, k * 512:(k + 1) * 512], ps[2 + k][:, :])
                        m.then_inc(hT_ready, 1)
                    if left > 0:
                        hidden(i + 1, 1 - u)
                    if l >= 2:
                        e = v.value_load(etab[0:1, bass.ds(i, 1)], min_val=0, max_val=E)
                    wait(v, d_done, e0 + i + 1)
                    if not (type(i) is int and i < 2):
                        wait(v, y_stored[u], 16 * (EP[l][u] + q))
                    elif l:
                        wait(v, y_stored[u], 16 * EP[l][u])
                    if l >= 2:
                        m = v.tensor_tensor(ybuf[:, u, :], ps[4][:, 0:D], b2b[:, bass.ds(e * D, D)], ALU.add)
                    else:
                        m = v.tensor_copy(ybuf[:, u, :], ps[4][:, 0:D])
                    m.then_inc(y_ready, 1)
                    if left > 1:
                        take_e(i + 2, u)
                expert_tiles(v, None, n, body)

                for g in (g1, g2):
                    stp.mark(v.tensor_scalar(g[:, :], g[:, :], tgf, None, ALU.mult))
                v.wait_ge(v_step[l], stp.count)

                def body(i, u, q, b, last):
                    wait(v, y_in[u], 32 * (NTB * l + q + 1))
                    then(v.scalar_tensor_tensor(X[:, i, :], ygat[:, u, 0, :], col(g1, i), X[:, i, :], ALU.mult, ALU.add))
                    then(v.scalar_tensor_tensor(X[:, i, :], ygat[:, u, 1, :], col(g2, i), X[:, i, :], ALU.mult, ALU.add))
                    if SHARED[l]:
                        k = sum(SHARED[:l])
                        wait(v, ysh_in[u], 16 * (NTB * k + q + 1))
                        then(v.scalar_tensor_tensor(X[:, i, :], ygat[:, u, 2, :], tgf, X[:, i, :], ALU.mult, ALU.add))
                    finish(i, c_done)
                token_tiles(v, stp, body)
                if l + 1 < LAYERS:
                    gather_statistics(c_done, (l + 1) * NT)


def kernel(**inputs):
    import numpy as _np
    import concourse.bacc as _bacc
    from concourse import mybir as _mybir
    from concourse.bass_utils import run_bass_kernel_spmd as _run

    x = {k: _np.asarray(v) for k, v in inputs.items()}

    def cols(w):
        return w.reshape(-1, P, w.shape[-1]).transpose(1, 0, 2)

    def flat(*ws):
        return _np.concatenate([cols(w).reshape(P, -1) for w in ws], axis=1)

    def part(v):
        return _np.moveaxis(v.reshape(v.shape[:-1] + (-1, P)), -1, 0)

    c = x["ctx_1024"]
    T_ = _np.transpose
    w0 = [flat(x["L0_ffn_experts_w1"][e].T, x["L0_ffn_experts_w2"][e].T) for e in range(E)]
    w0.append(flat(x["L0_ffn_shared_w1"].T, x["L0_ffn_shared_w2"].T))
    w1 = [flat(_np.concatenate([x["L1_ffn_W1"][e].T, x["L1_ffn_W2"][e].T], axis=1), x["L1_ffn_W3"][e].T)
          for e in range(E)]
    w2 = [flat(x["L2_ffn_ew1"][e], x["L2_ffn_ew2"][e]) for e in range(E)] + [flat(x["L2_ffn_sw1"], x["L2_ffn_sw2"])]
    w3 = [flat(x["L3_ffn_rw1"][e], x["L3_ffn_rw2"][e]) for e in range(E)] + [flat(x["L3_ffn_sw1"], x["L3_ffn_sw2"])]
    W3 = x["L3_xattn_W"]
    arrays = {
        "x": x["x"].reshape(T, D),
        "ctxT": T_(c.reshape(B, S2, DK, P), (3, 2, 0, 1)),
        "ctxr": T_(c.reshape(B, 2, KH, D), (2, 1, 0, 3)),
        "projT": cols(x["L0_xattn_projection"].T),
        "gateT": _np.stack([cols(x["L0_ffn_gate_w"].T), cols(x["L1_ffn_Wg"].T), cols(x["L2_ffn_router_w"].T),
                            cols(x["L3_ffn_router_w"])], axis=1),
        "gates": _np.concatenate([x["g_xattn"], x["g_ffn"]]),
        "bqk": part(_np.stack([x["L1_xattn_wq_b"], x["L1_xattn_wk_b"]])),
        "simw": part(x["L2_xattn_w_sim"].reshape(3, D)),
        "bsim": x["L2_xattn_b_sim"].reshape(1, 1),
        "rb3": x["L3_ffn_router_b"],
        "w0": _np.stack(w0), "w1": _np.stack(w1), "w2": _np.stack(w2), "w3": _np.stack(w3),
        "qkvo": _np.stack([cols(x[f"L1_xattn_w{n}_k"]) for n in "qkvo"]),
        "bv": x["L1_xattn_wv_b"], "bo": x["L1_xattn_wo_b"],
        "mask": x["mask_BxSxS2_ik1"].reshape(T, S2), "side": x["fside_BxSxS2_0"].reshape(T, S2),
        "Wqv": cols(x["L2_xattn_W_qv"]), "bqv": x["L2_xattn_b_qv"],
        "nw": x["L2_ffn_norm_weight"],
        "b2_2": _np.concatenate([x["L2_ffn_eb2"].reshape(-1), x["L2_ffn_sb2"]]),
        "b1_2": part(_np.concatenate([x["L2_ffn_eb1"], x["L2_ffn_sb1"][None]])).reshape(P, -1),
        "W3x": _np.stack([cols(W3[:, :D].T), cols(W3[:, D:].T)], axis=1),
        "b3": x["L3_xattn_b"],
        "b2_3": _np.concatenate([x["L3_ffn_rb2"].reshape(-1), x["L3_ffn_sb2"]]),
        "b1_3": part(_np.concatenate([x["L3_ffn_rb1"], x["L3_ffn_sb1"][None]])).reshape(P, -1),
    }
    nc = _bacc.Bacc("TRN2", target_bir_lowering=False, num_devices=1)
    maps, aps = {}, {}
    for name, v in arrays.items():
        v = _np.ascontiguousarray(v)
        maps[f"in_{name}"] = v
        aps[name] = nc.dram_tensor(f"in_{name}", v.shape, _mybir.dt.from_np(v.dtype), kind="ExternalInput").ap()
    out = nc.dram_tensor("out_x", (T, D), _mybir.dt.float32, kind="ExternalOutput").ap()
    xn_rows = nc.dram_tensor("xn_rows", (ROWS, D), _mybir.dt.float32).ap()
    y_rows = nc.dram_tensor("y_rows", (ROWS, D), _mybir.dt.float32).ap()
    bass_flamingo_moe_kernel(nc, aps, out, xn_rows, y_rows)
    r = _run(nc, [maps], core_ids=[0])
    return r.results[0]["out_x"].reshape(B, S, D)
```

```python
from contextlib import ExitStack

import numpy as np
import concourse.bass as bass
from concourse import mybir
from concourse.alu_op_type import AluOpType as ALU

F32 = mybir.dt.float32
I32 = mybir.dt.int32
U32 = mybir.dt.uint32
ACT = mybir.ActivationFunctionType
AX = mybir.AxisListType

P = 128
D = 256
DK = D // P
B = 2
S = 1024
T = B * S
NT = T // P
NTB = NT // B
S2 = 154
KH = S2 // 2
KR = S2 - P
E = 8
TOPK = 2
SLOT_TILES = T * TOPK // P + E - 1
ROWS = SLOT_TILES * P
HEADS = 16
DH = D // HEADS
HC = HEADS // DK
M = 64
NEG = 1.0e9
LAYERS = 4

UP = [1024, 1024, 1024, 512]
HID = [1024, 512, 1024, 512]
SHARED = [True, False, True, True]
WSLOTS = [E + SHARED[l] for l in range(LAYERS)]
WSIZE = [DK * UP[l] + HID[l] // P * D for l in range(LAYERS)]
ETILES = [SLOT_TILES + NT * SHARED[l] for l in range(LAYERS)]


def bass_flamingo_moe_kernel(nc, a, out, xn_tokens, xn_rows, y_rows):
    with ExitStack() as ctx:
        def sb(name, shape, dt=F32):
            return ctx.enter_context(nc.sbuf_tensor(name, shape, dt))

        def sem(name):
            return ctx.enter_context(nc.semaphore(name))

        def sems(name, n=2):
            return [sem(f"{name}{k}") for k in range(n)]

        X = sb("X", [P, NT, D])
        W = sb("W", [P, max(WSLOTS[l] * WSIZE[l] for l in range(LAYERS))])
        arena = sb("arena", [P, 4 * 1024])
        misc = sb("misc", [P, 2560])
        xn = sb("xn", [P, 2, D])
        xT = sb("xT", [P, 2, DK, P])
        tiles = sb("tiles", [P, 4 * D])
        ident = sb("ident", [P, P])
        ones = sb("ones", [P, P])
        upper = sb("upper", [P, P])
        ctxT = sb("ctxT", [P, DK, B, S2])
        ctxr = sb("ctxr", [KH, 2, B, D + 1])
        gateT = sb("gateT", [P, LAYERS, DK, E])
        tg = sb("tg", [P, 2 * LAYERS])
        junk = sb("junk", [1, 3])
        eps = sb("eps", [P, 2])
        MV = sb("MV", [P, NT, 2])
        STD = sb("STD", [P, NT])
        RSTD = sb("RSTD", [P, NT])
        VT = sb("VT", [P, NT])
        st6 = sb("st6", [P, NT, 6])
        g1 = sb("g1", [P, NT])
        g2 = sb("g2", [P, NT])
        pos = sb("pos", [P, NT, 2], I32)
        etab = sb("etab", [1, NT + SLOT_TILES], I32)
        idx = sb("idx", [P, 4, 2, 1], U32)
        b1T = sb("b1T", [P, (E + 1) * 8])
        bqk = sb("bqk", [P, 2, DK])
        headm = sb("headm", [P, HC])
        remm = sb("remm", [P, 4])
        zb = sb("zb", [P, 2 * P], mybir.dt.bfloat16)
        simw = sb("simw", [P, 3, DK])
        bsim = sb("bsim", [1, 1])
        rb3 = sb("rb3", [P, E])
        small = sb("small", [P, 24])
        rs = sb("rs", [P, 2, HEADS])
        rr = sb("rr", [P, 2, HEADS])
        MX = sb("MX", [P, NT])
        EB = sb("EB", [P, NT])
        simrow = sb("simrow", [1, B, S2])
        downb = sb("downb", [P, E])
        tidx = sb("tidx", [1, SLOT_TILES, E])
        cnti = sb("cnti", [P, E], I32)
        cntf = sb("cntf", [P, 3, E])
        negm = sb("negm", [P, 2, HC * 2])

        xs = tiles[:, 0:2 * D].rearrange("p (u n) -> p u n", u=2)
        ybuf = tiles[:, 2 * D:4 * D].rearrange("p (u n) -> p u n", u=2)
        KVZ = arena[0:M, 0:B * (D + 1)].rearrange("p (b n) -> p b n", b=B)
        rfk = arena[0:KH, 1024:1280].rearrange("p (s b m) -> p s b m", s=2, b=B)
        rf = arena[0:M, 2048:2304].rearrange("p (u n) -> p u n", u=2)
        tcmp = arena[0:1, 3072 + 392:3072 + 704].rearrange("p (i e) -> p i e", e=E)
        tsum = arena[0:1, 3072 + 704:3072 + 704 + SLOT_TILES]
        projT = arena[:, 2560:2560 + DK * M].rearrange("p (k n) -> p k n", k=DK)
        h = arena[:, 0:2048].rearrange("p (u n) -> p u n", u=2)
        hT = arena[:, 2048:4096].rearrange("p (u n) -> p u n", u=2)
        ygat = arena[:, 0:2048].rearrange("p (u r n) -> p u r n", u=4, r=TOPK)
        qkvo = arena[:, 2048:4096].rearrange("p (w k n) -> p w k n", w=4, k=DK)
        XN = arena[:, :].rearrange("p (i n) -> p i n", i=NT)
        qT = arena[:, 0:512].rearrange("p (u c n) -> p u c n", u=2, c=DK)
        hcW = arena[:, 0:1024].rearrange("p (b k n) -> p b k n", b=B, k=DK)
        AT2 = arena[:, 1024:1536].rearrange("p (u n) -> p u n", u=2)
        A2 = arena[:, 1536:1536 + 2 * S2].rearrange("p (u n) -> p u n", u=2)
        hqT = arena[:, 2048:2560].rearrange("p (u n) -> p u n", u=2)
        xhT = arena[:, 2560:3072].rearrange("p (u n) -> p u n", u=2)
        Rt = arena[:, 3072:4096]
        w_end = WSLOTS[1] * WSIZE[1]
        KBD = W[:, w_end:w_end + 4928].rearrange("p (c b h s) -> p c b h s", c=DK, b=B, h=HC)
        PR = W[:, w_end + 4928:w_end + 9856].rearrange("p (u h s) -> p u h s", u=2, h=HEADS)
        PT = W[:, w_end + 9856:w_end + 11904].rearrange("p (g n) -> p g n", g=4)
        PL = arena[:, 512:512 + 2 * HEADS * KR].rearrange("p (u h s) -> p u h s", u=2, h=HEADS)
        ctxR = PT[:, 0:1, 0:DK * B * 4 * KR].rearrange("p o (k b n) -> p (o k) b n", k=DK, b=B)
        XNs = W[:, w_end:w_end + NT * D].rearrange("p (i n) -> p i n", i=NT)
        kT = PR[:, 0, 0:4, :].rearrange("p h s -> p (h s)").rearrange("p (c n) -> p c n", c=DK)
        Vh = tiles[:, :].rearrange("p (b s n) -> p b s n", b=B, s=2)
        msk = misc[:, 0:2 * S2].bitcast(I32).rearrange("p (u s) -> p u s", u=2)
        side = misc[:, 2 * S2:4 * S2].rearrange("p (u s) -> p u s", u=2)
        neg = misc[:, 4 * S2:6 * S2].rearrange("p (u s) -> p u s", u=2)
        bvr = misc[:, 1024:1280]
        orow = misc[:, 1280:1536]
        obuf = misc[:, 1536:2048].rearrange("p (u n) -> p u n", u=2)
        oT = misc[:, 2048:2560].rearrange("p (u n) -> p u n", u=2)
        Wqv = misc[:, 0:2048].rearrange("p (k n) -> p k n", k=4 * DK)
        qvrow = misc[:, 2048:2304]
        W3x = misc[:, 0:1024].rearrange("p (w k n) -> p w k n", w=2, k=DK)
        rowB = misc[:, 1024:1536].rearrange("p (b n) -> p b n", b=B)
        b3row = misc[:, 1536:1792]
        csum = small[:, 0:4].rearrange("p (k b) -> p k b", k=DK)
        b2b = misc[:, 0:(E + 1) * D]
        nwrow = misc[:, 2304:2560]
        CW = tiles[:, 0:DK * B * S2].rearrange("p (k b s) -> p k b s", k=DK, b=B)

        ps = [ctx.enter_context(nc.psum_tensor(f"ps{k}", [P, 512], F32)) for k in range(8)]

        x_in, ctx_in, w_shared, w_in = sem("x_in"), sem("ctx_in"), sem("w_shared"), sem("w_in")
        xw_in, b2_in, pad_in, padz = sem("xw_in"), sem("b2_in"), sem("pad_in"), sem("padz")
        consts, consts_v, tg_ready = sem("consts"), sem("consts_v"), sem("tg_ready")
        stats, std_ready = sem("stats"), sem("std_ready")
        xn_ready, t_done, xT_ready = sem("xn_ready"), sem("t_done"), sem("xT_ready")
        xn_copied = sem("xn_copied")
        x_done = sem("x_done")
        set_pe, set_act, set_v, set_pool = sem("set_pe"), sem("set_act"), sem("set_v"), sem("set_pool")
        r_done, rf_ready, o_done = sem("r_done"), sem("rf_ready"), sem("o_done")
        q_done, q_ready = sem("q_done"), sem("q_ready")
        s_done, l_ready, e_ready, p_ready = sem("s_done"), sem("l_ready"), sem("e_ready"), sem("p_ready")
        pt_done, pt_v, pt_a, pv_done = sem("pt_done"), sem("pt_v"), sem("pt_a"), sem("pv_done")
        pvh = sem("pvh")
        on_ready, ot_done, ot_ready = sem("on_ready"), sem("ot_done"), sem("ot_ready")
        side_in, neg_ready = sems("side_in"), sem("neg_ready")
        mx_ready, a_ready, an_ready, at_done, at_ready = (sem("mx_ready"), sem("a_ready"), sem("an_ready"),
                                                          sem("at_done"), sem("at_ready"))
        hq_done, hq_ready = sem("hq_done"), sem("hq_ready")
        xn_stored, lg_done, lg_used = sems("xn_stored"), sem("lg_done"), sem("lg_used")
        rt_act, rt_v, rt_pe = sem("rt_act"), sem("rt_v"), sem("rt_pe")
        pos_ready, pool_step = sem("pos_ready"), sem("pool_step")
        sc_in, sc_out = sems("sc_in"), sems("sc_out")
        xs_in, et_done, exT_ready = sems("xs_in"), sem("et_done"), sem("exT_ready")
        u_done, half_ready, h_ready, ht_done, hT_ready = (sem("u_done"), sem("half_ready"), sem("h_ready"),
                                                          sem("ht_done"), sem("hT_ready"))
        d_done, y_ready, y_stored = sem("d_done"), sem("y_ready"), sems("y_stored")
        y_in, c_done = sems("y_in", 4), sem("c_done")
        y_sum, sc_all = sem("y_sum"), sem("sc_all")
        out_stored, x0_stats = sem("out_stored"), sem("x0_stats")
        v_step = [sem(f"v_step{l}") for l in range(LAYERS)]
        mx1, route, simset, gate_in, vready = sem("mx1"), sem("route"), sem("simset"), sem("gate_in"), sem("vready")
        last_keys = sem("last_keys")

        def wait(eng, s, value):
            if type(value) is int and value <= 0:
                return
            eng.wait_ge(s, value)

        def alone(eng):
            eng.wait_ge(consts, 12)

        def alone_pool(u):
            return nc.gpsimd.tensor_tensor(junk[:, u:u + 1], ones[0:1, 0:1], ones[0:1, 0:1], ALU.mult)

        class Steps:
            def __init__(self, eng, s, count=0):
                self.eng, self.s, self.count = eng, s, count

            def then(self, ins):
                self.mark(ins)
                self.eng.wait_ge(self.s, self.count)

            def mark(self, ins):
                self.count = self.count + 1
                ins.then_inc(self.s, 1)

        def loop(eng, steps, first, last, body):
            before = steps.count if steps else 0
            n0 = probe[0] if steps else 0
            with eng.Fori(first, last) as q:
                if steps and n0:
                    steps.count = before + (q - first) * n0
                body(q)
            if steps:
                steps.count = before + (last - first) * n0

        probe = [0]

        def token_tiles(eng, steps, body):
            def pair(q, b, end=False):
                for u in range(2):
                    body(2 * q + u, u, q, b, 0 if not end else (1 if u == 0 else 2))
            before = steps.count if steps else 0
            pair(0, 0)
            probe[0] = steps.count - before if steps else 0
            loop(eng, steps, 1, NTB // 2, lambda q: pair(q, 0))
            loop(eng, steps, NTB // 2, NT // 2 - 1, lambda q: pair(q, 1))
            pair(NT // 2 - 1, 1, True)

        def token_quads(eng, steps, body):
            def quad(q):
                for u in range(4):
                    body(4 * q + u, u, q)
            before = steps.count
            quad(0)
            probe[0] = steps.count - before
            loop(eng, steps, 1, NT // 4 - 1, quad)
            quad(NT // 4 - 1)

        def expert_tiles(eng, steps, n, body, at=None, between=None):
            q1 = (n - 3) // 2
            def pair(q):
                for u in range(2):
                    body(2 * q + u, u, q, 3)
            before = steps.count if steps else 0
            pair(0)
            probe[0] = steps.count - before if steps else 0
            if at:
                loop(eng, steps, 1, at, pair)
                if between:
                    between()
                pair(at)
                loop(eng, steps, at + 1, q1, pair)
            else:
                loop(eng, steps, 1, q1, pair)
            for k in range(3):
                i = 2 * q1 + k
                body(i, i % 2, i // 2, 2 - k)

        FX = [0, 32, 64, 112]
        FX2 = 80
        FG = [16, 48, 96, 128]
        EB0 = [sum(ETILES[:l]) for l in range(LAYERS)]
        EP = [[sum((ETILES[k] + 1 - u) // 2 for k in range(l)) for u in range(2)] for l in range(LAYERS + 1)]

        STORES = [(SLOT_TILES + 1 - u) // 2 for u in range(2)]

        block = ctx.enter_context(nc.Block())

        @block.sync
        def _(sp):
            sp.dma_start(X[:, :, :], a["x"].rearrange("(i p) d -> p i d", p=P)).then_inc(x_in, 16)
            first = [(ctxT[:, :, :, :], a["ctxT"]), (ctxr[:, :, :, 0:D], a["ctxr"]), (projT[:, :, :], a["projT"]),
                     (gateT[:, :, :, :], a["gateT"]), (small[:, 16:24], a["gates"].partition_broadcast(P)),
                     (bqk[:, :, :], a["bqk"]), (simw[:, :, :], a["simw"]), (bsim[:, :], a["bsim"]),
                     (rb3[:, :], a["rb3"].partition_broadcast(P))]
            for dst, src in first:
                sp.dma_start(dst, src).then_inc(ctx_in, 16)

            def weights(l):
                for k, e in enumerate(reversed(range(WSLOTS[l]))):
                    shared = SHARED[l] and e == E
                    if l:
                        sp.wait_ge(c_done, l * NT)
                        wait(sp, x_done, l * NT + k)
                    sp.dma_start(W[:, e * WSIZE[l]:(e + 1) * WSIZE[l]],
                                 a[f"w{l}"][e]).then_inc(w_shared if shared else w_in, 16)
            weights(0)

            for l in range(LAYERS):
                def store_xn(i, u, q, b, last):
                    wait(sp, xn_ready, FG[l] + i + 1)
                    sp.dma_start(xn_tokens[bass.ds(i * P, P), :], xn[:, u, :]).then_inc(xn_stored[u], 16)
                if l == 2:
                    sp.wait_ge(x_done, (l + 1) * NT)
                    sp.dma_start(nwrow, a["nw"].partition_broadcast(P)).then_inc(xw_in, 16)
                if l >= 2:
                    sp.wait_ge(x_done, (l + 1) * NT)
                    sp.dma_start(b2b, a[f"b2_{l}"].partition_broadcast(P)).then_inc(b2_in, 16)
                    sp.dma_start(b1T[:, 0:(E + 1) * HID[l] // P], a[f"b1_{l}"]).then_inc(b2_in, 16)
                if SHARED[l]:
                    token_tiles(sp, None, store_xn)
                    for u in range(2):
                        sp.wait_ge(xn_stored[u], 16 * NTB * sum(SHARED[:l + 1]))

                n, first = ETILES[l], NT if SHARED[l] else 0

                def sorted_rows_ready():
                    if l % 2:
                        sp.wait_ge(sc_all, 16 * TOPK * NT * (l // 2 + 1))
                    else:
                        for u in range(2):
                            sp.wait_ge(sc_out[u], 32 * NTB * (l // 2 + 1))
                    sp.wait_ge(w_in, 16 * E * (l + 1))

                def rows(i, u, q, left):
                    wait(sp, et_done, EB0[l] + i - 1 if not (type(i) is int and i < 2) else EB0[l])
                    src = xn_rows[bass.ds((i - first) * P, P), :] if listed[0] else xn_tokens[bass.ds(i * P, P), :]
                    sp.dma_start(xs[:, u, :], src).then_inc(xs_in[u], 16)
                    if (i >= first + 2) if type(i) is int else listed[0]:
                        store(i - 2, u)

                def store(i, u):
                    wait(sp, y_ready, EB0[l] + i + 1)
                    sp.dma_start(y_rows[bass.ds((i - first) * P, P), :], ybuf[:, u, :]).then_inc(y_stored[u], 16)

                def begin_list():
                    sorted_rows_ready()
                    listed[0] = True
                listed = [not SHARED[l]]
                if SHARED[l]:
                    expert_tiles(sp, None, n, rows, NT // 2, begin_list)
                else:
                    begin_list()
                    expert_tiles(sp, None, n, rows)
                store(n - 2, (n - 2) % 2)
                store(n - 1, (n - 1) % 2)
                if l + 1 < LAYERS:
                    sp.wait_ge(d_done, EB0[l] + n)
                    if l == 0:
                        for w in range(4):
                            sp.dma_start(qkvo[:, w, :, :], a["qkvo"][w]).then_inc(xw_in, 16)
                        sp.dma_start(bvr, a["bv"].partition_broadcast(P)).then_inc(xw_in, 16)
                        sp.dma_start(orow, a["bo"].partition_broadcast(P)).then_inc(xw_in, 16)
                    if l == 1:
                        sp.dma_start(Wqv, a["Wqv"]).then_inc(xw_in, 16)
                        sp.dma_start(qvrow, a["bqv"].partition_broadcast(P)).then_inc(xw_in, 16)
                    if l == 2:
                        sp.dma_start(W3x, a["W3x"]).then_inc(xw_in, 16)
                        sp.dma_start(b3row, a["b3"].partition_broadcast(P)).then_inc(xw_in, 16)
                    weights(l + 1)
            sp.wait_ge(c_done, LAYERS * NT)
            sp.dma_start(out.rearrange("(i p) d -> p i d", p=P), X[:, :, :]).then_inc(out_stored, 16)
            sp.wait_ge(out_stored, 16)

        @block.gpsimd
        def _(pool):
            st = Steps(pool, pool_step)
            st.mark(pool.memset(ident[:, :], 0.0))
            st.mark(pool.memset(upper[:, :], 0.0))
            st.mark(pool.memset(headm[:, :], 1.0))
            st.mark(pool.memset(remm[:, :], 1.0))
            st.then(pool.memset(misc[:, :], 0.0))
            for i in range(8):
                k0, k1 = SLOT_TILES * i // 8, SLOT_TILES * (i + 1) // 8
                pool.dma_start(xn_rows[k0 * P:k1 * P, :].rearrange("(p r) d -> p (r d)", p=P),
                               misc[:, 0:(k1 - k0) * D]).then_inc(pad_in, 16)
            pool.memset(ones[:, :], 1.0).then_inc(consts, 1)
            pool.memset(ctxr[:, :, :, D:D + 1], 1.0).then_inc(consts, 1)
            pool.memset(eps[:, 0:1], 1e-5).then_inc(consts, 1)
            pool.memset(eps[:, 1:2], 1e-8).then_inc(consts, 1)
            pool.affine_select(out=ident[:, :], in_=ident[:, :], compare_op=ALU.not_equal, fill=1.0, base=0,
                               pattern=[[-1, P]], channel_multiplier=1).then_inc(consts, 1)
            pool.affine_select(out=upper[:, :], in_=upper[:, :], compare_op=ALU.is_ge, fill=1.0, base=0,
                               pattern=[[-1, P]], channel_multiplier=1).then_inc(consts, 1)
            st.then(pool.affine_select(out=headm[:, :], in_=headm[:, :], compare_op=ALU.is_ge, fill=0.0, base=0,
                                       pattern=[[-DH, HC]], channel_multiplier=1))
            pool.affine_select(out=headm[:, :], in_=headm[:, :], compare_op=ALU.is_ge, fill=0.0, base=DH - 1,
                               pattern=[[DH, HC]], channel_multiplier=-1).then_inc(consts, 1)
            st.then(pool.affine_select(out=remm[:, :], in_=remm[:, :], compare_op=ALU.is_ge, fill=0.0, base=0,
                                       pattern=[[-KR, 4]], channel_multiplier=1))
            pool.affine_select(out=remm[:, :], in_=remm[:, :], compare_op=ALU.is_ge, fill=0.0, base=KR - 1,
                               pattern=[[KR, 4]], channel_multiplier=-1).then_inc(consts, 1)
            pool.memset(zb[:, :], 0.0).then_inc(consts, 1)
            pool.iota(downb[:, :], pattern=[[-1, E]], base=E, channel_multiplier=0,
                      allow_small_or_imprecise_dtypes=True).then_inc(consts, 1)
            pool.iota(tidx[:, :, :], pattern=[[1, SLOT_TILES], [0, E]], base=0, channel_multiplier=0,
                      allow_small_or_imprecise_dtypes=True).then_inc(consts, 1)
            pool.iota(etab[:, 0:NT], pattern=[[0, NT]], base=E, channel_multiplier=0).then_inc(consts, 1)

            for l in range(LAYERS):
                if l == 1:
                    def load(i, u, q):
                        wait(pool, p_ready, 2 * (i - 1))
                        wait(pool, neg_ready, i - 1)
                        pool.dma_start(msk[:, u, :], a["mask"][bass.ds(i * P, P), :]).then_inc(side_in[u], 16)
                        pool.dma_start(side[:, u, :], a["side"][bass.ds(i * P, P), :]).then_inc(side_in[u], 16)

                    def mask(i, u, q):
                        wait(pool, side_in[u], 32 * (q + 1))
                        wait(pool, l_ready, 6 * (i - 1))
                        alone_pool(u)
                        pool.tensor_scalar(neg[:, u, :], msk[:, u, :], 1.0, NEG, ALU.subtract,
                                           ALU.mult).then_inc(neg_ready, 1)

                    def weigh(i, u, q, chunks=range(DK)):
                        for c in chunks:
                            wait(pool, e_ready, 2 * i + c + 1)
                            for dst, k0, k1 in ((PR[:, u, c * HC:(c + 1) * HC, 0:P], 0, P),
                                                (PL[:, u, c * HC:(c + 1) * HC, :], P, S2)):
                                m = pool.tensor_tensor(dst, PR[:, u, c * HC:(c + 1) * HC, k0:k1],
                                                       side[:, u, k0:k1].unsqueeze(1).to_broadcast([P, HC, k1 - k0]),
                                                       ALU.mult)
                            m.then_inc(p_ready, 1)
                    pool.wait_ge(d_done, EB0[1])
                    load(0, 0, 0)
                    load(1, 1, 0)
                    mask(0, 0, 0)
                    weigh(0, 0, 0)
                    mask(1, 1, 0)

                    def body(i, u, q, b, last):
                        if not last:
                            load(i + 2, u, q + 1)
                        if last < 2:
                            weigh(i + 1, 1 - u, q + u, [0])
                        if not last:
                            mask(i + 2, u, q + 1)
                        if last < 2:
                            weigh(i + 1, 1 - u, q + u, [1])
                    token_tiles(pool, None, body)
                if l == 2:
                    pool.wait_ge(set_v, 6)
                    pool.partition_all_reduce(small[:, 6:8], small[:, 4:6], P,
                                              bass.bass_isa.ReduceOp.max).then_inc(set_pool, 1)

                pool.wait_ge(pos_ready, 2 * l + 1)
                if l == 0:
                    pool.wait_ge(pad_in, 16 * 8)

                def places(i, u):
                    st.mark(pool.tensor_copy(idx[:, u, 0, :], pos[:, i, 0:1].bitcast(U32)))
                    st.then(pool.tensor_copy(idx[:, u, 1, :], pos[:, i, 1:2].bitcast(U32)))

                def scatter(i, u, q, b, last):
                    k = l // 2
                    wait(pool, sc_out[u], 32 * (NTB * k + q))
                    pool.dma_start(xn[:, u, :], xn_tokens[bass.ds(i * P, P), :]).then_inc(sc_in[u], 16)
                    places(i, u)
                    wait(pool, sc_in[u], 16 * (NTB * k + q + 1))
                    st.mark(alone_pool(2))
                    for k in range(TOPK):
                        pool.indirect_dma_start(xn_rows[:, :], bass.IndirectOffsetOnAxis(ap=idx[:, u, k, :], axis=0),
                                                xn[:, u, :], None).then_inc(sc_out[u], 16)
                if l % 2 == 0:
                    for u in range(2):
                        pool.wait_ge(xn_stored[u], 16 * NTB * sum(SHARED[:l + 1]))
                    token_tiles(pool, st, scatter)
                else:
                    pool.wait_ge(xn_copied, (l + 1) // 2 * NT + (NT if l == 3 else 0))
                    for i in range(NT):
                        for k in range(TOPK):
                            pool.indirect_dma_start(xn_rows[:, :],
                                                    bass.IndirectOffsetOnAxis(ap=pos[:, i, k:k + 1].bitcast(U32), axis=0),
                                                    XNs[:, i, :], None).then_inc(sc_all, 16)

                if l % 2:
                    pool.wait_ge(sc_all, 16 * TOPK * NT * (l // 2 + 1))
                else:
                    for u in range(2):
                        pool.wait_ge(sc_out[u], 32 * NTB * (l // 2 + 1))
                for u in range(2):
                    pool.wait_ge(y_stored[u], 16 * STORES[u] * (l + 1))

                def gather(i, u, q):
                    wait(pool, y_in[u], 32 * (NT // 4 * l + q))
                    wait(pool, c_done, l * NT + i - 3 if not (type(i) is int and i < 4) else 0)
                    places(i, u)
                    st.mark(alone_pool(2))
                    for k in range(TOPK):
                        pool.indirect_dma_start(ygat[:, u, k, :], None, y_rows[:, :],
                                                bass.IndirectOffsetOnAxis(ap=idx[:, u, k, :], axis=0)).then_inc(y_in[u], 16)
                token_quads(pool, st, gather)

        @block.tensor
        def _(pe):
            def transpose_x(f, u):
                wait(pe, xn_ready, f + 1)
                wait(pe, xT_ready, f)
                for k in range(DK):
                    m = pe.transpose(ps[5][:, k * P:(k + 1) * P], xn[:, u, k * P:(k + 1) * P], ident[:, :])
                m.then_inc(t_done, 1)

            pe.wait_ge(consts, 12)
            pe.wait_ge(ctx_in, 16 * 9)
            for l in range(LAYERS):
                f0 = FX[l]
                if l == 0:
                    for b in range(B):
                        for s in range(2):
                            for k in range(DK):
                                m = pe.matmul(ps[0][0:KH, (2 * b + s) * M:(2 * b + s + 1) * M],
                                              ctxT[:, k, b, s * KH:(s + 1) * KH], projT[:, k, :],
                                              start=(k == 0), stop=(k == DK - 1))
                    m.then_inc(set_pe, 1)
                    pe.wait_ge(set_act, 1)
                    for b in range(B):
                        for s in range(2):
                            m = pe.matmul(ps[1 + b][0:M, 0:D + 1], rfk[:, s, b, :], ctxr[:, s, b, :],
                                          start=(s == 0), stop=(s == 1))
                    m.then_inc(set_pe, 1)
                    pe.wait_ge(set_v, 1)

                    def features(i, u):
                        wait(pe, xT_ready, f0 + i + 1)
                        wait(pe, rf_ready, i)
                        for k in range(DK):
                            m = pe.matmul(ps[0][0:M, 0:P], projT[:, k, :], xT[:, u, k, :],
                                          start=(k == 0), stop=(k == DK - 1))
                        m.then_inc(r_done, 1)
                    transpose_x(f0, 0)
                    features(0, 0)

                    def body(i, u, q, b, last):
                        if last < 2:
                            transpose_x(f0 + i + 1, 1 - u)
                        wait(pe, rf_ready, i + 1)
                        wait(pe, x_done, i)
                        pe.matmul(ps[1][:, 0:D + 1], rf[:, u, :], KVZ[:, b, :], start=True, stop=True).then_inc(o_done, 1)
                        if last < 2:
                            features(i + 1, 1 - u)
                    token_tiles(pe, None, body)
                if l == 1:
                    pe.wait_ge(xw_in, 16 * 6)
                    for c in range(DK):
                        for k in range(DK):
                            m = pe.matmul(ps[c][:, 0:B * S2], qkvo[:, 1, k, c * P:(c + 1) * P],
                                          ctxT[:, k, :, :].rearrange("p b s -> p (b s)"),
                                          start=(k == 0), stop=(k == DK - 1))
                    m.then_inc(set_pe, 1)
                    for b in range(B):
                        for k in range(DK):
                            pe.matmul(ps[2 + b][:, 0:D], ctxT[:, k, b, 0:P], qkvo[:, 2, k, :],
                                      start=(k == 0), stop=(k == DK - 1))
                        wait(pe, last_keys, DK * B)
                        for k in range(DK):
                            m = pe.matmul(ps[2 + b][0:4 * KR, D:2 * D], ctxR[:, k, b, :], qkvo[:, 2, k, :], start=(k == 0), stop=(k == DK - 1))
                    m.then_inc(set_pe, 1)
                    pe.wait_ge(set_v, 5)
                    pe.wait_ge(vready, B)

                    def queries(i, u):
                        wait(pe, xT_ready, f0 + i + 1)
                        wait(pe, q_ready, i)
                        for c in range(DK):
                            for k in range(DK):
                                m = pe.matmul(ps[1][:, c * P:(c + 1) * P], qkvo[:, 0, k, c * P:(c + 1) * P],
                                              xT[:, u, k, :], start=(k == 0), stop=(k == DK - 1))
                        m.then_inc(q_done, 1)

                    def scores(i, u, b, c):
                        if c == 0:
                            wait(pe, q_ready, i + 1)
                        for g in range(3):
                            n = min(3, HC - 3 * g)
                            wait(pe, l_ready, 6 * i + 3 * c + g - 2)
                            pe.matmul(ps[2 + g][:, 0:n * S2], qT[:, u, c, :],
                                      KBD[:, c, b, 3 * g:3 * g + n, :].rearrange("p h s -> p (h s)"),
                                      start=True, stop=True).then_inc(s_done, 1)

                    def copied(i, g):
                        return (pt_a, 2 * i + g // 2) if g % 2 else (pt_v, 3 * i + g // 2)

                    def turn(i, u, g):
                        if g in (0, 2, 4):
                            wait(pe, p_ready, 2 * i + (g // 2 + 1 if g < 4 else 2))
                        s_, n = copied(i, g)
                        wait(pe, s_, n)
                        for j in range(4):
                            src = PR[:, u, 4 * g + j, 0:P] if g < 4 else PL[:, u, 4 * j:4 * j + 4, :].rearrange("p h s -> p (h s)")
                            m = pe.transpose(ps[0 if g % 2 else 6][0:P if g < 4 else 4 * KR, j * P:(j + 1) * P],
                                             src, ident[:, :])
                        m.then_inc(pt_done, 1)

                    def product(i, b, g):
                        if g == 0:
                            wait(pe, on_ready, i)
                            pe.matmul(ps[7][:, 0:D], zb[:, 0:P], zb[:, :], start=True, stop=False)
                        s_, n = copied(i, g)
                        wait(pe, s_, n + 1)
                        for j in range(4):
                            if g < 4:
                                at, w = (4 * g + j) * DH, DH
                                m = pe.matmul(ps[7][:, at:at + w], PT[:, g, j * P:(j + 1) * P], Vh[:, b, 0, at:at + w],
                                              start=False, stop=False)
                            else:
                                at, w = 4 * j * DH, 4 * DH
                                m = pe.matmul(ps[7][:, at:at + w], PT[0:4 * KR, 0, j * P:(j + 1) * P],
                                              Vh[0:4 * KR, b, 1, at:at + w], start=False, stop=(j == 3))
                        m.then_inc(pv_done, 1)

                    def turn_out(i, u):
                        wait(pe, on_ready, i + 1)
                        for k in range(DK):
                            m = pe.transpose(ps[5][:, k * P:(k + 1) * P], obuf[:, u, k * P:(k + 1) * P], ident[:, :])
                        m.then_inc(ot_done, 1)

                    def project(i, u):
                        wait(pe, ot_ready, i + 1)
                        for k in range(DK):
                            m = pe.matmul(ps[1][:, 0:256], oT[:, u, k * P:(k + 1) * P], qkvo[:, 3, k, :],
                                          start=(k == 0), stop=(k == DK - 1))
                        m.then_inc(o_done, 1)
                    transpose_x(f0, 0)
                    queries(0, 0)
                    transpose_x(f0 + 1, 1)
                    scores(0, 0, 0, 0)
                    scores(0, 0, 0, 1)
                    queries(1, 1)

                    def body(i, u, q, b, last, f0=f0):
                        first = type(i) is int and i == 0
                        if last < 2:
                            scores(i + 1, 1 - u, (i + 1) // NTB, 0)
                        if not last:
                            wait(pe, ot_ready, i - 1)
                            transpose_x(f0 + i + 2, u)
                        turn(i, u, 0)
                        turn(i, u, 1)
                        if not last:
                            wait(pe, x_done, NT + i - 1)
                            queries(i + 2, u)
                        product(i, b, 0)
                        product(i, b, 1)
                        if last < 2:
                            scores(i + 1, 1 - u, (i + 1) // NTB, 1)
                        if not first:
                            wait(pe, xT_ready, f0 + i + 3 if not last else f0 + NT)
                            turn_out(i - 1, 1 - u)
                        turn(i, u, 2)
                        turn(i, u, 3)
                        product(i, b, 2)
                        if not first:
                            wait(pe, q_ready, i + 3 if not last else NT)
                            project(i - 1, 1 - u)
                        turn(i, u, 4)
                        product(i, b, 3)
                        product(i, b, 4)
                    token_tiles(pe, None, body)
                    turn_out(NT - 1, 1)
                    wait(pe, x_done, 2 * NT - 1)
                    project(NT - 1, 1)
                if l == 2:
                    pe.wait_ge(simset, 1)
                    for b in range(B):
                        for k in range(DK):
                            m = pe.matmul(ps[6][0:1, b * S2:(b + 1) * S2], simw[:, 1, k:k + 1], ctxT[:, k, b, :],
                                          start=(k == 0), stop=(k == DK - 1))
                    m.then_inc(set_pe, 1)
                    pe.wait_ge(simset, 2)

                    def similarity(i, u, b, n, used):
                        wait(pe, xT_ready, n + 1)
                        wait(pe, *used)
                        for k in range(DK):
                            pe.matmul(ps[2][:, 0:S2], xT[:, u, k, :], CW[:, k, b, :], start=(k == 0), stop=False)
                        pe.matmul(ps[2][:, 0:S2], ones[0:1, :], simrow[0:1, b, :], start=False, stop=True).then_inc(s_done, 1)
                    transpose_x(f0, 0)

                    def body(i, u, q, b, last, f0=f0):
                        if last < 2:
                            transpose_x(f0 + i + 1, 1 - u)
                        similarity(i, u, b, f0 + i, (mx_ready, i))
                    token_tiles(pe, None, body)
                    pe.wait_ge(set_act, 4)
                    pe.wait_ge(xn_copied, 2 * NT)
                    for b in range(B):
                        for k in range(DK):
                            for j in range(NTB):
                                i = b * NTB + j
                                m = pe.matmul(ps[6][:, 2 * b + k:2 * b + k + 1], XN[:, i, k * P:(k + 1) * P],
                                              EB[:, i:i + 1], start=(j == 0), stop=(j == NTB - 1))
                    m = pe.matmul(ps[6][:, 4:6], ones[:, :], small[:, 8:10], start=True, stop=True)
                    m.then_inc(set_pe, 1)
                    pe.wait_ge(simset, 3)
                    f1 = FX2

                    def mix(i, u, b):
                        wait(pe, an_ready, i + 1)
                        wait(pe, at_ready, i)
                        for s in range(2):
                            m = pe.transpose(ps[3][0:KH, s * P:(s + 1) * P], A2[:, u, s * KH:(s + 1) * KH], ident[:, :])
                        m.then_inc(at_done, 1)
                        wait(pe, at_ready, i + 1)
                        wait(pe, hq_ready, 2 * i)
                        for k in range(DK):
                            for s in range(2):
                                m = pe.matmul(ps[4][:, k * P:(k + 1) * P], ctxr[:, s, b, k * P:(k + 1) * P],
                                              AT2[0:KH, u, s * P:(s + 1) * P], start=(s == 0), stop=(s == 1))
                        m.then_inc(hq_done, 1)

                    def project(i, u, b):
                        wait(pe, x_done, 2 * NT + i)
                        for k in range(DK):
                            pe.matmul(ps[7][:, 0:D], xT[:, u, k, :], hcW[:, b, k, :], start=(k == 0), stop=False)
                        wait(pe, hq_ready, 2 * (i + 1))
                        for k in range(DK):
                            pe.matmul(ps[7][:, 0:D], hqT[:, u, k * P:(k + 1) * P], Wqv[:, DK + k, :], start=False, stop=False)
                        for k in range(DK):
                            m = pe.matmul(ps[7][:, 0:D], xhT[:, u, k * P:(k + 1) * P], Wqv[:, 2 * DK + k, :],
                                          start=False, stop=(k == DK - 1))
                        m.then_inc(o_done, 1)
                    transpose_x(f1, 0)
                    similarity(0, 0, 0, f1, (mx_ready, NT))
                    transpose_x(f1 + 1, 1)

                    def body(i, u, q, b, last, f1=f1):
                        if last < 2:
                            similarity(i + 1, 1 - u, (i + 1) // NTB, f1 + i + 1, (a_ready, i + 1))
                        mix(i, u, b)
                        project(i, u, b)
                        if not last:
                            transpose_x(f1 + i + 2, u)
                    token_tiles(pe, None, body)
                if l == 3:
                    pe.wait_ge(simset, 4)
                    for b in range(B):
                        for k in range(DK):
                            m = pe.matmul(ps[6][:, b * D:(b + 1) * D], csum[:, k, b:b + 1].to_broadcast([P, P]),
                                          W3x[:, 1, k, :], start=(k == 0), stop=(k == DK - 1))
                    m.then_inc(set_pe, 1)
                    transpose_x(f0, 0)

                    def body(i, u, q, b, last, f0=f0):
                        if last < 2:
                            transpose_x(f0 + i + 1, 1 - u)
                        wait(pe, xT_ready, f0 + i + 1)
                        wait(pe, x_done, 3 * NT + i)
                        for k in range(DK):
                            m = pe.matmul(ps[1][:, 0:D], xT[:, u, k, :], W3x[:, 0, k, :], start=(k == 0), stop=(k == DK - 1))
                        m.then_inc(o_done, 1)
                    token_tiles(pe, None, body)

                g0 = FG[l]
                transpose_x(g0, 0)

                def body(i, u, q, b, last, g0=g0, l=l):
                    if last < 2:
                        transpose_x(g0 + i + 1, 1 - u)
                    wait(pe, xT_ready, g0 + i + 1)
                    wait(pe, lg_used, l * NT + i)
                    for k in range(DK):
                        m = pe.matmul(ps[6][:, 0:E], xT[:, u, k, :], gateT[:, l, k, :], start=(k == 0), stop=(k == DK - 1))
                    m.then_inc(lg_done, 1)
                token_tiles(pe, None, body)
                pe.wait_ge(rt_v, 2 * l + 2)
                cnt = Rt[:, 0:(NT + 1) * E]
                pe.matmul(ps[7][:, 0:(NT + 1) * E], ones[:, :],
                          cnt[:, NT * E:].unsqueeze(1).to_broadcast([P, NT + 1, E]), start=True, stop=False)
                for i in range(NT):
                    pe.matmul(ps[7][:, (i + 1) * E:(NT + 1) * E], ones[:, :],
                              cnt[:, i * E:(i + 1) * E].unsqueeze(1).to_broadcast([P, NT - i, E]),
                              start=False, stop=False)
                pe.matmul(ps[7][:, 0:(NT + 1) * E], upper[:, :], cnt, start=False, stop=True).then_inc(rt_pe, 1)

                n, e0, up, hid = ETILES[l], EB0[l], UP[l], HID[l]
                nb, nh = up // 512, hid // P
                if SHARED[l]:
                    pe.wait_ge(w_shared, 16 * sum(SHARED[:l + 1]))

                def take(i, u, q):
                    wait(pe, xs_in[u], 16 * (EP[l][u] + q + 1))
                    wait(pe, exT_ready, e0 + i)
                    for k in range(DK):
                        m = pe.transpose(ps[5][:, k * P:(k + 1) * P], xs[:, u, k * P:(k + 1) * P], ident[:, :])
                    m.then_inc(et_done, 1)

                def expert(i):
                    at = i if SHARED[l] else i + NT
                    e = pe.value_load(etab[0:1, bass.ds(at, 1)], min_val=0, max_val=WSLOTS[l] - 1)
                    return e

                def upward(i, u):
                    e = expert(i)
                    wait(pe, exT_ready, e0 + i + 1)
                    wait(pe, h_ready, e0 + i)
                    for n_ in range(nb):
                        for k in range(DK):
                            m = pe.matmul(ps[n_][:, 0:512], xT[:, u, k, :],
                                          W[:, bass.ds(e * WSIZE[l] + (k * up + n_ * 512), 512)],
                                          start=(k == 0), stop=(k == DK - 1))
                    m.then_inc(u_done, 1)
                    return e

                def turn(i, u):
                    wait(pe, h_ready, e0 + i + 1)
                    wait(pe, hT_ready, e0 + i)
                    for c in range(nh):
                        m = pe.transpose(ps[2 + c // 4][:, c % 4 * P:(c % 4 + 1) * P], h[:, u, c * P:(c + 1) * P], ident[:, :])
                    m.then_inc(ht_done, 1)

                def downward(i, u):
                    e = expert(i)
                    wait(pe, hT_ready, e0 + i + 1)
                    wait(pe, y_ready, e0 + i)
                    for c in range(nh):
                        m = pe.matmul(ps[4][:, 0:D], hT[:, u, c * P:(c + 1) * P],
                                      W[:, bass.ds(e * WSIZE[l] + (DK * up + c * D), D)],
                                      start=(c == 0), stop=(c == nh - 1))
                    m.then_inc(d_done, 1)

                take(0, 0, 0)
                upward(0, 0)
                take(1, 1, 0)

                def body(i, u, q, left):
                    turn(i, u)
                    if left > 0:
                        upward(i + 1, 1 - u)
                    downward(i, u)
                    if left > 1:
                        take(i + 2, u, q + 1)
                expert_tiles(pe, None, n, body)

        @block.scalar
        def _(act):
            act.wait_ge(ctx_in, 16 * 9)
            act.activation(tg[:, :], small[:, 16:24], ACT.Tanh).then_inc(tg_ready, 1)
            act.wait_ge(consts, 12)

            def std(n):
                wait(act, stats, NT * (n + 1))
                act.activation(STD[:, :], MV[:, :, 1], ACT.Sqrt, bias=eps[:, 0:1]).then_inc(std_ready, 1)

            nstd = 0
            for l in range(LAYERS):
                std(2 * l)
                if l == 0:
                    act.wait_ge(set_pe, 1)
                    act.activation(rfk[:, :, :, :].rearrange("p s b m -> p b s m"),
                                   ps[0][0:KH, 0:4 * M].rearrange("p (b s m) -> p b s m", b=B, s=2),
                                   ACT.Exp, scale=1.0 / 16.0).then_inc(set_act, 1)

                    def expo(i, u):
                        wait(act, r_done, i + 1)
                        wait(act, o_done, i - 1)
                        act.activation(rf[:, u, :], ps[0][0:M, 0:P], ACT.Exp, scale=1.0 / 16.0).then_inc(rf_ready, 1)
                    expo(0, 0)

                    def body(i, u, q, b, last):
                        if last < 2:
                            expo(i + 1, 1 - u)
                    token_tiles(act, None, body)
                if l == 1:
                    act.wait_ge(set_pe, 3)
                    for c in range(DK):
                        m = act.activation(kT[:, c, :], ps[c][:, 0:B * S2], ACT.Identity, bias=bqk[:, 1, c:c + 1])
                    m.then_inc(set_act, 1)

                    def queries(i, u):
                        wait(act, q_done, i + 1)
                        wait(act, s_done, 6 * (i - 1))
                        for c in range(DK):
                            m = act.activation(qT[:, u, c, :], ps[1][:, c * P:(c + 1) * P], ACT.Identity,
                                               bias=bqk[:, 0, c:c + 1])
                        m.then_inc(q_ready, 1)

                    def expo(i, u, c):
                        wait(act, mx1, 2 * i + c + 1)
                        for j in range(HC):
                            hh = c * HC + j
                            m = act.activation(PR[:, u, hh, :], PR[:, u, hh, :], ACT.Exp, bias=negm[:, u, hh:hh + 1],
                                               accum_out=rs[:, u, hh:hh + 1])
                        m.then_inc(e_ready, 1)

                    def copy(i, g):
                        wait(act, pt_done, 5 * i + g + 1)
                        wait(act, pv_done, 5 * i)
                        act.activation(PT[:, g, :], ps[0][:, :], ACT.Copy).then_inc(pt_a, 1)
                    queries(0, 0)
                    expo(0, 0, 0)
                    expo(0, 0, 1)
                    queries(1, 1)

                    def body(i, u, q, b, last):
                        copy(i, 1)
                        if not last:
                            queries(i + 2, u)
                        if last < 2:
                            expo(i + 1, 1 - u, 0)
                        copy(i, 3)
                        if last < 2:
                            expo(i + 1, 1 - u, 1)
                    token_tiles(act, None, body)
                if l == 2:
                    def keep(i, u):
                        wait(act, xn_ready, FX[2] + i + 1)
                        act.activation(XN[:, i, :], xn[:, u, :], ACT.Copy).then_inc(xn_copied, 1)
                    keep(0, 0)

                    def body(i, u, q, b, last):
                        if last < 2:
                            keep(i + 1, 1 - u)
                    token_tiles(act, None, body)
                    act.wait_ge(set_v, 7)
                    for b in range(B):
                        m = act.activation(EB[:, b * NTB:(b + 1) * NTB], MX[:, b * NTB:(b + 1) * NTB], ACT.Exp,
                                           bias=small[:, 10 + b:11 + b], scale=-1.0, accum_out=small[:, 8 + b:9 + b])
                        m.then_inc(set_act, 1)

                    def expo(i, u):
                        wait(act, s_done, 6 * NT + NT + i + 1)
                        wait(act, at_done, i - 1)
                        wait(act, simset, 3)
                        act.activation(A2[:, u, :], ps[2][:, 0:S2], ACT.Exp, bias=MX[:, i:i + 1] if type(i) is int
                                       else MX[:, bass.ds(i, 1)], accum_out=rs[:, u, 0:1]).then_inc(a_ready, 1)
                    expo(0, 0)

                    def body(i, u, q, b, last):
                        if last < 2:
                            expo(i + 1, 1 - u)
                    token_tiles(act, None, body)
                std(2 * l + 1)
                if l % 2:
                    def body(i, u, q, b, last):
                        wait(act, xn_ready, FG[l] + i + 1)
                        act.activation(XNs[:, i, :], xn[:, u, :], ACT.Copy).then_inc(xn_copied, 1)
                    token_tiles(act, None, body)
                if l == 2:
                    act.wait_ge(rt_v, 2 * l + 1)
                    act.activation(STD[:, :], VT[:, :], ACT.Sqrt, bias=eps[:, 1:2]).then_inc(rt_act, 1)
                    act.wait_ge(route, 1)
                    act.activation(Rt[:, 896:1024], Rt[:, 136:264], ACT.Sigmoid).then_inc(rt_act, 1)
                elif l == 3:
                    act.wait_ge(route, 2)
                    act.activation(Rt[:, 136:264], Rt[:, 264:392], ACT.Exp).then_inc(rt_act, 1)
                else:
                    act.wait_ge(gate_in, l + 1)
                    act.activation(g2[:, :], g2[:, :], ACT.Exp).then_inc(rt_act, 1)
                n, e0, nh = ETILES[l], EB0[l], HID[l] // P

                def body(i, u, q, left):
                    if l == 0:
                        wait(act, u_done, e0 + i + 1)
                        wait(act, ht_done, e0 + i - 1)
                        for k in range(2):
                            m = act.activation(h[:, u, k * 512:(k + 1) * 512], ps[k][:, :], ACT.Silu)
                        m.then_inc(h_ready, 1)
                    elif l == 1:
                        wait(act, u_done, e0 + i + 1)
                        wait(act, h_ready, e0 + i - 1)
                        act.activation(h[:, u, 512:1024], ps[0][:, :], ACT.Silu).then_inc(half_ready, 1)
                    else:
                        at = i
                        e = act.value_load(etab[0:1, bass.ds(at, 1)], min_val=0, max_val=E)
                        wait(act, ht_done, e0 + i + 1)
                        wait(act, d_done, e0 + i - 1)
                        for c in range(nh):
                            m = act.activation(hT[:, u, c * P:(c + 1) * P], ps[2 + c // 4][:, c % 4 * P:(c % 4 + 1) * P],
                                               ACT.Relu if l == 2 else ACT.Gelu,
                                               bias=b1T[:, bass.ds(e * nh + c, 1)])
                        m.then_inc(hT_ready, 1)
                if l >= 2:
                    act.wait_ge(b2_in, 32 * (l - 1))
                expert_tiles(act, None, n, body)

        @block.vector
        def _(v):
            st = [Steps(v, v_step[0])]

            def then(ins):
                st[0].then(ins)

            def col(t, i):
                return t[:, bass.ds(i, 1)]

            def rstd(n):
                v.wait_ge(std_ready, n + 1)
                then(v.reciprocal(RSTD[:, :], STD[:, :]))

            def norm(i, u, f, extra=()):
                wait(v, t_done, f - 1)
                for s, k in extra:
                    wait(v, s, k)
                return v.tensor_scalar(xn[:, u, :], X[:, i, :], MV[:, i, 0:1], col(RSTD, i), ALU.subtract, ALU.mult)

            def take(u, f, used):
                wait(v, t_done, f + 1)
                for s, k in used:
                    wait(v, s, k)
                v.tensor_copy(xT[:, u, :, :].rearrange("p k n -> p (k n)"), ps[5][:, 0:D]).then_inc(xT_ready, 1)

            def finish(i, s):
                alone(v)
                v.bn_stats(st6[:, i, :], X[:, i, :]).then_inc(s, 1)

            def gather_statistics(s, count):
                v.wait_ge(s, count)
                for i in range(NT):
                    v.bn_aggr(MV[:, i, :], st6[:, i, :]).then_inc(stats, 1)

            v.wait_ge(x_in, 16)
            for i in range(NT):
                v.bn_stats(st6[:, i, :], X[:, i, :]).then_inc(x0_stats, 1)
            gather_statistics(x0_stats, NT)
            v.wait_ge(consts, 12)
            v.wait_ge(ctx_in, 16 * 9)
            v.wait_ge(tg_ready, 1)

            for l in range(LAYERS):
                if l:
                    st[0] = Steps(v, v_step[l])
                f0, tgx, tgf = FX[l], tg[:, l:l + 1], tg[:, LAYERS + l:LAYERS + l + 1]
                stp = st[0]
                rstd(2 * l)
                if l == 0:
                    norm(0, 0, f0).then_inc(xn_ready, 1)
                    v.wait_ge(set_pe, 2)
                    v.tensor_copy(KVZ[:, 0, :], ps[1][0:M, 0:D + 1])
                    v.tensor_copy(KVZ[:, 1, :], ps[2][0:M, 0:D + 1]).then_inc(set_v, 1)
                    take(0, f0, ())

                    def body(i, u, q, b, last):
                        if last < 2:
                            norm(i + 1, 1 - u, f0 + i + 1).then_inc(xn_ready, 1)
                            take(1 - u, f0 + i + 1, [(r_done, i)])
                        v.wait_ge(o_done, i + 1)
                        then(v.tensor_scalar(small[:, 12 + u:13 + u], ps[1][:, D:D + 1], 8e-6, None, ALU.add))
                        then(v.reciprocal(small[:, 14 + u:15 + u], small[:, 12 + u:13 + u]))
                        then(v.tensor_tensor(small[:, 12 + u:13 + u], small[:, 14 + u:15 + u], tgx, ALU.mult))
                        st[0].then(v.scalar_tensor_tensor(X[:, i, :], ps[1][:, 0:D], small[:, 12 + u:13 + u], X[:, i, :],
                                                          ALU.mult, ALU.add))
                        finish(i, x_done)
                    token_tiles(v, stp, body)
                if l == 1:
                    for k in range(DK):
                        for b in range(B):
                            v.tensor_copy(ctxR[:, k, b, :].rearrange("p (j s) -> p j s", j=4),
                                          ctxT[:, k, b, P:S2].unsqueeze(1).to_broadcast([P, 4, KR])).then_inc(last_keys, 1)
                    v.wait_ge(set_act, 2)
                    for c in range(DK):
                        for b in range(B):
                            m = v.tensor_tensor(KBD[:, c, b, :, :],
                                                kT[:, c, b * S2:(b + 1) * S2].unsqueeze(1).to_broadcast([P, HC, S2]),
                                                headm[:, :].unsqueeze(2).to_broadcast([P, HC, S2]), ALU.mult)
                            m.then_inc(set_v, 1)
                    v.wait_ge(set_pe, 4)
                    for b in range(B):
                        v.tensor_tensor(Vh[:, b, 0, :], ps[2 + b][:, 0:D], bvr, ALU.add)
                        then(v.tensor_tensor(Vh[0:4 * KR, b, 1, :], ps[2 + b][0:4 * KR, D:2 * D], bvr[0:4 * KR, :], ALU.add))
                        vr = Vh[0:4 * KR, b, 1, :].rearrange("p (j h d) -> p j h d", j=4, h=4)
                        v.tensor_tensor(vr, vr, remm[0:4 * KR, :].unsqueeze(1).unsqueeze(3).to_broadcast([4 * KR, 4, 4, DH]),
                                        ALU.mult).then_inc(vready, 1)
                    then(v.tensor_scalar(orow, orow, tgx, None, ALU.mult))

                    def logits(i, u, c):
                        if c == 0:
                            wait(v, neg_ready, i + 1)
                            wait(v, pt_done, 5 * (i - 1))
                        for g in range(3):
                            n = min(3, HC - 3 * g)
                            wait(v, s_done, 6 * i + 3 * c + g + 1)
                            v.scalar_tensor_tensor(
                                PR[:, u, c * HC + 3 * g:c * HC + 3 * g + n, :],
                                ps[2 + g][:, 0:n * S2].rearrange("p (h s) -> p h s", h=n), 0.25,
                                neg[:, u, :].unsqueeze(1).to_broadcast([P, n, S2]), ALU.mult, ALU.add).then_inc(l_ready, 1)

                    def maxima(i, u, c):
                        wait(v, l_ready, 6 * i + 3 * c + 3)
                        v.tensor_reduce(negm[:, u, c * HC:(c + 1) * HC], PR[:, u, c * HC:(c + 1) * HC, :], AX.X,
                                        ALU.max, negate=True).then_inc(mx1, 1)

                    def copy(i, g):
                        n = P if g < 4 else 4 * KR
                        wait(v, pt_done, 5 * i + g + 1)
                        wait(v, pv_done, 5 * i + (1 if g == 4 else 0))
                        v.tensor_copy(PT[0:n, g % 4, :], ps[6][0:n, :]).then_inc(pt_v, 1)

                    def final(i):
                        wait(v, o_done, NT + i + 1)
                        then(v.scalar_tensor_tensor(X[:, i, :], ps[1][:, 0:256], tgx, X[:, i, :], ALU.mult, ALU.add))
                        then(v.tensor_tensor(X[:, i, :], X[:, i, :], orow, ALU.add))
                        finish(i, x_done)

                    def turned(i, u):
                        wait(v, ot_done, i + 1)
                        wait(v, o_done, NT + i - 1)
                        v.tensor_copy(oT[:, u, :], ps[5][:, 0:D]).then_inc(ot_ready, 1)
                    norm(0, 0, f0).then_inc(xn_ready, 1)
                    take(0, f0, ())
                    norm(1, 1, f0 + 1).then_inc(xn_ready, 1)
                    take(1, f0 + 1, ())
                    for c in range(DK):
                        logits(0, 0, c)
                        maxima(0, 0, c)

                    def body(i, u, q, b, last):
                        first = type(i) is int and i == 0
                        if not last:
                            norm(i + 2, u, f0 + i + 2).then_inc(xn_ready, 1)
                        if last < 2:
                            logits(i + 1, 1 - u, 0)
                        copy(i, 0)
                        if not last:
                            take(u, f0 + i + 2, [(q_done, i + 1)])
                        if last < 2:
                            maxima(i + 1, 1 - u, 0)
                            logits(i + 1, 1 - u, 1)
                        if not first:
                            turned(i - 1, 1 - u)
                        copy(i, 2)
                        if last < 2:
                            maxima(i + 1, 1 - u, 1)
                        copy(i, 4)
                        if not first:
                            final(i - 1)
                        else:
                            for _ in range(2):
                                stp.mark(v.engine_nop())
                        wait(v, e_ready, 2 * (i + 1))
                        then(v.reciprocal(rr[:, u, :], rs[:, u, :]))
                        wait(v, pv_done, 5 * (i + 1))
                        v.tensor_tensor(obuf[:, u, :].rearrange("p (h d) -> p h d", h=HEADS),
                                        ps[7][:, 0:D].rearrange("p (h d) -> p h d", h=HEADS),
                                        rr[:, u, :].unsqueeze(2).to_broadcast([P, HEADS, DH]), ALU.mult).then_inc(on_ready, 1)
                    token_tiles(v, stp, body)
                    turned(NT - 1, 1)
                    final(NT - 1)
                if l == 2:
                    for k in range(DK):
                        m = v.tensor_scalar(CW[:, k, :, :].rearrange("p b s -> p (b s)"),
                                            ctxT[:, k, :, :].rearrange("p b s -> p (b s)"),
                                            simw[:, 2, k:k + 1], simw[:, 0, k:k + 1], ALU.mult, ALU.add)
                    m.then_inc(simset, 1)
                    v.wait_ge(set_pe, 5)
                    v.tensor_scalar(simrow[:, :, :].rearrange("p b s -> p (b s)"), ps[6][0:1, 0:B * S2], bsim[0:1, 0:1],
                                    None, ALU.add).then_inc(simset, 1)
                    norm(0, 0, f0).then_inc(xn_ready, 1)
                    take(0, f0, ())

                    def body(i, u, q, b, last):
                        if last < 2:
                            norm(i + 1, 1 - u, f0 + i + 1, [(xn_copied, NT + i)]).then_inc(xn_ready, 1)
                            take(1 - u, f0 + i + 1, [(s_done, 6 * NT + i)])
                        wait(v, s_done, 6 * NT + i + 1)
                        v.tensor_reduce(col(MX, i), ps[2][:, 0:S2], AX.X, ALU.max, negate=True).then_inc(mx_ready, 1)
                    token_tiles(v, stp, body)
                    v.wait_ge(mx_ready, NT)
                    for b in range(B):
                        m = v.tensor_reduce(small[:, 4 + b:5 + b], MX[:, b * NTB:(b + 1) * NTB], AX.X, ALU.min, negate=True)
                        stp.mark(m)
                    v.wait_ge(v_step[2], stp.count)
                    v.engine_nop().then_inc(set_v, 1)
                    v.wait_ge(set_pool, 1)
                    v.tensor_scalar(small[:, 10:12], small[:, 6:8], -1.0, None, ALU.mult).then_inc(set_v, 1)
                    v.wait_ge(set_pe, 6)
                    v.wait_ge(xw_in, 16 * 8)
                    then(v.reciprocal(small[:, 12:14], ps[6][:, 4:6]))
                    for b in range(B):
                        stp.mark(v.tensor_scalar(csum[:, b, :], ps[6][:, 2 * b:2 * b + 2], small[:, 12 + b:13 + b], None, ALU.mult))
                    v.wait_ge(v_step[2], stp.count)
                    for b in range(B):
                        for k in range(DK):
                            m = v.scalar_tensor_tensor(hcW[:, b, k, :], Wqv[:, 3 * DK + k, :], csum[:, b, k:k + 1],
                                                       Wqv[:, k, :], ALU.mult, ALU.add)
                    stp.mark(m)
                    stp.then(v.tensor_scalar(qvrow, qvrow, tgx, None, ALU.mult))
                    v.engine_nop().then_inc(simset, 1)
                    f1 = FX2

                    def soften(i, u):
                        wait(v, a_ready, i + 1)
                        then(v.reciprocal(rr[:, u, 0:1], rs[:, u, 0:1]))
                        v.tensor_scalar(A2[:, u, :], A2[:, u, :], rr[:, u, 0:1], None, ALU.mult).then_inc(an_ready, 1)
                    norm(0, 0, f1).then_inc(xn_ready, 1)
                    take(0, f1, ())
                    norm(1, 1, f1 + 1).then_inc(xn_ready, 1)
                    take(1, f1 + 1, ())
                    soften(0, 0)

                    def body(i, u, q, b, last):
                        if last < 2:
                            soften(i + 1, 1 - u)
                        wait(v, at_done, i + 1)
                        wait(v, hq_done, i - 1)
                        v.tensor_copy(AT2[0:KH, u, :], ps[3][0:KH, 0:D]).then_inc(at_ready, 1)
                        wait(v, hq_done, i + 1)
                        wait(v, o_done, 2 * NT + i - 1)
                        v.tensor_copy(hqT[:, u, :], ps[4][:, 0:D]).then_inc(hq_ready, 1)
                        wait(v, hq_ready, 2 * i + 1)
                        v.tensor_tensor(xhT[:, u, :], hqT[:, u, :], xT[:, u, :, :].rearrange("p k n -> p (k n)"),
                                        ALU.mult).then_inc(hq_ready, 1)
                        if not last:
                            norm(i + 2, u, f1 + i + 2).then_inc(xn_ready, 1)
                        wait(v, o_done, 2 * NT + i + 1)
                        then(v.scalar_tensor_tensor(X[:, i, :], ps[7][:, 0:D], tgx, X[:, i, :], ALU.mult, ALU.add))
                        then(v.tensor_tensor(X[:, i, :], X[:, i, :], qvrow, ALU.add))
                        finish(i, x_done)
                        if not last:
                            take(u, f1 + i + 2, [(o_done, 2 * NT + i + 1)])
                    token_tiles(v, stp, body)
                if l == 3:
                    v.wait_ge(xw_in, 16 * 11)
                    for k in range(DK):
                        for b in range(B):
                            stp.mark(v.tensor_reduce(csum[:, k, b:b + 1], ctxT[:, k, b, :], AX.X, ALU.add))
                    v.wait_ge(v_step[3], stp.count)
                    v.engine_nop().then_inc(simset, 1)
                    v.wait_ge(set_pe, 7)
                    for b in range(B):
                        stp.mark(v.scalar_tensor_tensor(rowB[:, b, :], ps[6][:, b * D:(b + 1) * D], 1.0 / S2, b3row,
                                                        ALU.mult, ALU.add))
                    v.wait_ge(v_step[3], stp.count)
                    stp.then(v.tensor_scalar(rowB[:, :, :].rearrange("p b n -> p (b n)"),
                                             rowB[:, :, :].rearrange("p b n -> p (b n)"), tgx, None, ALU.mult))
                    norm(0, 0, f0).then_inc(xn_ready, 1)
                    take(0, f0, ())

                    def body(i, u, q, b, last):
                        if last < 2:
                            norm(i + 1, 1 - u, f0 + i + 1).then_inc(xn_ready, 1)
                            take(1 - u, f0 + i + 1, [(o_done, 3 * NT + i)])
                        wait(v, o_done, 3 * NT + i + 1)
                        then(v.scalar_tensor_tensor(X[:, i, :], ps[1][:, 0:D], tgx, X[:, i, :], ALU.mult, ALU.add))
                        then(v.tensor_tensor(X[:, i, :], X[:, i, :], rowB[:, b, :], ALU.add))
                        finish(i, x_done)
                    token_tiles(v, stp, body)

                gather_statistics(x_done, (l + 1) * NT)

                g0 = FG[l]
                rstd(2 * l + 1)
                if l == 2:
                    then(v.tensor_tensor(VT[:, :], RSTD[:, :], RSTD[:, :], ALU.mult))
                    v.tensor_tensor(VT[:, :], VT[:, :], MV[:, :, 1], ALU.mult).then_inc(rt_v, 1)
                    v.wait_ge(rt_act, 3)
                    then(v.reciprocal(VT[:, :], STD[:, :]))
                    then(v.tensor_tensor(RSTD[:, :], RSTD[:, :], VT[:, :], ALU.mult))
                    v.wait_ge(xw_in, 16 * 9)
                else:
                    v.engine_nop().then_inc(rt_v, 1)
                LG = Rt[:, 136:264]

                def normg(i, u):
                    f = g0 + i
                    used = []
                    if SHARED[l]:
                        used.append((xn_stored[u], 16 * (NTB * sum(SHARED[:l]) + (i - u) // 2)))
                    if l % 2:
                        used.append((xn_copied, (l - 1) * NT + i - 1))
                    m = norm(i, u, f, used)
                    if l == 2:
                        then(m)
                        m = v.tensor_tensor(xn[:, u, :], xn[:, u, :], nwrow, ALU.mult)
                    m.then_inc(xn_ready, 1)
                normg(0, 0)
                take(0, g0, ())

                def body(i, u, q, b, last):
                    if last < 2:
                        normg(i + 1, 1 - u)
                        take(1 - u, g0 + i + 1, [(lg_done, l * NT + i)])
                    wait(v, lg_done, l * NT + i + 1)
                    m = v.tensor_copy(LG[:, bass.ds(i * E, E)], ps[6][:, 0:E]).then_inc(lg_used, 1)
                token_tiles(v, stp, body)
                v.wait_ge(lg_used, NT * (l + 1))
                sc3 = LG.rearrange("p (i e) -> p i e", e=E)
                SC = LG
                t16 = small[:, 0:16]
                bc = lambda ap: ap.unsqueeze(2).to_broadcast([P, NT, E])
                tmp = Rt[:, 264:392]
                tmp3 = tmp.rearrange("p (i e) -> p i e", e=E)
                if l == 2:
                    v.engine_nop().then_inc(route, 1)
                    v.wait_ge(rt_act, 4)
                    then(v.tensor_copy(LG, Rt[:, 896:1024]))
                if l == 3:
                    then(v.tensor_tensor(sc3, sc3, rb3[:, :].unsqueeze(1).to_broadcast([P, NT, E]), ALU.add))
                    then(v.tensor_reduce(t16, sc3, AX.X, ALU.max))
                    then(v.tensor_tensor(tmp3, sc3, bc(t16), ALU.subtract))
                    v.engine_nop().then_inc(route, 1)
                    v.wait_ge(rt_act, 5)
                    then(v.tensor_reduce(t16, sc3, AX.X, ALU.add))
                    then(v.reciprocal(t16, t16))
                    then(v.tensor_tensor(sc3, sc3, bc(t16), ALU.mult))
                down3 = downb[:, :].unsqueeze(1).to_broadcast([P, NT, E])
                oh = [Rt[:, 392:520].rearrange("p (i e) -> p i e", e=E), Rt[:, 520:648].rearrange("p (i e) -> p i e", e=E)]
                best = [g1, g2]
                for k in range(TOPK):
                    then(v.tensor_reduce(best[k][:, :], sc3, AX.X, ALU.max))
                    then(v.tensor_tensor(tmp3, sc3, bc(best[k][:, :]), ALU.is_equal))
                    then(v.tensor_tensor(tmp3, tmp3, down3, ALU.mult))
                    then(v.tensor_reduce(t16, tmp3, AX.X, ALU.max))
                    then(v.tensor_tensor(oh[k], down3, bc(t16), ALU.is_equal))
                    if k == 0:
                        then(v.scalar_tensor_tensor(sc3, oh[0], -3.0e38, sc3, ALU.mult, ALU.add))
                then(v.memset(Rt[:, NT * E:(NT + 1) * E], 0.0))
                then(v.tensor_tensor(Rt[:, 0:NT * E].rearrange("p (i e) -> p i e", e=E), oh[0], oh[1], ALU.add))
                v.engine_nop().then_inc(rt_v, 1)
                if l < 2:
                    then(v.tensor_tensor(g2[:, :], g2[:, :], g1[:, :], ALU.subtract))
                    v.engine_nop().then_inc(gate_in, 1)
                    v.wait_ge(rt_act, l + 1)
                    then(v.tensor_scalar(t16, g2[:, :], 1.0, None, ALU.add))
                    then(v.reciprocal(g1[:, :], t16))
                    then(v.tensor_tensor(g2[:, :], g2[:, :], g1[:, :], ALU.mult))
                elif l == 2:
                    then(v.tensor_tensor(t16, g1[:, :], g2[:, :], ALU.add))
                    then(v.tensor_scalar(t16, t16, 1e-6, None, ALU.add))
                    then(v.reciprocal(t16, t16))
                    then(v.tensor_tensor(g1[:, :], g1[:, :], t16, ALU.mult))
                    then(v.tensor_tensor(g2[:, :], g2[:, :], t16, ALU.mult))
                v.wait_ge(rt_pe, l + 1)
                then(v.tensor_scalar(cnti[:, :], ps[7][:, NT * E:(NT + 1) * E], float(P - 1), None, ALU.add))
                then(v.tensor_scalar(cnti[:, :], cnti[:, :], 7, None, ALU.logical_shift_right))
                then(v.tensor_copy(cntf[:, 0, :], cnti[:, :]))
                then(v.tensor_tensor_scan(cntf[:, 1, :], ones[:, 0:E], cntf[:, 0, :], 0.0, ALU.mult, ALU.add))
                then(v.tensor_tensor(cntf[:, 2, :], cntf[:, 1, :], cntf[:, 0, :], ALU.subtract))
                then(v.tensor_scalar(cntf[:, 2, :], cntf[:, 2, :], float(P), None, ALU.mult))
                then(v.tensor_tensor(tmp3, ps[7][:, 0:NT * E].rearrange("p (i e) -> p i e", e=E),
                                     cntf[:, 2, :].unsqueeze(1).to_broadcast([P, NT, E]), ALU.add))
                for k in range(TOPK):
                    then(v.tensor_tensor(oh[k], oh[k], tmp3, ALU.mult))
                    then(v.tensor_reduce(t16, oh[k], AX.X, ALU.add))
                    then(v.tensor_copy(pos[:, :, k], t16))
                then(v.tensor_tensor(tcmp[:, :, :], cntf[0:1, 1, :].unsqueeze(1).to_broadcast([1, SLOT_TILES, E]),
                                     tidx[:, :, :], ALU.is_le))
                then(v.tensor_reduce(tsum[:, :], tcmp[:, :, :], AX.X, ALU.add))
                then(v.tensor_scalar(etab[:, NT:], tsum[:, :], float(E - 1), None, ALU.min))
                v.engine_nop().then_inc(pos_ready, 2)

                n, e0, nh, up = ETILES[l], EB0[l], HID[l] // P, UP[l]
                if l >= 2:
                    v.wait_ge(b2_in, 32 * (l - 1))

                def take_e(i, u):
                    wait(v, et_done, e0 + i + 1)
                    wait(v, u_done, e0 + i - 1)
                    v.tensor_copy(xT[:, u, :, :].rearrange("p k n -> p (k n)"), ps[5][:, 0:D]).then_inc(exT_ready, 1)

                def hidden(i, u):
                    if l == 1:
                        wait(v, half_ready, i + 1)
                        wait(v, ht_done, e0 + i - 1)
                        v.tensor_tensor(h[:, u, 0:512], h[:, u, 512:1024], ps[1][:, :], ALU.mult)\
                            .then_inc(h_ready, 1)
                    if l >= 2:
                        wait(v, u_done, e0 + i + 1)
                        wait(v, ht_done, e0 + i - 1)
                        for k in range(up // 512):
                            m = v.tensor_copy(h[:, u, k * 512:(k + 1) * 512], ps[k][:, :])
                        m.then_inc(h_ready, 1)
                take_e(0, 0)
                hidden(0, 0)
                take_e(1, 1)
                shared_tiles = [SHARED[l]]

                def to_list():
                    shared_tiles[0] = False

                def body(i, u, q, left):
                    if l < 2:
                        wait(v, ht_done, e0 + i + 1)
                        wait(v, d_done, e0 + i - 1)
                        for k in range(nh // 4):
                            m = v.tensor_copy(hT[:, u, k * 512:(k + 1) * 512], ps[2 + k][:, :])
                        m.then_inc(hT_ready, 1)
                    if left > 0:
                        hidden(i + 1, 1 - u)
                    if l >= 2:
                        e = v.value_load(etab[0:1, bass.ds(i, 1)], min_val=0, max_val=E)
                    wait(v, d_done, e0 + i + 1)
                    if shared_tiles[0]:
                        if l >= 2:
                            v.tensor_tensor(ybuf[:, u, :], ps[4][:, 0:D], b2b[:, bass.ds(e * D, D)], ALU.add).then_inc(y_sum, 1)
                            wait(v, y_sum, NT * (l - 2) + i + 1)
                            v.scalar_tensor_tensor(X[:, i, :], ybuf[:, u, :], tgf, X[:, i, :], ALU.mult,
                                                   ALU.add).then_inc(y_ready, 1)
                        else:
                            v.scalar_tensor_tensor(X[:, i, :], ps[4][:, 0:D], tgf, X[:, i, :], ALU.mult,
                                                   ALU.add).then_inc(y_ready, 1)
                    else:
                        stored = q - NT // 2 if SHARED[l] else q
                        wait(v, y_stored[u], 16 * (STORES[u] * l + stored))
                        if l >= 2:
                            m = v.tensor_tensor(ybuf[:, u, :], ps[4][:, 0:D], b2b[:, bass.ds(e * D, D)], ALU.add)
                        else:
                            m = v.tensor_copy(ybuf[:, u, :], ps[4][:, 0:D])
                        m.then_inc(y_ready, 1)
                    if left > 1:
                        take_e(i + 2, u)
                expert_tiles(v, None, n, body, NT // 2 if SHARED[l] else None, to_list)
                v.wait_ge(y_ready, e0 + n)

                for g in (g1, g2):
                    stp.mark(v.tensor_scalar(g[:, :], g[:, :], tgf, None, ALU.mult))
                v.wait_ge(v_step[l], stp.count)

                def body(i, u, q):
                    wait(v, y_in[u], 32 * (NT // 4 * l + q + 1))
                    then(v.scalar_tensor_tensor(X[:, i, :], ygat[:, u, 0, :], col(g1, i), X[:, i, :], ALU.mult, ALU.add))
                    then(v.scalar_tensor_tensor(X[:, i, :], ygat[:, u, 1, :], col(g2, i), X[:, i, :], ALU.mult, ALU.add))
                    finish(i, c_done)
                token_quads(v, stp, body)
                if l + 1 < LAYERS:
                    gather_statistics(c_done, (l + 1) * NT)


def kernel(**inputs):
    import numpy as _np
    import concourse.bacc as _bacc
    from concourse import mybir as _mybir
    from concourse.bass_utils import run_bass_kernel_spmd as _run

    x = {k: _np.asarray(v) for k, v in inputs.items()}

    def cols(w):
        return w.reshape(-1, P, w.shape[-1]).transpose(1, 0, 2)

    def flat(*ws):
        return _np.concatenate([cols(w).reshape(P, -1) for w in ws], axis=1)

    def part(v):
        return _np.moveaxis(v.reshape(v.shape[:-1] + (-1, P)), -1, 0)

    c = x["ctx_1024"]
    T_ = _np.transpose
    w0 = [flat(x["L0_ffn_experts_w1"][e].T, x["L0_ffn_experts_w2"][e].T) for e in range(E)]
    w0.append(flat(x["L0_ffn_shared_w1"].T, x["L0_ffn_shared_w2"].T))
    w1 = [flat(_np.concatenate([x["L1_ffn_W1"][e].T, x["L1_ffn_W2"][e].T], axis=1), x["L1_ffn_W3"][e].T)
          for e in range(E)]
    w2 = [flat(x["L2_ffn_ew1"][e], x["L2_ffn_ew2"][e]) for e in range(E)] + [flat(x["L2_ffn_sw1"], x["L2_ffn_sw2"])]
    w3 = [flat(x["L3_ffn_rw1"][e], x["L3_ffn_rw2"][e]) for e in range(E)] + [flat(x["L3_ffn_sw1"], x["L3_ffn_sw2"])]
    W3 = x["L3_xattn_W"]
    arrays = {
        "x": x["x"].reshape(T, D),
        "ctxT": T_(c.reshape(B, S2, DK, P), (3, 2, 0, 1)),
        "ctxr": T_(c.reshape(B, 2, KH, D), (2, 1, 0, 3)),
        "projT": cols(x["L0_xattn_projection"].T),
        "gateT": _np.stack([cols(x["L0_ffn_gate_w"].T), cols(x["L1_ffn_Wg"].T), cols(x["L2_ffn_router_w"].T),
                            cols(x["L3_ffn_router_w"])], axis=1),
        "gates": _np.concatenate([x["g_xattn"], x["g_ffn"]]),
        "bqk": part(_np.stack([x["L1_xattn_wq_b"], x["L1_xattn_wk_b"]])),
        "simw": part(x["L2_xattn_w_sim"].reshape(3, D)),
        "bsim": x["L2_xattn_b_sim"].reshape(1, 1),
        "rb3": x["L3_ffn_router_b"],
        "w0": _np.stack(w0), "w1": _np.stack(w1), "w2": _np.stack(w2), "w3": _np.stack(w3),
        "qkvo": _np.stack([cols(x[f"L1_xattn_w{n}_k"]) for n in "qkvo"]),
        "bv": x["L1_xattn_wv_b"], "bo": x["L1_xattn_wo_b"],
        "mask": x["mask_BxSxS2_ik1"].reshape(T, S2), "side": x["fside_BxSxS2_0"].reshape(T, S2),
        "Wqv": cols(x["L2_xattn_W_qv"]), "bqv": x["L2_xattn_b_qv"],
        "nw": x["L2_ffn_norm_weight"],
        "b2_2": _np.concatenate([x["L2_ffn_eb2"].reshape(-1), x["L2_ffn_sb2"]]),
        "b1_2": part(_np.concatenate([x["L2_ffn_eb1"], x["L2_ffn_sb1"][None]])).reshape(P, -1),
        "W3x": _np.stack([cols(W3[:, :D].T), cols(W3[:, D:].T)], axis=1),
        "b3": x["L3_xattn_b"],
        "b2_3": _np.concatenate([x["L3_ffn_rb2"].reshape(-1), x["L3_ffn_sb2"]]),
        "b1_3": part(_np.concatenate([x["L3_ffn_rb1"], x["L3_ffn_sb1"][None]])).reshape(P, -1),
    }
    nc = _bacc.Bacc("TRN2", target_bir_lowering=False, num_devices=1)
    maps, aps = {}, {}
    for name, v in arrays.items():
        v = _np.ascontiguousarray(v)
        maps[f"in_{name}"] = v
        aps[name] = nc.dram_tensor(f"in_{name}", v.shape, _mybir.dt.from_np(v.dtype), kind="ExternalInput").ap()
    out = nc.dram_tensor("out_x", (T, D), _mybir.dt.float32, kind="ExternalOutput").ap()
    xn_tokens = nc.dram_tensor("xn_tokens", (T, D), _mybir.dt.float32).ap()
    xn_rows = nc.dram_tensor("xn_rows", (ROWS, D), _mybir.dt.float32).ap()
    y_rows = nc.dram_tensor("y_rows", (ROWS, D), _mybir.dt.float32).ap()
    bass_flamingo_moe_kernel(nc, aps, out, xn_tokens, xn_rows, y_rows)
    r = _run(nc, [maps], core_ids=[0])
    return r.results[0]["out_x"].reshape(B, S, D)
```

```python
from contextlib import ExitStack

import numpy as np
import concourse.bass as bass
from concourse import mybir
from concourse.alu_op_type import AluOpType as ALU

F32 = mybir.dt.float32
I32 = mybir.dt.int32
U32 = mybir.dt.uint32
ACT = mybir.ActivationFunctionType
AX = mybir.AxisListType

P = 128
D = 256
DK = D // P
B = 2
S = 1024
T = B * S
NT = T // P
NTB = NT // B
S2 = 154
KH = S2 // 2
KR = S2 - P
E = 8
TOPK = 2
SLOT_TILES = T * TOPK // P + E - 1
ROWS = SLOT_TILES * P
HEADS = 16
DH = D // HEADS
HC = HEADS // DK
M = 64
NEG = 1.0e9
LAYERS = 4

UP = [1024, 1024, 1024, 512]
HID = [1024, 512, 1024, 512]
SHARED = [True, False, True, True]
WSLOTS = [E + SHARED[l] for l in range(LAYERS)]
WSIZE = [DK * UP[l] + HID[l] // P * D for l in range(LAYERS)]
ETILES = [SLOT_TILES + NT * SHARED[l] for l in range(LAYERS)]


def bass_flamingo_moe_kernel(nc, a, out, xn_tokens, xn_rows, y_rows):
    with ExitStack() as ctx:
        def sb(name, shape, dt=F32):
            return ctx.enter_context(nc.sbuf_tensor(name, shape, dt))

        def sem(name):
            return ctx.enter_context(nc.semaphore(name))

        def sems(name, n=2):
            return [sem(f"{name}{k}") for k in range(n)]

        X = sb("X", [P, NT, D])
        W = sb("W", [P, max(WSLOTS[l] * WSIZE[l] for l in range(LAYERS))])
        arena = sb("arena", [P, 4 * 1024])
        misc = sb("misc", [P, 2560])
        xn = sb("xn", [P, 2, D])
        xT = sb("xT", [P, 2, DK, P])
        tiles = sb("tiles", [P, 4 * D])
        ident = sb("ident", [P, P])
        ones = sb("ones", [P, P])
        upper = sb("upper", [P, P])
        ctxT = sb("ctxT", [P, DK, B, S2])
        ctxr = sb("ctxr", [KH, 2, B, D + 1])
        gateT = sb("gateT", [P, LAYERS, DK, E])
        tg = sb("tg", [P, 2 * LAYERS])
        junk = sb("junk", [1, 3])
        eps = sb("eps", [P, 2])
        MV = sb("MV", [P, NT, 2])
        STD = sb("STD", [P, NT])
        RSTD = sb("RSTD", [P, NT])
        VT = sb("VT", [P, NT])
        st6 = sb("st6", [P, NT, 6])
        g1 = sb("g1", [P, NT])
        g2 = sb("g2", [P, NT])
        pos = sb("pos", [P, NT, 2], I32)
        etab = sb("etab", [1, NT + SLOT_TILES], I32)
        idx = sb("idx", [P, 2, 2, 1], U32)
        b1T = sb("b1T", [P, (E + 1) * 8])
        bqk = sb("bqk", [P, 2, DK])
        headm = sb("headm", [P, HC])
        remm = sb("remm", [P, 4])
        zb = sb("zb", [P, 2 * P], mybir.dt.bfloat16)
        simw = sb("simw", [P, 3, DK])
        bsim = sb("bsim", [1, 1])
        rb3 = sb("rb3", [P, E])
        small = sb("small", [P, 24])
        rs = sb("rs", [P, 2, HEADS])
        rr = sb("rr", [P, 2, HEADS])
        MX = sb("MX", [P, NT])
        EB = sb("EB", [P, NT])
        simrow = sb("simrow", [1, B, S2])
        downb = sb("downb", [P, E])
        tidx = sb("tidx", [1, SLOT_TILES, E])
        cnti = sb("cnti", [P, E], I32)
        cntf = sb("cntf", [P, 3, E])
        negm = sb("negm", [P, 2, HC * 2])

        xs = tiles[:, 0:2 * D].rearrange("p (u n) -> p u n", u=2)
        ybuf = tiles[:, 2 * D:4 * D].rearrange("p (u n) -> p u n", u=2)
        KVZ = arena[0:M, 0:B * (D + 1)].rearrange("p (b n) -> p b n", b=B)
        rfk = arena[0:KH, 1024:1280].rearrange("p (s b m) -> p s b m", s=2, b=B)
        rf = arena[0:M, 2048:2304].rearrange("p (u n) -> p u n", u=2)
        tcmp = arena[0:1, 3072 + 392:3072 + 704].rearrange("p (i e) -> p i e", e=E)
        tsum = arena[0:1, 3072 + 704:3072 + 704 + SLOT_TILES]
        projT = arena[:, 2560:2560 + DK * M].rearrange("p (k n) -> p k n", k=DK)
        half = arena[:, 0:1024].rearrange("p (u n) -> p u n", u=2)
        hT = arena[:, 2048:4096].rearrange("p (u n) -> p u n", u=2)
        ygat = arena[:, 0:2048].rearrange("p (u r n) -> p u r n", u=4, r=TOPK)
        qkvo = arena[:, 2048:4096].rearrange("p (w k n) -> p w k n", w=4, k=DK)
        XN = arena[:, :].rearrange("p (i n) -> p i n", i=NT)
        qT = arena[:, 0:512].rearrange("p (u c n) -> p u c n", u=2, c=DK)
        hcW = arena[:, 0:1024].rearrange("p (b k n) -> p b k n", b=B, k=DK)
        AT2 = arena[:, 1024:1536].rearrange("p (u n) -> p u n", u=2)
        A2 = arena[:, 1536:1536 + 2 * S2].rearrange("p (u n) -> p u n", u=2)
        hqT = arena[:, 2048:2560].rearrange("p (u n) -> p u n", u=2)
        xhT = arena[:, 2560:3072].rearrange("p (u n) -> p u n", u=2)
        Rt = arena[:, 3072:4096]
        w_end = WSLOTS[1] * WSIZE[1]
        KBD = W[:, w_end:w_end + 4928].rearrange("p (c b h s) -> p c b h s", c=DK, b=B, h=HC)
        PR = W[:, w_end + 4928:w_end + 9856].rearrange("p (u h s) -> p u h s", u=2, h=HEADS)
        PT = W[:, w_end + 9856:w_end + 11904].rearrange("p (g n) -> p g n", g=4)
        PL = arena[:, 512:512 + 2 * HEADS * KR].rearrange("p (u h s) -> p u h s", u=2, h=HEADS)
        ctxR = PT[:, 0:1, 0:DK * B * 4 * KR].rearrange("p o (k b n) -> p (o k) b n", k=DK, b=B)
        w1 = [[arena[:, 0:2048]] * 2, [W[:, w_end + NT * D + 2048 * u:w_end + NT * D + 2048 * (u + 1)] for u in range(2)]]
        XNs = W[:, w_end:w_end + NT * D].rearrange("p (i n) -> p i n", i=NT)
        kT = PR[:, 0, 0:4, :].rearrange("p h s -> p (h s)").rearrange("p (c n) -> p c n", c=DK)
        Vh = tiles[:, :].rearrange("p (b s n) -> p b s n", b=B, s=2)
        msk = misc[:, 0:2 * S2].bitcast(I32).rearrange("p (u s) -> p u s", u=2)
        side = misc[:, 2 * S2:4 * S2].rearrange("p (u s) -> p u s", u=2)
        neg = misc[:, 4 * S2:6 * S2].rearrange("p (u s) -> p u s", u=2)
        bvr = misc[:, 1024:1280]
        orow = misc[:, 1280:1536]
        obuf = misc[:, 1536:2048].rearrange("p (u n) -> p u n", u=2)
        oT = misc[:, 2048:2560].rearrange("p (u n) -> p u n", u=2)
        Wqv = misc[:, 0:2048].rearrange("p (k n) -> p k n", k=4 * DK)
        qvrow = misc[:, 2048:2304]
        W3x = misc[:, 0:1024].rearrange("p (w k n) -> p w k n", w=2, k=DK)
        rowB = misc[:, 1024:1536].rearrange("p (b n) -> p b n", b=B)
        b3row = misc[:, 1536:1792]
        csum = small[:, 0:4].rearrange("p (k b) -> p k b", k=DK)
        b2b = misc[:, 0:(E + 1) * D]
        nwrow = misc[:, 2304:2560]
        CW = tiles[:, 0:DK * B * S2].rearrange("p (k b s) -> p k b s", k=DK, b=B)

        ps = [ctx.enter_context(nc.psum_tensor(f"ps{k}", [P, 512], F32)) for k in range(8)]

        TWO, ONE = [ps[5], ps[0]], [ps[5], ps[5]]

        x_in, ctx_in, w_shared, w_in = sems("x_in", NT // 4), sem("ctx_in"), sem("w_shared"), sem("w_in")
        xw_in, b2_in, pad_in = sem("xw_in"), sem("b2_in"), sem("pad_in")
        consts, tg_ready = sem("consts"), sem("tg_ready")
        stats, std_ready = sem("stats"), sem("std_ready")
        xn_ready, t_done, xT_ready = sem("xn_ready"), sem("t_done"), sem("xT_ready")
        xn_copied = sem("xn_copied")
        x_done = sem("x_done")
        set_pe, set_act, set_v, set_pool = sem("set_pe"), sem("set_act"), sem("set_v"), sem("set_pool")
        r_done, rf_ready, o_done = sem("r_done"), sem("rf_ready"), sem("o_done")
        q_done, q_ready = sem("q_done"), sem("q_ready")
        s_done, l_ready, e_ready, p_ready = sem("s_done"), sem("l_ready"), sem("e_ready"), sem("p_ready")
        pt_done, pt_v, pt_a, pv_done = sem("pt_done"), sem("pt_v"), sem("pt_a"), sem("pv_done")
        on_ready, ot_done, ot_ready = sem("on_ready"), sem("ot_done"), sem("ot_ready")
        side_in, neg_ready = sems("side_in"), sem("neg_ready")
        mx_ready, a_ready, an_ready, at_done, at_ready = (sem("mx_ready"), sem("a_ready"), sem("an_ready"),
                                                          sem("at_done"), sem("at_ready"))
        hq_done, hq_ready = sem("hq_done"), sem("hq_ready")
        xn_stored, lg_done, lg_used = sems("xn_stored"), sem("lg_done"), sem("lg_used")
        rt_act, rt_v, rt_pe = sem("rt_act"), sem("rt_v"), sem("rt_pe")
        pos_ready, pool_step = sem("pos_ready"), sem("pool_step")
        sc_in, sc_out = sems("sc_in"), sems("sc_out")
        xs_in, et_done, exT_ready = sems("xs_in"), sem("et_done"), sem("exT_ready")
        w1_ready, u_done, half_ready, hT_ready = sem("w1_ready"), sem("u_done"), sem("half_ready"), sem("hT_ready")
        d_done, y_ready, y_stored = sem("d_done"), sem("y_ready"), sems("y_stored")
        y_in, c_done = sems("y_in", 4), sem("c_done")
        xpart_done = sem("xpart_done")
        y_sum, sc_all = sem("y_sum"), sem("sc_all")
        out_stored, x0_stats = sem("out_stored"), sem("x0_stats")
        v_step = [sem(f"v_step{l}") for l in range(LAYERS)]
        mx1, route, simset, gate_in, vready = sem("mx1"), sem("route"), sem("simset"), sem("gate_in"), sem("vready")
        last_keys = sem("last_keys")

        def wait(eng, s, value):
            if type(value) is int and value <= 0:
                return
            eng.wait_ge(s, value)

        def alone(eng):
            eng.wait_ge(consts, 12)

        def alone_pool(u):
            return nc.gpsimd.tensor_tensor(junk[:, u:u + 1], ones[0:1, 0:1], ones[0:1, 0:1], ALU.mult)

        class Steps:
            def __init__(self, eng, s, count=0):
                self.eng, self.s, self.count = eng, s, count

            def then(self, ins):
                self.mark(ins)
                self.eng.wait_ge(self.s, self.count)

            def mark(self, ins):
                self.count = self.count + 1
                ins.then_inc(self.s, 1)

        def loop(eng, steps, first, last, body):
            before = steps.count if steps else 0
            n0 = probe[0] if steps else 0
            with eng.Fori(first, last) as q:
                if steps and n0:
                    steps.count = before + (q - first) * n0
                body(q)
            if steps:
                steps.count = before + (last - first) * n0

        probe = [0]

        def token_tiles(eng, steps, body):
            def pair(q, b, end=False):
                for u in range(2):
                    body(2 * q + u, u, q, b, 0 if not end else (1 if u == 0 else 2))
            before = steps.count if steps else 0
            pair(0, 0)
            probe[0] = steps.count - before if steps else 0
            loop(eng, steps, 1, NTB // 2, lambda q: pair(q, 0))
            loop(eng, steps, NTB // 2, NT // 2 - 1, lambda q: pair(q, 1))
            pair(NT // 2 - 1, 1, True)

        def token_quads(eng, steps, body):
            def quad(q):
                for u in range(4):
                    body(4 * q + u, u, q)
            before = steps.count
            quad(0)
            probe[0] = steps.count - before
            loop(eng, steps, 1, NT // 4 - 1, quad)
            quad(NT // 4 - 1)

        def expert_tiles(eng, steps, n, body, at=None, between=None):
            q1 = (n - 3) // 2
            def pair(q):
                for u in range(2):
                    body(2 * q + u, u, q, 3)
            before = steps.count if steps else 0
            pair(0)
            probe[0] = steps.count - before if steps else 0
            if at:
                loop(eng, steps, 1, at, pair)
                if between:
                    between()
                pair(at)
                loop(eng, steps, at + 1, q1, pair)
            else:
                loop(eng, steps, 1, q1, pair)
            for k in range(3):
                i = 2 * q1 + k
                body(i, i % 2, i // 2, 2 - k)

        FX = [0, 32, 64, 112]
        FX2 = 80
        FG = [16, 48, 96, 128]
        EB0 = [sum(ETILES[:l]) for l in range(LAYERS)]
        EP = [[sum((ETILES[k] + 1 - u) // 2 for k in range(l)) for u in range(2)] for l in range(LAYERS + 1)]

        STORES = [(SLOT_TILES + 1 - u) // 2 for u in range(2)]

        block = ctx.enter_context(nc.Block())

        @block.sync
        def _(sp):
            for i in range(0, NT, 4):
                sp.dma_start(X[:, i:i + 4, :], a["x"][i * P:(i + 4) * P, :].rearrange("(i p) d -> p i d", p=P)).then_inc(x_in[i // 4], 16)
            first = [(ctxT[:, :, :, :], a["ctxT"]), (ctxr[:, :, :, 0:D], a["ctxr"]), (projT[:, :, :], a["projT"]),
                     (gateT[:, :, :, :], a["gateT"]), (small[:, 16:24], a["gates"].partition_broadcast(P)),
                     (bqk[:, :, :], a["bqk"]), (simw[:, :, :], a["simw"]), (bsim[:, :], a["bsim"]),
                     (rb3[:, :], a["rb3"].partition_broadcast(P))]
            for dst, src in first:
                sp.dma_start(dst, src).then_inc(ctx_in, 16)

            def weights(l):
                for k, e in enumerate(reversed(range(WSLOTS[l]))):
                    shared = SHARED[l] and e == E
                    if l:
                        sp.wait_ge(c_done, l * NT)
                        wait(sp, x_done, l * NT + k)
                    sp.dma_start(W[:, e * WSIZE[l]:(e + 1) * WSIZE[l]],
                                 a[f"w{l}"][e]).then_inc(w_shared if shared else w_in, 16)
            weights(0)

            for l in range(LAYERS):
                def store_xn(i, u, q, b, last):
                    wait(sp, xn_ready, FG[l] + i + 1)
                    sp.dma_start(xn_tokens[bass.ds(i * P, P), :], xn[:, u, :]).then_inc(xn_stored[u], 16)
                if l == 2:
                    sp.wait_ge(x_done, (l + 1) * NT)
                    sp.dma_start(nwrow, a["nw"].partition_broadcast(P)).then_inc(xw_in, 16)
                if l >= 2:
                    sp.wait_ge(x_done, (l + 1) * NT)
                    sp.dma_start(b2b, a[f"b2_{l}"].partition_broadcast(P)).then_inc(b2_in, 16)
                    sp.dma_start(b1T[:, 0:(E + 1) * HID[l] // P], a[f"b1_{l}"]).then_inc(b2_in, 16)
                if SHARED[l]:
                    token_tiles(sp, None, store_xn)
                    for u in range(2):
                        sp.wait_ge(xn_stored[u], 16 * NTB * sum(SHARED[:l + 1]))

                n, first = ETILES[l], NT if SHARED[l] else 0

                def sorted_rows_ready():
                    if l % 2:
                        sp.wait_ge(sc_all, 16 * TOPK * NT * (l // 2 + 1))
                    else:
                        for u in range(2):
                            sp.wait_ge(sc_out[u], 32 * NTB * (l // 2 + 1))
                    sp.wait_ge(w_in, 16 * E * (l + 1))

                def rows(i, u, q, left):
                    wait(sp, et_done, EB0[l] + i - 1 if not (type(i) is int and i < 2) else EB0[l])
                    src = xn_rows[bass.ds((i - first) * P, P), :] if listed[0] else xn_tokens[bass.ds(i * P, P), :]
                    sp.dma_start(xs[:, u, :], src).then_inc(xs_in[u], 16)

                def begin_list():
                    sorted_rows_ready()
                    listed[0] = True
                listed = [not SHARED[l]]
                if SHARED[l]:
                    expert_tiles(sp, None, n, rows, NT // 2, begin_list)
                else:
                    begin_list()
                    expert_tiles(sp, None, n, rows)
                if l + 1 < LAYERS:
                    sp.wait_ge(y_ready, EB0[l] + n)
                    if l == 0:
                        for w in range(4):
                            sp.dma_start(qkvo[:, w, :, :], a["qkvo"][w]).then_inc(xw_in, 16)
                        sp.dma_start(bvr, a["bv"].partition_broadcast(P)).then_inc(xw_in, 16)
                        sp.dma_start(orow, a["bo"].partition_broadcast(P)).then_inc(xw_in, 16)
                    if l == 1:
                        sp.dma_start(Wqv, a["Wqv"]).then_inc(xw_in, 16)
                        sp.dma_start(qvrow, a["bqv"].partition_broadcast(P)).then_inc(xw_in, 16)
                    if l == 2:
                        sp.dma_start(W3x, a["W3x"]).then_inc(xw_in, 16)
                        sp.dma_start(b3row, a["b3"].partition_broadcast(P)).then_inc(xw_in, 16)
                    weights(l + 1)
            def store_out(i, u, q, b, last):
                wait(sp, c_done, (LAYERS - 1) * NT + i + 1)
                sp.dma_start(out[bass.ds(i * P, P), :], X[:, i, :]).then_inc(out_stored, 16)
            token_tiles(sp, None, store_out)
            sp.wait_ge(out_stored, 16 * NT)

        @block.gpsimd
        def _(pool):
            st = Steps(pool, pool_step)
            st.mark(pool.memset(ident[:, :], 0.0))
            st.mark(pool.memset(upper[:, :], 0.0))
            st.mark(pool.memset(headm[:, :], 1.0))
            st.then(pool.memset(remm[:, :], 1.0))
            pool.memset(ones[:, :], 1.0).then_inc(consts, 1)
            pool.memset(ctxr[:, :, :, D:D + 1], 1.0).then_inc(consts, 1)
            pool.memset(eps[:, 0:1], 1e-5).then_inc(consts, 1)
            pool.memset(eps[:, 1:2], 1e-8).then_inc(consts, 1)
            pool.affine_select(out=ident[:, :], in_=ident[:, :], compare_op=ALU.not_equal, fill=1.0, base=0,
                               pattern=[[-1, P]], channel_multiplier=1).then_inc(consts, 1)
            pool.affine_select(out=upper[:, :], in_=upper[:, :], compare_op=ALU.is_ge, fill=1.0, base=0,
                               pattern=[[-1, P]], channel_multiplier=1).then_inc(consts, 1)
            st.then(pool.affine_select(out=headm[:, :], in_=headm[:, :], compare_op=ALU.is_ge, fill=0.0, base=0,
                                       pattern=[[-DH, HC]], channel_multiplier=1))
            pool.affine_select(out=headm[:, :], in_=headm[:, :], compare_op=ALU.is_ge, fill=0.0, base=DH - 1,
                               pattern=[[DH, HC]], channel_multiplier=-1).then_inc(consts, 1)
            st.then(pool.affine_select(out=remm[:, :], in_=remm[:, :], compare_op=ALU.is_ge, fill=0.0, base=0,
                                       pattern=[[-KR, 4]], channel_multiplier=1))
            pool.affine_select(out=remm[:, :], in_=remm[:, :], compare_op=ALU.is_ge, fill=0.0, base=KR - 1,
                               pattern=[[KR, 4]], channel_multiplier=-1).then_inc(consts, 1)
            pool.memset(zb[:, :], 0.0).then_inc(consts, 1)
            pool.iota(downb[:, :], pattern=[[-1, E]], base=E, channel_multiplier=0,
                      allow_small_or_imprecise_dtypes=True).then_inc(consts, 1)
            pool.iota(tidx[:, :, :], pattern=[[1, SLOT_TILES], [0, E]], base=0, channel_multiplier=0,
                      allow_small_or_imprecise_dtypes=True).then_inc(consts, 1)
            pool.iota(etab[:, 0:NT], pattern=[[0, NT]], base=E, channel_multiplier=0).then_inc(consts, 1)
            st.then(pool.memset(misc[:, :], 0.0))
            for i in range(8):
                k0, k1 = SLOT_TILES * i // 8, SLOT_TILES * (i + 1) // 8
                pool.dma_start(xn_rows[k0 * P:k1 * P, :].rearrange("(p r) d -> p (r d)", p=P),
                               misc[:, 0:(k1 - k0) * D]).then_inc(pad_in, 16)

            for l in range(LAYERS):
                if l == 1:
                    def load(i, u, q):
                        wait(pool, p_ready, 2 * (i - 1))
                        wait(pool, neg_ready, i - 1)
                        pool.dma_start(msk[:, u, :], a["mask"][bass.ds(i * P, P), :]).then_inc(side_in[u], 16)
                        pool.dma_start(side[:, u, :], a["side"][bass.ds(i * P, P), :]).then_inc(side_in[u], 16)

                    def mask(i, u, q):
                        wait(pool, side_in[u], 32 * (q + 1))
                        wait(pool, l_ready, 6 * (i - 1))
                        alone_pool(u)
                        pool.tensor_scalar(neg[:, u, :], msk[:, u, :], 1.0, NEG, ALU.subtract,
                                           ALU.mult).then_inc(neg_ready, 1)

                    def weigh(i, u, q, chunks=range(DK)):
                        for c in chunks:
                            wait(pool, e_ready, 2 * i + c + 1)
                            for dst, k0, k1 in ((PR[:, u, c * HC:(c + 1) * HC, 0:P], 0, P),
                                                (PL[:, u, c * HC:(c + 1) * HC, :], P, S2)):
                                m = pool.tensor_tensor(dst, PR[:, u, c * HC:(c + 1) * HC, k0:k1],
                                                       side[:, u, k0:k1].unsqueeze(1).to_broadcast([P, HC, k1 - k0]),
                                                       ALU.mult)
                            m.then_inc(p_ready, 1)
                    pool.wait_ge(d_done, EB0[1])
                    load(0, 0, 0)
                    load(1, 1, 0)
                    mask(0, 0, 0)
                    mask(1, 1, 0)
                    weigh(0, 0, 0)

                    def body(i, u, q, b, last):
                        if not last:
                            load(i + 2, u, q + 1)
                        if last < 2:
                            weigh(i + 1, 1 - u, q + u, [0])
                        if not last:
                            mask(i + 2, u, q + 1)
                        if last < 2:
                            weigh(i + 1, 1 - u, q + u, [1])
                    token_tiles(pool, None, body)
                if l == 2:
                    pool.wait_ge(set_v, 6)
                    pool.partition_all_reduce(small[:, 6:8], small[:, 4:6], P,
                                              bass.bass_isa.ReduceOp.max).then_inc(set_pool, 1)

                pool.wait_ge(pos_ready, 2 * l + 1)
                if l == 0:
                    pool.wait_ge(pad_in, 16 * 8)

                def places(i, u):
                    st.mark(pool.tensor_copy(idx[:, u, 0, :], pos[:, i, 0:1].bitcast(U32)))
                    st.then(pool.tensor_copy(idx[:, u, 1, :], pos[:, i, 1:2].bitcast(U32)))

                def scatter(i, u, q, b, last):
                    k = l // 2
                    wait(pool, sc_out[u], 32 * (NTB * k + q))
                    pool.dma_start(xn[:, u, :], xn_tokens[bass.ds(i * P, P), :]).then_inc(sc_in[u], 16)
                    places(i, u)
                    wait(pool, sc_in[u], 16 * (NTB * k + q + 1))
                    st.mark(alone_pool(2))
                    for k in range(TOPK):
                        pool.indirect_dma_start(xn_rows[:, :], bass.IndirectOffsetOnAxis(ap=idx[:, u, k, :], axis=0),
                                                xn[:, u, :], None).then_inc(sc_out[u], 16)
                if l % 2 == 0:
                    for u in range(2):
                        pool.wait_ge(xn_stored[u], 16 * NTB * sum(SHARED[:l + 1]))
                    token_tiles(pool, st, scatter)
                else:
                    pool.wait_ge(xn_copied, (l + 1) // 2 * NT + (NT if l == 3 else 0))
                    for i in range(NT):
                        for k in range(TOPK):
                            pool.indirect_dma_start(xn_rows[:, :],
                                                    bass.IndirectOffsetOnAxis(ap=pos[:, i, k:k + 1].bitcast(U32), axis=0),
                                                    XNs[:, i, :], None).then_inc(sc_all, 16)

                first = NT if SHARED[l] else 0

                def store(j, u, q, left):
                    wait(pool, y_ready, EB0[l] + first + j + 1)
                    pool.dma_start(y_rows[bass.ds(j * P, P), :], ybuf[:, u, :]).then_inc(y_stored[u], 16)
                expert_tiles(pool, None, SLOT_TILES, store)

                if l % 2:
                    pool.wait_ge(sc_all, 16 * TOPK * NT * (l // 2 + 1))
                else:
                    for u in range(2):
                        pool.wait_ge(sc_out[u], 32 * NTB * (l // 2 + 1))
                for u in range(2):
                    pool.wait_ge(y_stored[u], 16 * STORES[u] * (l + 1))

                for i in range(NT):
                    u = i % 4
                    wait(pool, c_done, l * NT + i - 3 if i > 3 else 0)
                    for k in range(TOPK):
                        pool.indirect_dma_start(ygat[:, u, k, :], None, y_rows[:, :],
                                                bass.IndirectOffsetOnAxis(ap=pos[:, i, k:k + 1].bitcast(U32),
                                                                          axis=0)).then_inc(y_in[u], 16)

        @block.tensor
        def _(pe):
            def transpose_x(f, u, banks=TWO):
                wait(pe, xn_ready, f + 1)
                wait(pe, xT_ready, f - 1 if banks is TWO else f)
                for k in range(DK):
                    m = pe.transpose(banks[u][:, k * P:(k + 1) * P], xn[:, u, k * P:(k + 1) * P], ident[:, :])
                m.then_inc(t_done, 1)

            pe.wait_ge(consts, 12)
            pe.wait_ge(ctx_in, 16 * 9)
            for l in range(LAYERS):
                f0 = FX[l]
                if l == 0:
                    for b in range(B):
                        for s in range(2):
                            for k in range(DK):
                                m = pe.matmul(ps[0][0:KH, (2 * b + s) * M:(2 * b + s + 1) * M],
                                              ctxT[:, k, b, s * KH:(s + 1) * KH], projT[:, k, :],
                                              start=(k == 0), stop=(k == DK - 1))
                    m.then_inc(set_pe, 1)
                    pe.wait_ge(set_act, 1)
                    for b in range(B):
                        for s in range(2):
                            m = pe.matmul(ps[1 + b][0:M, 0:D + 1], rfk[:, s, b, :], ctxr[:, s, b, :],
                                          start=(s == 0), stop=(s == 1))
                    m.then_inc(set_pe, 1)
                    pe.wait_ge(set_v, 1)

                    def features(i, u):
                        wait(pe, xT_ready, f0 + i + 1)
                        wait(pe, rf_ready, i)
                        for k in range(DK):
                            m = pe.matmul(ps[2][0:M, 0:P], projT[:, k, :], xT[:, u, k, :],
                                          start=(k == 0), stop=(k == DK - 1))
                        m.then_inc(r_done, 1)
                    transpose_x(f0, 0)
                    transpose_x(f0 + 1, 1)
                    features(0, 0)

                    def body(i, u, q, b, last):
                        wait(pe, rf_ready, i + 1)
                        wait(pe, x_done, i - 1)
                        pe.matmul(ps[1 + 2 * u][:, 0:D + 1], rf[:, u, :], KVZ[:, b, :], start=True,
                                  stop=True).then_inc(o_done, 1)
                        if not last:
                            transpose_x(f0 + i + 2, u)
                        if last < 2:
                            features(i + 1, 1 - u)
                    token_tiles(pe, None, body)
                if l == 1:
                    pe.wait_ge(xw_in, 16 * 6)
                    for c in range(DK):
                        for k in range(DK):
                            m = pe.matmul(ps[c][:, 0:B * S2], qkvo[:, 1, k, c * P:(c + 1) * P],
                                          ctxT[:, k, :, :].rearrange("p b s -> p (b s)"),
                                          start=(k == 0), stop=(k == DK - 1))
                    m.then_inc(set_pe, 1)
                    for b in range(B):
                        for k in range(DK):
                            pe.matmul(ps[2 + b][:, 0:D], ctxT[:, k, b, 0:P], qkvo[:, 2, k, :],
                                      start=(k == 0), stop=(k == DK - 1))
                        wait(pe, last_keys, DK * B)
                        for k in range(DK):
                            m = pe.matmul(ps[2 + b][0:4 * KR, D:2 * D], ctxR[:, k, b, :], qkvo[:, 2, k, :], start=(k == 0), stop=(k == DK - 1))
                    m.then_inc(set_pe, 1)
                    pe.wait_ge(set_v, 5)
                    pe.wait_ge(vready, B)

                    def queries(i, u):
                        wait(pe, xT_ready, f0 + i + 1)
                        wait(pe, q_ready, i)
                        for c in range(DK):
                            for k in range(DK):
                                m = pe.matmul(ps[1][:, c * P:(c + 1) * P], qkvo[:, 0, k, c * P:(c + 1) * P],
                                              xT[:, u, k, :], start=(k == 0), stop=(k == DK - 1))
                        m.then_inc(q_done, 1)

                    def scores(i, u, b, c):
                        if c == 0:
                            wait(pe, q_ready, i + 1)
                        for g in range(3):
                            n = min(3, HC - 3 * g)
                            wait(pe, l_ready, 6 * i + 3 * c + g - 2)
                            pe.matmul(ps[2 + g][:, 0:n * S2], qT[:, u, c, :],
                                      KBD[:, c, b, 3 * g:3 * g + n, :].rearrange("p h s -> p (h s)"),
                                      start=True, stop=True).then_inc(s_done, 1)

                    def copied(i, g):
                        return (pt_a, 2 * i + g // 2) if g % 2 else (pt_v, 3 * i + g // 2)

                    def turn(i, u, g):
                        if g in (0, 2, 4):
                            wait(pe, p_ready, 2 * i + (g // 2 + 1 if g < 4 else 2))
                        s_, n = copied(i, g)
                        wait(pe, s_, n)
                        for j in range(4):
                            src = PR[:, u, 4 * g + j, 0:P] if g < 4 else PL[:, u, 4 * j:4 * j + 4, :].rearrange("p h s -> p (h s)")
                            m = pe.transpose(ps[0 if g % 2 else 6][0:P if g < 4 else 4 * KR, j * P:(j + 1) * P],
                                             src, ident[:, :])
                        m.then_inc(pt_done, 1)

                    def product(i, b, g):
                        if g == 0:
                            wait(pe, on_ready, i)
                            pe.matmul(ps[7][:, 0:D], zb[:, 0:P], zb[:, :], start=True, stop=False)
                        s_, n = copied(i, g)
                        wait(pe, s_, n + 1)
                        for j in range(4):
                            if g < 4:
                                at, w = (4 * g + j) * DH, DH
                                m = pe.matmul(ps[7][:, at:at + w], PT[:, g, j * P:(j + 1) * P], Vh[:, b, 0, at:at + w],
                                              start=False, stop=False)
                            else:
                                at, w = 4 * j * DH, 4 * DH
                                m = pe.matmul(ps[7][:, at:at + w], PT[0:4 * KR, 0, j * P:(j + 1) * P],
                                              Vh[0:4 * KR, b, 1, at:at + w], start=False, stop=(j == 3))
                        m.then_inc(pv_done, 1)

                    def turn_out(i, u):
                        wait(pe, on_ready, i + 1)
                        for k in range(DK):
                            m = pe.transpose(ps[5][:, k * P:(k + 1) * P], obuf[:, u, k * P:(k + 1) * P], ident[:, :])
                        m.then_inc(ot_done, 1)

                    def project(i, u):
                        wait(pe, ot_ready, i + 1)
                        for k in range(DK):
                            m = pe.matmul(ps[1][:, 0:256], oT[:, u, k * P:(k + 1) * P], qkvo[:, 3, k, :],
                                          start=(k == 0), stop=(k == DK - 1))
                        m.then_inc(o_done, 1)
                    transpose_x(f0, 0, ONE)
                    queries(0, 0)
                    transpose_x(f0 + 1, 1, ONE)
                    scores(0, 0, 0, 0)
                    queries(1, 1)
                    scores(0, 0, 0, 1)

                    def body(i, u, q, b, last, f0=f0):
                        first = type(i) is int and i == 0
                        if last < 2:
                            scores(i + 1, 1 - u, (i + 1) // NTB, 0)
                        if not last:
                            wait(pe, ot_ready, i - 1)
                            transpose_x(f0 + i + 2, u, ONE)
                        turn(i, u, 0)
                        turn(i, u, 1)
                        if last < 2:
                            scores(i + 1, 1 - u, (i + 1) // NTB, 1)
                        if not last:
                            wait(pe, x_done, NT + i - 1)
                            queries(i + 2, u)
                        product(i, b, 0)
                        product(i, b, 1)
                        if not first:
                            wait(pe, xT_ready, f0 + i + 3 if not last else f0 + NT)
                            turn_out(i - 1, 1 - u)
                        turn(i, u, 2)
                        turn(i, u, 3)
                        product(i, b, 2)
                        if not first:
                            wait(pe, q_ready, i + 3 if not last else NT)
                            project(i - 1, 1 - u)
                        turn(i, u, 4)
                        product(i, b, 3)
                        product(i, b, 4)
                    token_tiles(pe, None, body)
                    turn_out(NT - 1, 1)
                    wait(pe, x_done, 2 * NT - 1)
                    project(NT - 1, 1)
                if l == 2:
                    pe.wait_ge(simset, 1)
                    for b in range(B):
                        for k in range(DK):
                            m = pe.matmul(ps[6][0:1, b * S2:(b + 1) * S2], simw[:, 1, k:k + 1], ctxT[:, k, b, :],
                                          start=(k == 0), stop=(k == DK - 1))
                    m.then_inc(set_pe, 1)
                    pe.wait_ge(simset, 2)

                    def similarity(i, u, b, n, used):
                        wait(pe, xT_ready, n + 1)
                        wait(pe, *used)
                        for k in range(DK):
                            pe.matmul(ps[2 - u][:, 0:S2], xT[:, u, k, :], CW[:, k, b, :], start=(k == 0), stop=False)
                        pe.matmul(ps[2 - u][:, 0:S2], ones[0:1, :], simrow[0:1, b, :], start=False, stop=True).then_inc(s_done, 1)
                    transpose_x(f0, 0)
                    transpose_x(f0 + 1, 1)

                    def body(i, u, q, b, last, f0=f0):
                        similarity(i, u, b, f0 + i, (mx_ready, i - 1))
                        if not last:
                            transpose_x(f0 + i + 2, u)
                    token_tiles(pe, None, body)
                    pe.wait_ge(set_act, 4)
                    pe.wait_ge(xn_copied, 2 * NT)
                    for b in range(B):
                        for k in range(DK):
                            for j in range(NTB):
                                i = b * NTB + j
                                m = pe.matmul(ps[6][:, 2 * b + k:2 * b + k + 1], XN[:, i, k * P:(k + 1) * P],
                                              EB[:, i:i + 1], start=(j == 0), stop=(j == NTB - 1))
                    m = pe.matmul(ps[6][:, 4:6], ones[:, :], small[:, 8:10], start=True, stop=True)
                    m.then_inc(set_pe, 1)
                    pe.wait_ge(simset, 3)
                    f1 = FX2

                    def turn(i, u):
                        wait(pe, an_ready, i + 1)
                        wait(pe, at_ready, i)
                        for s in range(2):
                            m = pe.transpose(ps[3][0:KH, s * P:(s + 1) * P], A2[:, u, s * KH:(s + 1) * KH], ident[:, :])
                        m.then_inc(at_done, 1)

                    def mix(i, u, b):
                        wait(pe, at_ready, i + 1)
                        wait(pe, hq_ready, 2 * i)
                        for k in range(DK):
                            for s in range(2):
                                m = pe.matmul(ps[4][:, k * P:(k + 1) * P], ctxr[:, s, b, k * P:(k + 1) * P],
                                              AT2[0:KH, u, s * P:(s + 1) * P], start=(s == 0), stop=(s == 1))
                        m.then_inc(hq_done, 1)

                    def project_x(i, u, b):
                        wait(pe, x_done, 2 * NT + i - 1)
                        for k in range(DK):
                            m = pe.matmul(ps[7 - u][:, 0:D], xT[:, u, k, :], hcW[:, b, k, :], start=(k == 0), stop=False)
                        m.then_inc(xpart_done, 1)

                    def project(i, u):
                        wait(pe, hq_ready, 2 * (i + 1))
                        for k in range(DK):
                            pe.matmul(ps[7 - u][:, 0:D], hqT[:, u, k * P:(k + 1) * P], Wqv[:, DK + k, :], start=False, stop=False)
                        for k in range(DK):
                            m = pe.matmul(ps[7 - u][:, 0:D], xhT[:, u, k * P:(k + 1) * P], Wqv[:, 2 * DK + k, :],
                                          start=False, stop=(k == DK - 1))
                        m.then_inc(o_done, 1)
                    transpose_x(f1, 0)
                    similarity(0, 0, 0, f1, (mx_ready, NT))
                    transpose_x(f1 + 1, 1)

                    def body(i, u, q, b, last, f1=f1):
                        turn(i, u)
                        project_x(i, u, b)
                        mix(i, u, b)
                        if last < 2:
                            similarity(i + 1, 1 - u, (i + 1) // NTB, f1 + i + 1, (a_ready, i))
                        if not last:
                            transpose_x(f1 + i + 2, u)
                        project(i, u)
                    token_tiles(pe, None, body)
                if l == 3:
                    pe.wait_ge(simset, 4)
                    for b in range(B):
                        for k in range(DK):
                            m = pe.matmul(ps[6][:, b * D:(b + 1) * D], csum[:, k, b:b + 1].to_broadcast([P, P]),
                                          W3x[:, 1, k, :], start=(k == 0), stop=(k == DK - 1))
                    m.then_inc(set_pe, 1)
                    transpose_x(f0, 0)
                    transpose_x(f0 + 1, 1)
                    pe.wait_ge(simset, 5)

                    def body(i, u, q, b, last, f0=f0):
                        wait(pe, xT_ready, f0 + i + 1)
                        wait(pe, x_done, 3 * NT + i - 1)
                        for k in range(DK):
                            pe.matmul(ps[1 + 2 * u][:, 0:D], xT[:, u, k, :], W3x[:, 0, k, :], start=(k == 0), stop=False)
                        pe.matmul(ps[1 + 2 * u][:, 0:D], ones[0:1, :], rowB[0:1, b, :], start=False,
                                  stop=True).then_inc(o_done, 1)
                        if not last:
                            transpose_x(f0 + i + 2, u)
                    token_tiles(pe, None, body)

                g0 = FG[l]
                transpose_x(g0, 0)
                transpose_x(g0 + 1, 1)

                def body(i, u, q, b, last, g0=g0, l=l):
                    wait(pe, xT_ready, g0 + i + 1)
                    wait(pe, lg_used, l * NT + i - 1)
                    for k in range(DK):
                        m = pe.matmul(ps[6 - 2 * u][:, 0:E], xT[:, u, k, :], gateT[:, l, k, :], start=(k == 0), stop=(k == DK - 1))
                    m.then_inc(lg_done, 1)
                    if not last:
                        transpose_x(g0 + i + 2, u)
                token_tiles(pe, None, body)
                pe.wait_ge(rt_v, 2 * l + 2)
                cnt = Rt[:, 0:(NT + 1) * E]
                pe.matmul(ps[7][:, 0:(NT + 1) * E], ones[:, :], Rt[:, 136:136 + (NT + 1) * E], start=True, stop=False)
                pe.matmul(ps[7][:, 0:(NT + 1) * E], upper[:, :], cnt, start=False, stop=True).then_inc(rt_pe, 1)

                n, e0, up, nh = ETILES[l], EB0[l], UP[l], HID[l] // P
                if SHARED[l]:
                    pe.wait_ge(w_shared, 16 * sum(SHARED[:l + 1]))

                def take(i, u, q):
                    wait(pe, xs_in[u], 16 * (EP[l][u] + q + 1))
                    wait(pe, exT_ready, e0 + i)
                    for k in range(DK):
                        m = pe.transpose(ps[5][:, k * P:(k + 1) * P], xs[:, u, k * P:(k + 1) * P], ident[:, :])
                    m.then_inc(et_done, 1)

                def upward(i, u):
                    wait(pe, exT_ready, e0 + i + 1)
                    wait(pe, w1_ready, e0 + i + 1)
                    wait(pe, hT_ready, e0 + i - 1)
                    for c in range(up // P):
                        for k in range(DK):
                            m = pe.matmul(ps[2 * u + c // 4][:, c % 4 * P:(c % 4 + 1) * P],
                                          w1[l % 2][u][:, k * up + c * P:k * up + (c + 1) * P],
                                          xT[:, u, k, :], start=(k == 0), stop=(k == DK - 1))
                    m.then_inc(u_done, 1)

                def downward(i, u):
                    at = i if SHARED[l] else i + NT
                    e = pe.value_load(etab[0:1, bass.ds(at, 1)], min_val=0, max_val=WSLOTS[l] - 1)
                    wait(pe, hT_ready, e0 + i + 1)
                    wait(pe, y_ready, e0 + i - 1)
                    for c in range(nh):
                        m = pe.matmul(ps[4 + 2 * u][:, 0:D], hT[:, u, c * P:(c + 1) * P],
                                      W[:, bass.ds(e * WSIZE[l] + (DK * up + c * D), D)],
                                      start=(c == 0), stop=(c == nh - 1))
                    m.then_inc(d_done, 1)

                take(0, 0, 0)
                take(1, 1, 0)
                upward(0, 0)
                take(2, 0, 1)

                def body(i, u, q, left):
                    if left > 0:
                        upward(i + 1, 1 - u)
                    if left > 2:
                        take(i + 3, 1 - u, q + 1 + u)
                    downward(i, u)
                expert_tiles(pe, None, n, body)

        @block.scalar
        def _(act):
            act.wait_ge(ctx_in, 16 * 9)
            act.activation(tg[:, :], small[:, 16:24], ACT.Tanh).then_inc(tg_ready, 1)
            act.wait_ge(consts, 12)

            def take(i, u, f, used):
                wait(act, t_done, f + i + 1)
                wait(act, *used)
                act.activation(xT[:, u, :, :].rearrange("p k n -> p (k n)"), TWO[u][:, 0:D], ACT.Copy).then_inc(xT_ready, 1)

            def std(n):
                wait(act, stats, NT * (n + 1))
                act.activation(STD[:, :], MV[:, :, 1], ACT.Sqrt, bias=eps[:, 0:1]).then_inc(std_ready, 1)

            for l in range(LAYERS):
                if l == 1:
                    act.wait_ge(set_pe, 3)
                    for c in range(DK):
                        m = act.activation(kT[:, c, :], ps[c][:, 0:B * S2], ACT.Identity, bias=bqk[:, 1, c:c + 1])
                    m.then_inc(set_act, 1)
                std(2 * l)
                if l == 0:
                    act.wait_ge(set_pe, 1)
                    act.activation(rfk[:, :, :, :].rearrange("p s b m -> p b s m"),
                                   ps[0][0:KH, 0:4 * M].rearrange("p (b s m) -> p b s m", b=B, s=2),
                                   ACT.Exp, scale=1.0 / 16.0).then_inc(set_act, 1)

                    def expo(i, u):
                        wait(act, r_done, i + 1)
                        wait(act, o_done, i - 1)
                        act.activation(rf[:, u, :], ps[2][0:M, 0:P], ACT.Exp, scale=1.0 / 16.0).then_inc(rf_ready, 1)
                    expo(0, 0)

                    def body(i, u, q, b, last):
                        if last < 2:
                            expo(i + 1, 1 - u)
                    token_tiles(act, None, body)
                if l == 1:
                    def queries(i, u):
                        wait(act, q_done, i + 1)
                        wait(act, s_done, 6 * (i - 1))
                        for c in range(DK):
                            m = act.activation(qT[:, u, c, :], ps[1][:, c * P:(c + 1) * P], ACT.Identity,
                                               bias=bqk[:, 0, c:c + 1])
                        m.then_inc(q_ready, 1)

                    def expo(i, u, c):
                        wait(act, mx1, 2 * i + c + 1)
                        for j in range(HC):
                            hh = c * HC + j
                            m = act.activation(PR[:, u, hh, :], PR[:, u, hh, :], ACT.Exp, bias=negm[:, u, hh:hh + 1],
                                               accum_out=rs[:, u, hh:hh + 1])
                        m.then_inc(e_ready, 1)

                    def copy(i, g):
                        wait(act, pt_done, 5 * i + g + 1)
                        wait(act, pv_done, 5 * i)
                        act.activation(PT[:, g, :], ps[0][:, :], ACT.Copy).then_inc(pt_a, 1)
                    queries(0, 0)
                    queries(1, 1)
                    expo(0, 0, 0)
                    expo(0, 0, 1)

                    def body(i, u, q, b, last):
                        copy(i, 1)
                        if not last:
                            queries(i + 2, u)
                        if last < 2:
                            expo(i + 1, 1 - u, 0)
                        copy(i, 3)
                        if last < 2:
                            expo(i + 1, 1 - u, 1)
                    token_tiles(act, None, body)
                if l == 2:
                    def body(i, u, q, b, last):
                        wait(act, xn_ready, FX[2] + i + 1)
                        act.activation(XN[:, i, :], xn[:, u, :], ACT.Copy).then_inc(xn_copied, 1)
                    token_tiles(act, None, body)
                    act.wait_ge(set_v, 7)
                    for b in range(B):
                        m = act.activation(EB[:, b * NTB:(b + 1) * NTB], MX[:, b * NTB:(b + 1) * NTB], ACT.Exp,
                                           bias=small[:, 10 + b:11 + b], scale=-1.0, accum_out=small[:, 8 + b:9 + b])
                        m.then_inc(set_act, 1)

                    def expo(i, u):
                        wait(act, s_done, 6 * NT + NT + i + 1)
                        wait(act, at_done, i - 1)
                        wait(act, simset, 3)
                        act.activation(A2[:, u, :], ps[2 - u][:, 0:S2], ACT.Exp, bias=MX[:, i:i + 1] if type(i) is int
                                       else MX[:, bass.ds(i, 1)], accum_out=rs[:, u, 0:1]).then_inc(a_ready, 1)
                    expo(0, 0)

                    def body(i, u, q, b, last):
                        if last < 2:
                            expo(i + 1, 1 - u)
                    token_tiles(act, None, body)
                if l == 3:
                    token_tiles(act, None, lambda i, u, q, b, last: take(i, u, FX[3], (o_done, 3 * NT + i - 1)))
                std(2 * l + 1)
                if l == 2:
                    act.wait_ge(rt_v, 2 * l + 1)
                    act.activation(STD[:, :], VT[:, :], ACT.Sqrt, bias=eps[:, 1:2]).then_inc(rt_act, 1)

                def body(i, u, q, b, last):
                    if l % 2:
                        wait(act, xn_ready, FG[l] + i + 1)
                        act.activation(XNs[:, i, :], xn[:, u, :], ACT.Copy).then_inc(xn_copied, 1)
                    take(i, u, FG[l], (lg_done, l * NT + i - 1))
                token_tiles(act, None, body)
                if l == 2:
                    act.wait_ge(route, 1)
                    act.activation(Rt[:, 896:1024], Rt[:, 136:264], ACT.Sigmoid).then_inc(rt_act, 1)
                elif l == 3:
                    act.wait_ge(route, 2)
                    act.activation(Rt[:, 136:264], Rt[:, 264:392], ACT.Exp).then_inc(rt_act, 1)
                else:
                    act.wait_ge(gate_in, l + 1)
                    act.activation(g2[:, :], g2[:, :], ACT.Exp).then_inc(rt_act, 1)
                n, e0, nh = ETILES[l], EB0[l], HID[l] // P

                def body(i, u, q, left):
                    if l == 0:
                        wait(act, u_done, e0 + i + 1)
                        wait(act, d_done, e0 + i - 1)
                        for k in range(2):
                            m = act.activation(hT[:, u, k * 512:(k + 1) * 512], ps[2 * u + k][:, :], ACT.Silu)
                        m.then_inc(hT_ready, 1)
                    elif l == 1:
                        wait(act, u_done, e0 + i + 1)
                        wait(act, hT_ready, e0 + i - 1)
                        act.activation(half[:, u, :], ps[2 * u][:, :], ACT.Silu).then_inc(half_ready, 1)
                    else:
                        e = act.value_load(etab[0:1, bass.ds(i, 1)], min_val=0, max_val=E)
                        wait(act, u_done, e0 + i + 1)
                        wait(act, d_done, e0 + i - 1)
                        for c in range(nh):
                            m = act.activation(hT[:, u, c * P:(c + 1) * P],
                                               ps[2 * u + c // 4][:, c % 4 * P:(c % 4 + 1) * P],
                                               ACT.Relu if l == 2 else ACT.Gelu,
                                               bias=b1T[:, bass.ds(e * nh + c, 1)])
                        m.then_inc(hT_ready, 1)
                if l >= 2:
                    act.wait_ge(b2_in, 32 * (l - 1))
                expert_tiles(act, None, n, body)

        @block.vector
        def _(v):
            st = [Steps(v, v_step[0])]

            def then(ins):
                st[0].then(ins)

            def col(t, i):
                return t[:, bass.ds(i, 1)]

            def rstd(n):
                v.wait_ge(std_ready, n + 1)
                then(v.reciprocal(RSTD[:, :], STD[:, :]))

            def norm(i, u, f, extra=()):
                wait(v, t_done, f - 1)
                for s, k in extra:
                    wait(v, s, k)
                return v.tensor_scalar(xn[:, u, :], X[:, i, :], MV[:, i, 0:1], col(RSTD, i), ALU.subtract, ALU.mult)

            def take(u, f, used, banks=TWO):
                wait(v, t_done, f + 1)
                for s, k in used:
                    wait(v, s, k)
                v.tensor_copy(xT[:, u, :, :].rearrange("p k n -> p (k n)"), banks[u][:, 0:D]).then_inc(xT_ready, 1)

            def finish(i, s):
                alone(v)
                v.bn_stats(st6[:, i, :], X[:, i, :]).then_inc(s, 1)

            def gather_statistics(s, count):
                v.wait_ge(s, count)
                for i in range(NT):
                    v.bn_aggr(MV[:, i, :], st6[:, i, :]).then_inc(stats, 1)

            def setup(l, stp):
                for u in range(2):
                    v.wait_ge(y_stored[u], 16 * STORES[u] * l)
                if l == 1:
                    for k in range(DK):
                        for b in range(B):
                            v.tensor_copy(ctxR[:, k, b, :].rearrange("p (j s) -> p j s", j=4),
                                          ctxT[:, k, b, P:S2].unsqueeze(1).to_broadcast([P, 4, KR])).then_inc(last_keys, 1)
                    v.wait_ge(set_act, 2)
                    for c in range(DK):
                        for b in range(B):
                            m = v.tensor_tensor(KBD[:, c, b, :, :],
                                                kT[:, c, b * S2:(b + 1) * S2].unsqueeze(1).to_broadcast([P, HC, S2]),
                                                headm[:, :].unsqueeze(2).to_broadcast([P, HC, S2]), ALU.mult)
                            m.then_inc(set_v, 1)
                    v.wait_ge(set_pe, 4)
                    for b in range(B):
                        v.tensor_tensor(Vh[:, b, 0, :], ps[2 + b][:, 0:D], bvr, ALU.add)
                        then(v.tensor_tensor(Vh[0:4 * KR, b, 1, :], ps[2 + b][0:4 * KR, D:2 * D], bvr[0:4 * KR, :], ALU.add))
                        vr = Vh[0:4 * KR, b, 1, :].rearrange("p (j h d) -> p j h d", j=4, h=4)
                        v.tensor_tensor(vr, vr, remm[0:4 * KR, :].unsqueeze(1).unsqueeze(3).to_broadcast([4 * KR, 4, 4, DH]),
                                        ALU.mult).then_inc(vready, 1)
                    then(v.tensor_scalar(orow, orow, tg[:, 1:2], None, ALU.mult))
                if l == 2:
                    for k in range(DK):
                        m = v.tensor_scalar(CW[:, k, :, :].rearrange("p b s -> p (b s)"),
                                            ctxT[:, k, :, :].rearrange("p b s -> p (b s)"),
                                            simw[:, 2, k:k + 1], simw[:, 0, k:k + 1], ALU.mult, ALU.add)
                    m.then_inc(simset, 1)
                    v.wait_ge(set_pe, 5)
                    v.tensor_scalar(simrow[:, :, :].rearrange("p b s -> p (b s)"), ps[6][0:1, 0:B * S2], bsim[0:1, 0:1],
                                    None, ALU.add).then_inc(simset, 1)
                if l == 3:
                    v.wait_ge(xw_in, 16 * 11)
                    for k in range(DK):
                        for b in range(B):
                            stp.mark(v.tensor_reduce(csum[:, k, b:b + 1], ctxT[:, k, b, :], AX.X, ALU.add))
                    v.wait_ge(stp.s, stp.count)
                    v.engine_nop().then_inc(simset, 1)
                    v.wait_ge(set_pe, 7)
                    for b in range(B):
                        stp.mark(v.scalar_tensor_tensor(rowB[:, b, :], ps[6][:, b * D:(b + 1) * D], 1.0 / S2, b3row,
                                                        ALU.mult, ALU.add))
                    v.wait_ge(stp.s, stp.count)
                    v.engine_nop().then_inc(simset, 1)

            for i in range(NT):
                if i % 4 == 0:
                    v.wait_ge(x_in[i // 4], 16)
                v.bn_stats(st6[:, i, :], X[:, i, :]).then_inc(x0_stats, 1)
            gather_statistics(x0_stats, NT)
            v.wait_ge(consts, 12)
            v.wait_ge(ctx_in, 16 * 9)
            v.wait_ge(tg_ready, 1)

            for l in range(LAYERS):
                if l:
                    st[0] = Steps(v, v_step[l])
                f0, tgx, tgf = FX[l], tg[:, l:l + 1], tg[:, LAYERS + l:LAYERS + l + 1]
                stp = st[0]
                rstd(2 * l)
                if l == 0:
                    norm(0, 0, f0).then_inc(xn_ready, 1)
                    norm(1, 1, f0 + 1).then_inc(xn_ready, 1)
                    v.wait_ge(set_pe, 2)
                    for b in range(B):
                        v.tensor_scalar(KVZ[:, b, 0:D], ps[1 + b][0:M, 0:D], tgx[0:M, :], None, ALU.mult)
                        m = v.tensor_copy(KVZ[:, b, D:D + 1], ps[1 + b][0:M, D:D + 1])
                    m.then_inc(set_v, 1)
                    take(0, f0, ())

                    def body(i, u, q, b, last):
                        if not last:
                            norm(i + 2, u, f0 + i + 2).then_inc(xn_ready, 1)
                        if last < 2:
                            take(1 - u, f0 + i + 1, [(r_done, i)])
                        v.wait_ge(o_done, i + 1)
                        then(v.tensor_scalar(small[:, 12 + u:13 + u], ps[1 + 2 * u][:, D:D + 1], 8e-6, None, ALU.add))
                        then(v.reciprocal(small[:, 14 + u:15 + u], small[:, 12 + u:13 + u]))
                        st[0].then(v.scalar_tensor_tensor(X[:, i, :], ps[1 + 2 * u][:, 0:D], small[:, 14 + u:15 + u],
                                                          X[:, i, :], ALU.mult, ALU.add))
                        finish(i, x_done)
                    token_tiles(v, stp, body)
                if l == 1:

                    def logits(i, u, c):
                        if c == 0:
                            wait(v, neg_ready, i + 1)
                            wait(v, pt_done, 5 * (i - 1))
                        for g in range(3):
                            n = min(3, HC - 3 * g)
                            wait(v, s_done, 6 * i + 3 * c + g + 1)
                            v.scalar_tensor_tensor(
                                PR[:, u, c * HC + 3 * g:c * HC + 3 * g + n, :],
                                ps[2 + g][:, 0:n * S2].rearrange("p (h s) -> p h s", h=n), 0.25,
                                neg[:, u, :].unsqueeze(1).to_broadcast([P, n, S2]), ALU.mult, ALU.add).then_inc(l_ready, 1)

                    def maxima(i, u, c):
                        wait(v, l_ready, 6 * i + 3 * c + 3)
                        v.tensor_reduce(negm[:, u, c * HC:(c + 1) * HC], PR[:, u, c * HC:(c + 1) * HC, :], AX.X,
                                        ALU.max, negate=True).then_inc(mx1, 1)

                    def copy(i, g):
                        n = P if g < 4 else 4 * KR
                        wait(v, pt_done, 5 * i + g + 1)
                        wait(v, pv_done, 5 * i + (1 if g == 4 else 0))
                        v.tensor_copy(PT[0:n, g % 4, :], ps[6][0:n, :]).then_inc(pt_v, 1)

                    def final(i):
                        wait(v, o_done, NT + i + 1)
                        then(v.scalar_tensor_tensor(X[:, i, :], ps[1][:, 0:256], tgx, X[:, i, :], ALU.mult, ALU.add))
                        then(v.tensor_tensor(X[:, i, :], X[:, i, :], orow, ALU.add))
                        finish(i, x_done)

                    def turned(i, u):
                        wait(v, ot_done, i + 1)
                        wait(v, o_done, NT + i - 1)
                        v.tensor_copy(oT[:, u, :], ps[5][:, 0:D]).then_inc(ot_ready, 1)
                    norm(0, 0, f0).then_inc(xn_ready, 1)
                    take(0, f0, (), ONE)
                    norm(1, 1, f0 + 1).then_inc(xn_ready, 1)
                    take(1, f0 + 1, (), ONE)
                    for c in range(DK):
                        logits(0, 0, c)
                        maxima(0, 0, c)

                    def body(i, u, q, b, last):
                        first = type(i) is int and i == 0
                        if not last:
                            norm(i + 2, u, f0 + i + 2).then_inc(xn_ready, 1)
                        if last < 2:
                            logits(i + 1, 1 - u, 0)
                        copy(i, 0)
                        if not last:
                            take(u, f0 + i + 2, [(q_done, i + 1)], ONE)
                        if last < 2:
                            maxima(i + 1, 1 - u, 0)
                            logits(i + 1, 1 - u, 1)
                        if not first:
                            turned(i - 1, 1 - u)
                        copy(i, 2)
                        if last < 2:
                            maxima(i + 1, 1 - u, 1)
                        copy(i, 4)
                        if not first:
                            final(i - 1)
                        else:
                            for _ in range(2):
                                stp.mark(v.engine_nop())
                        wait(v, e_ready, 2 * (i + 1))
                        then(v.reciprocal(rr[:, u, :], rs[:, u, :]))
                        wait(v, pv_done, 5 * (i + 1))
                        v.tensor_tensor(obuf[:, u, :].rearrange("p (h d) -> p h d", h=HEADS),
                                        ps[7][:, 0:D].rearrange("p (h d) -> p h d", h=HEADS),
                                        rr[:, u, :].unsqueeze(2).to_broadcast([P, HEADS, DH]), ALU.mult).then_inc(on_ready, 1)
                    token_tiles(v, stp, body)
                    turned(NT - 1, 1)
                    final(NT - 1)
                if l == 2:
                    norm(0, 0, f0).then_inc(xn_ready, 1)
                    norm(1, 1, f0 + 1).then_inc(xn_ready, 1)
                    take(0, f0, ())

                    def body(i, u, q, b, last):
                        if not last:
                            norm(i + 2, u, f0 + i + 2, [(xn_copied, NT + i + 1)]).then_inc(xn_ready, 1)
                        if last < 2:
                            take(1 - u, f0 + i + 1, [(s_done, 6 * NT + i)])
                        wait(v, s_done, 6 * NT + i + 1)
                        v.tensor_reduce(col(MX, i), ps[2 - u][:, 0:S2], AX.X, ALU.max, negate=True).then_inc(mx_ready, 1)
                    token_tiles(v, stp, body)
                    v.wait_ge(mx_ready, NT)
                    for b in range(B):
                        m = v.tensor_reduce(small[:, 4 + b:5 + b], MX[:, b * NTB:(b + 1) * NTB], AX.X, ALU.min, negate=True)
                        stp.mark(m)
                    v.wait_ge(v_step[2], stp.count)
                    v.engine_nop().then_inc(set_v, 1)
                    v.wait_ge(set_pool, 1)
                    v.tensor_scalar(small[:, 10:12], small[:, 6:8], -1.0, None, ALU.mult).then_inc(set_v, 1)
                    v.wait_ge(set_pe, 6)
                    v.wait_ge(xw_in, 16 * 8)
                    then(v.reciprocal(small[:, 12:14], ps[6][:, 4:6]))
                    for b in range(B):
                        stp.mark(v.tensor_scalar(csum[:, b, :], ps[6][:, 2 * b:2 * b + 2], small[:, 12 + b:13 + b], None, ALU.mult))
                    v.wait_ge(v_step[2], stp.count)
                    for b in range(B):
                        for k in range(DK):
                            m = v.scalar_tensor_tensor(hcW[:, b, k, :], Wqv[:, 3 * DK + k, :], csum[:, b, k:k + 1],
                                                       Wqv[:, k, :], ALU.mult, ALU.add)
                    stp.mark(m)
                    stp.then(v.tensor_scalar(qvrow, qvrow, tgx, None, ALU.mult))
                    v.engine_nop().then_inc(simset, 1)
                    f1 = FX2

                    def soften(i, u):
                        wait(v, a_ready, i + 1)
                        then(v.reciprocal(rr[:, u, 0:1], rs[:, u, 0:1]))
                        v.tensor_scalar(A2[:, u, :], A2[:, u, :], rr[:, u, 0:1], None, ALU.mult).then_inc(an_ready, 1)
                    norm(0, 0, f1).then_inc(xn_ready, 1)
                    take(0, f1, ())
                    norm(1, 1, f1 + 1).then_inc(xn_ready, 1)
                    take(1, f1 + 1, ())
                    soften(0, 0)

                    def final(i, u):
                        wait(v, o_done, 2 * NT + i + 1)
                        then(v.scalar_tensor_tensor(X[:, i, :], ps[7 - u][:, 0:D], tgx, X[:, i, :], ALU.mult, ALU.add))
                        then(v.tensor_tensor(X[:, i, :], X[:, i, :], qvrow, ALU.add))
                        finish(i, x_done)

                    def body(i, u, q, b, last):
                        if not last:
                            norm(i + 2, u, f1 + i + 2).then_inc(xn_ready, 1)
                        wait(v, at_done, i + 1)
                        wait(v, hq_done, i - 1)
                        v.tensor_copy(AT2[0:KH, u, :], ps[3][0:KH, 0:D]).then_inc(at_ready, 1)
                        if type(i) is int and i == 0:
                            for _ in range(2):
                                stp.mark(v.engine_nop())
                        else:
                            final(i - 1, 1 - u)
                        wait(v, hq_done, i + 1)
                        wait(v, o_done, 2 * NT + i - 1)
                        v.tensor_copy(hqT[:, u, :], ps[4][:, 0:D]).then_inc(hq_ready, 1)
                        wait(v, hq_ready, 2 * i + 1)
                        v.tensor_tensor(xhT[:, u, :], hqT[:, u, :], xT[:, u, :, :].rearrange("p k n -> p (k n)"),
                                        ALU.mult).then_inc(hq_ready, 1)
                        if last < 2:
                            soften(i + 1, 1 - u)
                        if not last:
                            take(u, f1 + i + 2, [(xpart_done, i + 1)])
                    token_tiles(v, stp, body)
                    final(NT - 1, 1)
                if l == 3:
                    norm(0, 0, f0).then_inc(xn_ready, 1)
                    norm(1, 1, f0 + 1).then_inc(xn_ready, 1)

                    def body(i, u, q, b, last):
                        if not last:
                            norm(i + 2, u, f0 + i + 2).then_inc(xn_ready, 1)
                        wait(v, o_done, 3 * NT + i + 1)
                        then(v.scalar_tensor_tensor(X[:, i, :], ps[1 + 2 * u][:, 0:D], tgx, X[:, i, :], ALU.mult, ALU.add))
                        finish(i, x_done)
                    token_tiles(v, stp, body)

                gather_statistics(x_done, (l + 1) * NT)

                g0 = FG[l]
                rstd(2 * l + 1)
                if l == 2:
                    then(v.tensor_tensor(VT[:, :], RSTD[:, :], RSTD[:, :], ALU.mult))
                    v.tensor_tensor(VT[:, :], VT[:, :], MV[:, :, 1], ALU.mult).then_inc(rt_v, 1)
                    v.wait_ge(rt_act, 3)
                    then(v.reciprocal(VT[:, :], STD[:, :]))
                    then(v.tensor_tensor(RSTD[:, :], RSTD[:, :], VT[:, :], ALU.mult))
                    v.wait_ge(xw_in, 16 * 9)
                else:
                    v.engine_nop().then_inc(rt_v, 1)
                LG = Rt[:, 136:264]

                def normg(i, u):
                    f = g0 + i
                    used = []
                    if SHARED[l]:
                        used.append((xn_stored[u], 16 * (NTB * sum(SHARED[:l]) + (i - u) // 2)))
                    if l % 2:
                        used.append((xn_copied, (l - 1) * NT + i - 1))
                    m = norm(i, u, f, used)
                    if l == 2:
                        then(m)
                        m = v.tensor_tensor(xn[:, u, :], xn[:, u, :], nwrow, ALU.mult)
                    m.then_inc(xn_ready, 1)
                normg(0, 0)
                normg(1, 1)

                def body(i, u, q, b, last):
                    if not last:
                        normg(i + 2, u)
                    wait(v, lg_done, l * NT + i + 1)
                    m = v.tensor_copy(LG[:, bass.ds(i * E, E)], ps[6 - 2 * u][:, 0:E]).then_inc(lg_used, 1)
                token_tiles(v, stp, body)
                v.wait_ge(lg_used, NT * (l + 1))
                sc3 = LG.rearrange("p (i e) -> p i e", e=E)
                t16 = small[:, 0:16]
                bc = lambda ap: ap.unsqueeze(2).to_broadcast([P, NT, E])
                tmp = Rt[:, 264:392]
                tmp3 = tmp.rearrange("p (i e) -> p i e", e=E)
                if l == 2:
                    v.engine_nop().then_inc(route, 1)
                    v.wait_ge(rt_act, 4)
                    then(v.tensor_copy(LG, Rt[:, 896:1024]))
                if l == 3:
                    then(v.tensor_tensor(sc3, sc3, rb3[:, :].unsqueeze(1).to_broadcast([P, NT, E]), ALU.add))
                    then(v.tensor_reduce(t16, sc3, AX.X, ALU.max))
                    then(v.tensor_tensor(tmp3, sc3, bc(t16), ALU.subtract))
                    v.engine_nop().then_inc(route, 1)
                    v.wait_ge(rt_act, 5)
                    then(v.tensor_reduce(t16, sc3, AX.X, ALU.add))
                    then(v.reciprocal(t16, t16))
                    then(v.tensor_tensor(sc3, sc3, bc(t16), ALU.mult))
                down3 = downb[:, :].unsqueeze(1).to_broadcast([P, NT, E])
                oh = [Rt[:, 392:520].rearrange("p (i e) -> p i e", e=E), Rt[:, 520:648].rearrange("p (i e) -> p i e", e=E)]
                best = [g1, g2]
                for k in range(TOPK):
                    then(v.tensor_reduce(best[k][:, :], sc3, AX.X, ALU.max))
                    then(v.tensor_tensor(tmp3, sc3, bc(best[k][:, :]), ALU.is_equal))
                    then(v.tensor_tensor(tmp3, tmp3, down3, ALU.mult))
                    then(v.tensor_reduce(t16, tmp3, AX.X, ALU.max))
                    then(v.tensor_tensor(oh[k], down3, bc(t16), ALU.is_equal))
                    if k == 0:
                        then(v.scalar_tensor_tensor(sc3, oh[0], -3.0e38, sc3, ALU.mult, ALU.add))
                then(v.memset(Rt[:, NT * E:(NT + 1) * E], 0.0))
                cnt3 = Rt[:, 0:NT * E].rearrange("p (i e) -> p i e", e=E)
                then(v.tensor_tensor(cnt3, oh[0], oh[1], ALU.add))
                before3 = Rt[:, 136:136 + (NT + 1) * E].rearrange("p (i e) -> p i e", e=E)
                stp.mark(v.memset(Rt[:, 136:136 + E], 0.0))
                for e in range(E):
                    stp.mark(v.tensor_tensor_scan(before3[:, 1:NT + 1, e], ones[:, 0:NT], cnt3[:, :, e], 0.0,
                                                  ALU.mult, ALU.add))
                v.wait_ge(v_step[l], stp.count)
                v.engine_nop().then_inc(rt_v, 1)
                if l < 2:
                    then(v.tensor_tensor(g2[:, :], g2[:, :], g1[:, :], ALU.subtract))
                    v.engine_nop().then_inc(gate_in, 1)
                    v.wait_ge(rt_act, l + 1)
                    then(v.tensor_scalar(t16, g2[:, :], 1.0, None, ALU.add))
                    then(v.reciprocal(g1[:, :], t16))
                    then(v.tensor_tensor(g2[:, :], g2[:, :], g1[:, :], ALU.mult))
                elif l == 2:
                    then(v.tensor_tensor(t16, g1[:, :], g2[:, :], ALU.add))
                    then(v.tensor_scalar(t16, t16, 1e-6, None, ALU.add))
                    then(v.reciprocal(t16, t16))
                    then(v.tensor_tensor(g1[:, :], g1[:, :], t16, ALU.mult))
                    then(v.tensor_tensor(g2[:, :], g2[:, :], t16, ALU.mult))
                n, e0, nh, up = ETILES[l], EB0[l], HID[l] // P, UP[l]

                def take_e(i, u):
                    wait(v, et_done, e0 + i + 1)
                    wait(v, u_done, e0 + i - 1)
                    v.tensor_copy(xT[:, u, :, :].rearrange("p k n -> p (k n)"), ps[5][:, 0:D]).then_inc(exT_ready, 1)

                def expert_weights(i, u):
                    at = i if SHARED[l] else i + NT
                    e = v.value_load(etab[0:1, bass.ds(at, 1)], min_val=0, max_val=WSLOTS[l] - 1)
                    wait(v, u_done, e0 + i - 1 if l % 2 else e0 + i)
                    v.tensor_copy(w1[l % 2][u][:, 0:DK * up], W[:, bass.ds(e * WSIZE[l], DK * up)]).then_inc(w1_ready, 1)


                def begin():
                    if SHARED[l]:
                        v.wait_ge(w_shared, 16 * sum(SHARED[:l + 1]))
                    take_e(0, 0)
                    expert_weights(0, 0)
                    take_e(1, 1)
                if SHARED[l]:
                    begin()
                v.wait_ge(rt_pe, l + 1)
                then(v.tensor_scalar(cnti[:, :], ps[7][:, NT * E:(NT + 1) * E], float(P - 1), None, ALU.add))
                then(v.tensor_scalar(cnti[:, :], cnti[:, :], 7, None, ALU.logical_shift_right))
                then(v.tensor_copy(cntf[:, 0, :], cnti[:, :]))
                then(v.tensor_tensor_scan(cntf[:, 1, :], ones[:, 0:E], cntf[:, 0, :], 0.0, ALU.mult, ALU.add))
                then(v.tensor_tensor(cntf[:, 2, :], cntf[:, 1, :], cntf[:, 0, :], ALU.subtract))
                then(v.tensor_scalar(cntf[:, 2, :], cntf[:, 2, :], float(P), None, ALU.mult))
                then(v.tensor_tensor(tmp3, ps[7][:, 0:NT * E].rearrange("p (i e) -> p i e", e=E),
                                     cntf[:, 2, :].unsqueeze(1).to_broadcast([P, NT, E]), ALU.add))
                for k in range(TOPK):
                    then(v.tensor_tensor(oh[k], oh[k], tmp3, ALU.mult))
                    then(v.tensor_reduce(t16, oh[k], AX.X, ALU.add))
                    then(v.tensor_copy(pos[:, :, k], t16))
                then(v.tensor_tensor(tcmp[:, :, :], cntf[0:1, 1, :].unsqueeze(1).to_broadcast([1, SLOT_TILES, E]),
                                     tidx[:, :, :], ALU.is_le))
                then(v.tensor_reduce(tsum[:, :], tcmp[:, :, :], AX.X, ALU.add))
                then(v.tensor_scalar(etab[:, NT:], tsum[:, :], float(E - 1), None, ALU.min))
                v.engine_nop().then_inc(pos_ready, 2)

                if l >= 2:
                    v.wait_ge(b2_in, 32 * (l - 1))

                def hidden(i, u):
                    wait(v, half_ready, i + 1)
                    wait(v, d_done, e0 + i - 1)
                    v.tensor_tensor(hT[:, u, 0:512], half[:, u, :], ps[2 * u + 1][:, :], ALU.mult).then_inc(hT_ready, 1)
                if not SHARED[l]:
                    begin()
                expert_weights(1, 1)
                take_e(2, 0)
                if l == 1:
                    hidden(0, 0)
                shared_tiles = [SHARED[l]]

                def to_list():
                    shared_tiles[0] = False

                def body(i, u, q, left):
                    if left > 1:
                        expert_weights(i + 2, u)
                    if left > 2:
                        take_e(i + 3, 1 - u)
                    if l == 1 and left > 0:
                        hidden(i + 1, 1 - u)
                    if l >= 2:
                        e = v.value_load(etab[0:1, bass.ds(i, 1)], min_val=0, max_val=E)
                    wait(v, d_done, e0 + i + 1)
                    if shared_tiles[0]:
                        if l >= 2:
                            v.tensor_tensor(ybuf[:, u, :], ps[4 + 2 * u][:, 0:D], b2b[:, bass.ds(e * D, D)], ALU.add).then_inc(y_sum, 1)
                            wait(v, y_sum, NT * (l - 2) + i + 1)
                            v.scalar_tensor_tensor(X[:, i, :], ybuf[:, u, :], tgf, X[:, i, :], ALU.mult,
                                                   ALU.add).then_inc(y_ready, 1)
                        else:
                            v.scalar_tensor_tensor(X[:, i, :], ps[4 + 2 * u][:, 0:D], tgf, X[:, i, :], ALU.mult,
                                                   ALU.add).then_inc(y_ready, 1)
                    else:
                        stored = q - NT // 2 if SHARED[l] else q
                        wait(v, y_stored[u], 16 * (STORES[u] * l + stored))
                        if l >= 2:
                            m = v.tensor_tensor(ybuf[:, u, :], ps[4 + 2 * u][:, 0:D], b2b[:, bass.ds(e * D, D)], ALU.add)
                        else:
                            m = v.tensor_copy(ybuf[:, u, :], ps[4 + 2 * u][:, 0:D])
                        m.then_inc(y_ready, 1)
                expert_tiles(v, None, n, body, NT // 2 if SHARED[l] else None, to_list)
                v.wait_ge(y_ready, e0 + n)

                for g in (g1, g2):
                    stp.mark(v.tensor_scalar(g[:, :], g[:, :], tgf, None, ALU.mult))
                v.wait_ge(v_step[l], stp.count)

                if l + 1 < LAYERS:
                    setup(l + 1, stp)

                def body(i, u, q):
                    wait(v, y_in[u], 32 * (NT // 4 * l + q + 1))
                    then(v.scalar_tensor_tensor(X[:, i, :], ygat[:, u, 0, :], col(g1, i), X[:, i, :], ALU.mult, ALU.add))
                    then(v.scalar_tensor_tensor(X[:, i, :], ygat[:, u, 1, :], col(g2, i), X[:, i, :], ALU.mult, ALU.add))
                    finish(i, c_done)
                token_quads(v, stp, body)
                if l + 1 < LAYERS:
                    gather_statistics(c_done, (l + 1) * NT)


def kernel(**inputs):
    import numpy as _np
    import concourse.bacc as _bacc
    from concourse import mybir as _mybir
    from concourse.bass_utils import run_bass_kernel_spmd as _run

    x = {k: _np.asarray(v) for k, v in inputs.items()}

    def cols(w):
        return w.reshape(-1, P, w.shape[-1]).transpose(1, 0, 2)

    def flat(*ws):
        return _np.concatenate([cols(w).reshape(P, -1) for w in ws], axis=1)

    def part(v):
        return _np.moveaxis(v.reshape(v.shape[:-1] + (-1, P)), -1, 0)

    c = x["ctx_1024"]
    T_ = _np.transpose
    w0 = [flat(x["L0_ffn_experts_w1"][e].T, x["L0_ffn_experts_w2"][e].T) for e in range(E)]
    w0.append(flat(x["L0_ffn_shared_w1"].T, x["L0_ffn_shared_w2"].T))
    w1 = [flat(_np.concatenate([x["L1_ffn_W1"][e].T, x["L1_ffn_W2"][e].T], axis=1), x["L1_ffn_W3"][e].T)
          for e in range(E)]
    w2 = [flat(x["L2_ffn_ew1"][e], x["L2_ffn_ew2"][e]) for e in range(E)] + [flat(x["L2_ffn_sw1"], x["L2_ffn_sw2"])]
    w3 = [flat(x["L3_ffn_rw1"][e], x["L3_ffn_rw2"][e]) for e in range(E)] + [flat(x["L3_ffn_sw1"], x["L3_ffn_sw2"])]
    W3 = x["L3_xattn_W"]
    arrays = {
        "x": x["x"].reshape(T, D),
        "ctxT": T_(c.reshape(B, S2, DK, P), (3, 2, 0, 1)),
        "ctxr": T_(c.reshape(B, 2, KH, D), (2, 1, 0, 3)),
        "projT": cols(x["L0_xattn_projection"].T),
        "gateT": _np.stack([cols(x["L0_ffn_gate_w"].T), cols(x["L1_ffn_Wg"].T), cols(x["L2_ffn_router_w"].T),
                            cols(x["L3_ffn_router_w"])], axis=1),
        "gates": _np.concatenate([x["g_xattn"], x["g_ffn"]]),
        "bqk": part(_np.stack([x["L1_xattn_wq_b"], x["L1_xattn_wk_b"]])),
        "simw": part(x["L2_xattn_w_sim"].reshape(3, D)),
        "bsim": x["L2_xattn_b_sim"].reshape(1, 1),
        "rb3": x["L3_ffn_router_b"],
        "w0": _np.stack(w0), "w1": _np.stack(w1), "w2": _np.stack(w2), "w3": _np.stack(w3),
        "qkvo": _np.stack([cols(x[f"L1_xattn_w{n}_k"]) for n in "qkvo"]),
        "bv": x["L1_xattn_wv_b"], "bo": x["L1_xattn_wo_b"],
        "mask": x["mask_BxSxS2_ik1"].reshape(T, S2), "side": x["fside_BxSxS2_0"].reshape(T, S2),
        "Wqv": cols(x["L2_xattn_W_qv"]), "bqv": x["L2_xattn_b_qv"],
        "nw": x["L2_ffn_norm_weight"],
        "b2_2": _np.concatenate([x["L2_ffn_eb2"].reshape(-1), x["L2_ffn_sb2"]]),
        "b1_2": part(_np.concatenate([x["L2_ffn_eb1"], x["L2_ffn_sb1"][None]])).reshape(P, -1),
        "W3x": _np.stack([cols(W3[:, :D].T), cols(W3[:, D:].T)], axis=1),
        "b3": x["L3_xattn_b"],
        "b2_3": _np.concatenate([x["L3_ffn_rb2"].reshape(-1), x["L3_ffn_sb2"]]),
        "b1_3": part(_np.concatenate([x["L3_ffn_rb1"], x["L3_ffn_sb1"][None]])).reshape(P, -1),
    }
    nc = _bacc.Bacc("TRN2", target_bir_lowering=False, num_devices=1)
    maps, aps = {}, {}
    for name, v in arrays.items():
        v = _np.ascontiguousarray(v)
        maps[f"in_{name}"] = v
        aps[name] = nc.dram_tensor(f"in_{name}", v.shape, _mybir.dt.from_np(v.dtype), kind="ExternalInput").ap()
    out = nc.dram_tensor("out_x", (T, D), _mybir.dt.float32, kind="ExternalOutput").ap()
    xn_tokens = nc.dram_tensor("xn_tokens", (T, D), _mybir.dt.float32).ap()
    xn_rows = nc.dram_tensor("xn_rows", (ROWS, D), _mybir.dt.float32).ap()
    y_rows = nc.dram_tensor("y_rows", (ROWS, D), _mybir.dt.float32).ap()
    bass_flamingo_moe_kernel(nc, aps, out, xn_tokens, xn_rows, y_rows)
    r = _run(nc, [maps], core_ids=[0])
    return r.results[0]["out_x"].reshape(B, S, D)
```
